# Optimizing a Trainium2 kernel written in Bass

```python
import numpy as np
import jax
import jax.numpy as jnp

def _softmax(x, axis=-1):
    return jax.nn.softmax(x, axis=axis)

def _gelu(x):
    return jax.nn.gelu(x, approximate=True)

def _silu(x):
    return jax.nn.silu(x)

def _sigmoid(x):
    return jax.nn.sigmoid(x)

def _layernorm(x, axis=-1, eps=1e-05):
    m = jnp.mean(x, axis=axis, keepdims=True)
    v = jnp.var(x, axis=axis, keepdims=True)
    return (x - m) / jnp.sqrt(v + eps)

def _scatter_add(tgt, idx, src, axis=0):
    return tgt.at[idx].add(src)

def _segment_sum(src, seg, n):
    return jax.ops.segment_sum(src, seg, n)
kernel_name = 'mk_seq_preln_d1_jaxref_r8_18ed53'

def setup_inputs(seed: int=0):
    np.random.seed(seed)
    _w = jnp.asarray

    def _L0_attn_setup():
        import jax, jax.numpy as jnp
        import numpy as np
        import math
        D_MODEL = 128
        NUM_HEADS = 16
        key = jax.random.key(seed)
        k1, k2, k3 = jax.random.split(key, 3)
        B, S = (2, 256)
        x = jax.random.normal(k1, (B, S, D_MODEL), dtype=jnp.float32)
        W_kqv = jax.random.normal(k2, (D_MODEL, 3 * D_MODEL), dtype=jnp.float32) * (1.0 / math.sqrt(D_MODEL))
        m = jax.random.normal(k3, (NUM_HEADS, 1, 1), dtype=jnp.float32)
        return {'x': x, 'W_kqv': W_kqv, 'm': m}
    _L0_attn_in = _L0_attn_setup()

    def _L0_ffn_setup():
        import jax, jax.numpy as jnp
        import numpy as np
        DIM = 128
        DEPTH = 6
        HEADS = 16
        DIM_HEAD = 64
        WINDOW = 32
        INNER = HEADS * DIM_HEAD
        DIM_INNER = int(DIM * 4 * 2 / 3)
        QK_SCALE = 8.0

        def shift_tokens(t):
            a, s = jnp.split(t, 2, -1)
            s = jnp.pad(s, ((0, 0), (1, 0), (0, 0)))[:, :-1]
            return jnp.concatenate([a, s], -1)

        def l2norm(t):
            return t / jnp.maximum(jnp.linalg.norm(t, axis=-1, keepdims=True), 1e-12)

        def rotate_half(x):
            x1, x2 = jnp.split(x, 2, -1)
            return jnp.concatenate([-x2, x1], -1)

        def rotary_tables(n):
            half = jnp.arange(0, DIM_HEAD, 2, dtype=jnp.float32)
            inv_freq = 1.0 / 10000.0 ** (half / DIM_HEAD)
            t = jnp.arange(n, dtype=jnp.float32)
            freqs = t[:, None] * inv_freq[None, :]
            freqs = jnp.concatenate([freqs, freqs], -1)
            base_scale = (half + 0.4 * DIM_HEAD) / (1.4 * DIM_HEAD)
            power = (t - n // 2) / (WINDOW // 2)
            scale = base_scale[None, :] ** power[:, None]
            scale = jnp.concatenate([scale, scale], -1)
            return (freqs, scale)

        def local_attention(q, k, v):
            b, h, n, d = q.shape
            w = WINDOW
            nw = n // w
            bq = q.reshape(b, h, nw, w, d)
            bk = k.reshape(b, h, nw, w, d)
            bv = v.reshape(b, h, nw, w, d)

            def look(t):
                p = jnp.pad(t, ((0, 0), (0, 0), (1, 0), (0, 0), (0, 0)))
                return jnp.concatenate([p[:, :, :nw], p[:, :, 1:]], axis=3)
            bk2, bv2 = (look(bk), look(bv))
            seq = jnp.arange(n).reshape(nw, w)
            seq_p = jnp.pad(seq, ((1, 0), (0, 0)), constant_values=-1)
            jt = jnp.concatenate([seq_p[:nw], seq_p[1:]], axis=1)
            it = seq[:, :, None]
            jb = jt[:, None, :]
            mask = (it < jb) | (it > jb + w) | (jb == -1)
            sim = jnp.einsum('bhwie,bhwje->bhwij', bq, bk2) * QK_SCALE
            sim = jnp.where(mask, -jnp.finfo(sim.dtype).max, sim)
            attn = jax.nn.softmax(sim, -1)
            out = jnp.einsum('bhwij,bhwje->bhwie', attn, bv2)
            return out.reshape(b, h, n, d)

        def attn_layer(x, Wqkv, qs, ksc, Wo):
            b, n, _ = x.shape
            qkv = x @ Wqkv
            q, k, v = jnp.split(qkv, 3, -1)
            sh = lambda t: t.reshape(b, n, HEADS, DIM_HEAD).transpose(0, 2, 1, 3)
            q, k, v = (sh(q), sh(k), sh(v))
            q = l2norm(q) * qs
            k = l2norm(k) * ksc
            freqs, scale = rotary_tables(n)
            cos, sin = (jnp.cos(freqs), jnp.sin(freqs))
            q = q * cos * scale + rotate_half(q) * sin * scale
            inv = 1.0 / scale
            k = k * cos * inv + rotate_half(k) * sin * inv
            out = local_attention(q, k, v)
            out = out.transpose(0, 2, 1, 3).reshape(b, n, INNER)
            return out @ Wo

        def ffn_layer(x, g, bln, W1, b1, W2, b2):
            mu = x.mean(-1, keepdims=True)
            var = ((x - mu) ** 2).mean(-1, keepdims=True)
            xn = (x - mu) / jnp.sqrt(var + 1e-05) * g + bln
            hg = xn @ W1 + b1
            a, gate = jnp.split(hg, 2, -1)
            return a * jax.nn.gelu(gate, approximate=False) @ W2 + b2
        key = jax.random.key(seed)
        ks = jax.random.split(key, 8)
        B, N = (2, 256)
        init = lambda k, shape: jax.random.normal(k, shape, jnp.float32) * 0.02
        return {'x': jax.random.normal(ks[0], (B, N, DIM), jnp.float32), 'Wqkv': init(ks[1], (DEPTH, DIM, 3 * INNER)), 'q_scale': jnp.ones((DEPTH, DIM_HEAD), jnp.float32), 'k_scale': jnp.ones((DEPTH, DIM_HEAD), jnp.float32), 'Wo': init(ks[2], (DEPTH, INNER, DIM)), 'ln_g': jnp.ones((DEPTH, DIM), jnp.float32), 'ln_b': jnp.zeros((DEPTH, DIM), jnp.float32), 'W1': init(ks[3], (DEPTH, DIM, 2 * DIM_INNER)), 'b1': jnp.zeros((DEPTH, 2 * DIM_INNER), jnp.float32), 'W2': init(ks[4], (DEPTH, DIM_INNER, DIM)), 'b2': jnp.zeros((DEPTH, DIM), jnp.float32)}
    _L0_ffn_in = _L0_ffn_setup()
    _d = {'L0_attn_x': _L0_attn_in['x'], 'L0_attn_W_kqv': _L0_attn_in['W_kqv'], 'L0_attn_m': _L0_attn_in['m'], 'L0_ffn_Wqkv': _L0_ffn_in['Wqkv'], 'L0_ffn_q_scale': _L0_ffn_in['q_scale'], 'L0_ffn_k_scale': _L0_ffn_in['k_scale'], 'L0_ffn_Wo': _L0_ffn_in['Wo'], 'L0_ffn_ln_g': _L0_ffn_in['ln_g'], 'L0_ffn_ln_b': _L0_ffn_in['ln_b'], 'L0_ffn_W1': _L0_ffn_in['W1'], 'L0_ffn_b1': _L0_ffn_in['b1'], 'L0_ffn_W2': _L0_ffn_in['W2'], 'L0_ffn_b2': _L0_ffn_in['b2']}
    _x0 = _d['L0_attn_x']
    _d['L0_attn_x'] = jax.random.normal(jax.random.fold_in(jax.random.key(seed), 1), (4, 512, 128), dtype=_x0.dtype)
    del _x0
    return _d

def reference(L0_attn_x, L0_attn_W_kqv, L0_attn_m, L0_ffn_Wqkv, L0_ffn_q_scale, L0_ffn_k_scale, L0_ffn_Wo, L0_ffn_ln_g, L0_ffn_ln_b, L0_ffn_W1, L0_ffn_b1, L0_ffn_W2, L0_ffn_b2):

    def _L0_attn_ref(x, W_kqv, m):
        import jax, jax.numpy as jnp
        import numpy as np
        import math
        D_MODEL = 128
        NUM_HEADS = 16
        B, S, D = x.shape
        H = NUM_HEADS
        hd = D // H
        scale = math.sqrt(D)
        kqv = x @ W_kqv
        k, q, v = jnp.split(kqv, 3, axis=-1)
        q = q.reshape(B, S, H, hd)
        k = k.reshape(B, S, H, hd)
        v = v.reshape(B, S, H, hd)
        rel = (jnp.arange(S)[None, :] - jnp.arange(S)[:, None]).astype(x.dtype)
        bias = m[None, :, :, :] * rel[None, None, :, :]
        score = jnp.einsum('bqhd,bkhd->bhqk', q, k) / scale + bias
        causal = jnp.tril(jnp.ones((S, S), dtype=bool))
        score = jnp.where(causal[None, None, :, :], score, -jnp.inf)
        attn = jax.nn.softmax(score, axis=-1)
        out = jnp.einsum('bhqk,bkhd->bqhd', attn, v).reshape(B, S, D)
        return out

    def _L0_ffn_ref(x, Wqkv, q_scale, k_scale, Wo, ln_g, ln_b, W1, b1, W2, b2):
        import jax, jax.numpy as jnp
        import numpy as np
        DIM = 128
        DEPTH = 6
        HEADS = 16
        DIM_HEAD = 64
        WINDOW = 32
        INNER = HEADS * DIM_HEAD
        DIM_INNER = int(DIM * 4 * 2 / 3)
        QK_SCALE = 8.0

        def shift_tokens(t):
            a, s = jnp.split(t, 2, -1)
            s = jnp.pad(s, ((0, 0), (1, 0), (0, 0)))[:, :-1]
            return jnp.concatenate([a, s], -1)

        def l2norm(t):
            return t / jnp.maximum(jnp.linalg.norm(t, axis=-1, keepdims=True), 1e-12)

        def rotate_half(x):
            x1, x2 = jnp.split(x, 2, -1)
            return jnp.concatenate([-x2, x1], -1)

        def rotary_tables(n):
            half = jnp.arange(0, DIM_HEAD, 2, dtype=jnp.float32)
            inv_freq = 1.0 / 10000.0 ** (half / DIM_HEAD)
            t = jnp.arange(n, dtype=jnp.float32)
            freqs = t[:, None] * inv_freq[None, :]
            freqs = jnp.concatenate([freqs, freqs], -1)
            base_scale = (half + 0.4 * DIM_HEAD) / (1.4 * DIM_HEAD)
            power = (t - n // 2) / (WINDOW // 2)
            scale = base_scale[None, :] ** power[:, None]
            scale = jnp.concatenate([scale, scale], -1)
            return (freqs, scale)

        def local_attention(q, k, v):
            b, h, n, d = q.shape
            w = WINDOW
            nw = n // w
            bq = q.reshape(b, h, nw, w, d)
            bk = k.reshape(b, h, nw, w, d)
            bv = v.reshape(b, h, nw, w, d)

            def look(t):
                p = jnp.pad(t, ((0, 0), (0, 0), (1, 0), (0, 0), (0, 0)))
                return jnp.concatenate([p[:, :, :nw], p[:, :, 1:]], axis=3)
            bk2, bv2 = (look(bk), look(bv))
            seq = jnp.arange(n).reshape(nw, w)
            seq_p = jnp.pad(seq, ((1, 0), (0, 0)), constant_values=-1)
            jt = jnp.concatenate([seq_p[:nw], seq_p[1:]], axis=1)
            it = seq[:, :, None]
            jb = jt[:, None, :]
            mask = (it < jb) | (it > jb + w) | (jb == -1)
            sim = jnp.einsum('bhwie,bhwje->bhwij', bq, bk2) * QK_SCALE
            sim = jnp.where(mask, -jnp.finfo(sim.dtype).max, sim)
            attn = jax.nn.softmax(sim, -1)
            out = jnp.einsum('bhwij,bhwje->bhwie', attn, bv2)
            return out.reshape(b, h, n, d)

        def attn_layer(x, Wqkv, qs, ksc, Wo):
            b, n, _ = x.shape
            qkv = x @ Wqkv
            q, k, v = jnp.split(qkv, 3, -1)
            sh = lambda t: t.reshape(b, n, HEADS, DIM_HEAD).transpose(0, 2, 1, 3)
            q, k, v = (sh(q), sh(k), sh(v))
            q = l2norm(q) * qs
            k = l2norm(k) * ksc
            freqs, scale = rotary_tables(n)
            cos, sin = (jnp.cos(freqs), jnp.sin(freqs))
            q = q * cos * scale + rotate_half(q) * sin * scale
            inv = 1.0 / scale
            k = k * cos * inv + rotate_half(k) * sin * inv
            out = local_attention(q, k, v)
            out = out.transpose(0, 2, 1, 3).reshape(b, n, INNER)
            return out @ Wo

        def ffn_layer(x, g, bln, W1, b1, W2, b2):
            mu = x.mean(-1, keepdims=True)
            var = ((x - mu) ** 2).mean(-1, keepdims=True)
            xn = (x - mu) / jnp.sqrt(var + 1e-05) * g + bln
            hg = xn @ W1 + b1
            a, gate = jnp.split(hg, 2, -1)
            return a * jax.nn.gelu(gate, approximate=False) @ W2 + b2
        for i in range(DEPTH):
            x = attn_layer(shift_tokens(x), Wqkv[i], q_scale[i], k_scale[i], Wo[i]) + x
            x = ffn_layer(shift_tokens(x), ln_g[i], ln_b[i], W1[i], b1[i], W2[i], b2[i]) + x
        return x
    x = L0_attn_x
    x = x + _L0_attn_ref(_layernorm(x, axis=-1), L0_attn_W_kqv, L0_attn_m)
    x = x + _L0_ffn_ref(_layernorm(x, axis=-1), L0_ffn_Wqkv, L0_ffn_q_scale, L0_ffn_k_scale, L0_ffn_Wo, L0_ffn_ln_g, L0_ffn_ln_b, L0_ffn_W1, L0_ffn_b1, L0_ffn_W2, L0_ffn_b2)
    return x

_drawn_inputs = setup_inputs


def setup_inputs(seed=0):
    import zlib

    import numpy as np

    out = dict(_drawn_inputs(seed))
    spreads = {'L0_ffn_q_scale': (1.0, 0.6),
     'L0_ffn_k_scale': (1.0, 0.6),
     'L0_ffn_ln_g': (1.0, 0.6),
     'L0_ffn_ln_b': (0.0, 0.8),
     'L0_ffn_b1': (0.0, 0.8),
     'L0_ffn_b2': (0.0, 0.1)}
    factors = {'L0_ffn_W1': 3.916, 'L0_ffn_W2': 3.829}
    for name, (base, spread) in spreads.items():
        noise = np.random.default_rng([zlib.crc32(name.encode()), seed]).standard_normal(out[name].shape)
        drawn = base * np.exp(spread * noise) if base else spread * noise
        out[name] = jnp.asarray(drawn.astype(out[name].dtype))
    for name, factor in factors.items():
        out[name] = (out[name] * factor).astype(out[name].dtype)
    return out
```

```python
from contextlib import ExitStack

import numpy as np

import concourse.bass as bass
from concourse import mybir

F32 = mybir.dt.float32
F32R = mybir.dt.float32r
BF16 = mybir.dt.bfloat16
ALU = mybir.AluOpType
ACT = mybir.ActivationFunctionType
AX_X = mybir.AxisListType.X

P = 128
SEQS, TOK, D = 4, 512, 128
CHUNKS = TOK // P
HEADS = 16
GLOBAL_DIM = D // HEADS
GROUP = 4
SLOT = P // GROUP
DEPTH = 6
DIM_HEAD = 64
INNER = HEADS * DIM_HEAD
PAIRS = INNER // P
WINDOW = 32
QK_SCALE = 8.0
KEYS = WINDOW + P
FFN = int(D * 4 * 2 / 3)
FFN_TILES = [(j * P, min(P, FFN - j * P)) for j in range(-(-FFN // P))]
NF = len(FFN_TILES)
BODIES = DEPTH * SEQS
LN_EPS = 1e-5
MASKED = -1e30
NORM_SHIFT = 20
NORM_CAP = 1e12
LN_EXP = "natural_log_exp_and_others"
V_TILES = 2 * (CHUNKS + 1)
Q_A, Q_B, K_A, K_B, V_W = range(5)


def rotary_constants():
    half = np.arange(0, DIM_HEAD, 2, dtype=np.float32)
    inv_freq = (1.0 / np.float32(10000.0) ** (half / DIM_HEAD)).astype(np.float32)
    t = np.arange(TOK, dtype=np.float32)
    freqs = t[:, None] * inv_freq[None, :]
    freqs = np.concatenate([freqs, freqs], -1)
    base = ((half + np.float32(0.4 * DIM_HEAD)) / np.float32(1.4 * DIM_HEAD)).astype(np.float32)
    power = ((t - TOK // 2) / np.float32(WINDOW // 2)).astype(np.float32)
    scale = base[None, :] ** power[:, None]
    scale = np.concatenate([scale, scale], -1).astype(np.float32)
    sign = np.where(np.arange(DIM_HEAD) < DIM_HEAD // 2, -1.0, 1.0).astype(np.float32)
    inv = np.float32(1.0) / scale
    tables = [np.cos(freqs) * scale * np.float32(QK_SCALE), np.sin(freqs) * sign * scale * np.float32(QK_SCALE),
              np.cos(freqs) * inv, np.sin(freqs) * sign * inv]
    return np.stack([np.concatenate([x.T, x.T], 0) for x in tables], 1).astype(np.float32)


def shape_constants():
    i = np.arange(P)[:, None]
    j = np.arange(KEYS)[None, :] - WINDOW
    seen = (j <= i) & (j >= i - WINDOW)
    local = np.stack([np.where(seen & (j >= 0), 0.0, MASKED), np.where(seen, 0.0, MASKED),
                      np.where(seen, 0.0, MASKED)], 1)
    causal = np.where(np.arange(P)[None, :] <= i, 0.0, MASKED)
    masks = np.concatenate([local.reshape(P, -1), causal, np.eye(P)], 1).astype(np.float32)
    eye = np.eye(P, dtype=np.float32)
    mean = np.full((P, P), 1.0 / D, np.float32)
    pair = (np.arange(P)[:, None] // DIM_HEAD == np.arange(P)[None, :] // DIM_HEAD).astype(np.float32)
    squares = np.concatenate([eye, mean, pair], 1)
    row = np.arange(P) % SLOT
    n = GLOBAL_DIM
    pos = np.arange(TOK, dtype=np.float32)[None, :]
    low_q = ((row >= n) & (row < 2 * n)).astype(np.float32)
    low_k = ((row >= 2 * n) & (row < 3 * n)).astype(np.float32)
    real = (row < 3 * n).astype(np.float32)
    q_pos = ((row == 3 * n + 2) | (row == 3 * n + 3))[:, None] * pos
    k_pos = ((row == 3 * n) | (row == 3 * n + 1))[:, None] * pos
    q_m_hi, q_m_lo = (row == 3 * n), (row == 3 * n + 1)
    k_m_hi, k_m_lo = (row == 3 * n + 2), (row == 3 * n + 3)
    cols = np.stack([low_q, low_k, real - 2 * low_q, real - 2 * low_k, q_m_hi, q_m_lo,
                     -1.0 * k_m_hi, -1.0 * k_m_lo,
                     np.full(P, LN_EPS), np.full(P, 2.0 ** -64), np.full(P, 0.5 * NORM_SHIFT * np.log(2.0)),
                     np.zeros(P)], 1).astype(np.float32)
    wide = np.concatenate([squares, q_pos, k_pos, cols], 1).astype(np.float32)
    return masks, np.ascontiguousarray(wide)


LOW_Q, LOW_K, SIGN_Q, SIGN_K, M_HI_Q, M_LO_Q, M_HI_K, M_LO_K, C_EPS, C_TINY, C_SHIFT, C_ZERO = range(12)


def build_program(nc, x, w_kqv, m, w_qkv, q_scale, k_scale, w_o, ln_g, ln_b, w_1, b_1, w_2, b_2,
                  rotary, masks, wide, out):
    with ExitStack() as ctx:
        def sb(name, shape, dt=F32):
            return ctx.enter_context(nc.sbuf_tensor(name, shape, dt))

        def sem(name):
            return ctx.enter_context(nc.semaphore(name))

        bank = [ctx.enter_context(nc.psum_tensor(f"bank{i}", [P, 512], F32)) for i in range(8)]

        mask_sb = sb("mask_sb", [P, 3 * KEYS + 2 * P], BF16)
        local_mask = mask_sb[:, 0:3 * KEYS]
        causal_mask = mask_sb[:, 3 * KEYS:3 * KEYS + P]
        eye16 = mask_sb[:, 3 * KEYS + P:3 * KEYS + 2 * P]
        wide_sb = sb("wide_sb", [P, 3 * P + 2 * TOK + 12])
        eye, mean_w, pair_ones = (wide_sb[:, i * P:(i + 1) * P] for i in range(3))
        q_pos = wide_sb[:, 3 * P:3 * P + TOK]
        k_pos = wide_sb[:, 3 * P + TOK:3 * P + 2 * TOK]

        def const(i, rows=P):
            return wide_sb[0:rows, 3 * P + 2 * TOK + i:3 * P + 2 * TOK + i + 1]

        zero = const(C_ZERO)
        scratch = sb("scratch", [P, 2])

        rot_sb = sb("rot_sb", [P, 4, TOK])
        scales = sb("scales", [P, 4, DEPTH])
        vecs = sb("vecs", [P, 3, DEPTH])
        b1_sb = sb("b1_sb", [P, 2 * NF, DEPTH])
        m_col = sb("m_col", [P, GROUP])

        x_tok = sb("x_tok", [P, SEQS * CHUNKS, D])
        state = sb("state", [P, SEQS * TOK])

        w_hi = sb("w_hi", [P, 5, PAIRS, P], F32R)
        w_lo = sb("w_lo", [P, 5, PAIRS, P], F32R)
        w_raw = sb("w_raw", [P, 2, 3, P])
        wo_sb = sb("wo_sb", [P, PAIRS, D])
        w1_raw = sb("w1_raw", [P, 2 * FFN])
        w1_hi = sb("w1_hi", [P, 2 * FFN], F32R)
        w1_lo = sb("w1_lo", [P, 2 * FFN], F32R)
        w2_sb = sb("w2_sb", [P, NF, D])

        parts_sb = sb("parts_sb", [P, 4, TOK], F32R)
        xs_hi, xs_lo, y_hi, y_lo = (parts_sb[:, i, :] for i in range(4))
        xe_hi = sb("xe_hi", [P, (CHUNKS - 1) * WINDOW], F32R)
        xe_lo = sb("xe_lo", [P, (CHUNKS - 1) * WINDOW], F32R)
        v_sb = sb("v_sb", [P, CHUNKS, INNER])
        v_edge = sb("v_edge", [(CHUNKS - 1) * WINDOW, INNER])
        sq = [sb("sq_q", [P, TOK]), sb("sq_k", [P, TOK])]
        r_norm = [sb("r_q", [P, TOK]), sb("r_k", [P, TOK])]
        t_cos = [sb("tc_q", [P, TOK]), sb("tc_k", [P, TOK])]
        t_sin = [sb("ts_q", [P, TOK]), sb("ts_k", [P, TOK])]
        rotated = [sb("rot_q", [P, TOK]), sb("rot_k", [P, TOK])]
        q_fin = sb("q_fin", [P, TOK])
        k_fin = sb("k_fin", [P, WINDOW + TOK])
        neg_max = sb("neg_max", [P, 2, 2 * CHUNKS])
        row_sum = sb("row_sum", [P, 2, 2 * CHUNKS])
        inv_sum = sb("inv_sum", [P, 2 * CHUNKS])
        probs = sb("probs", [P, 2, CHUNKS, 2, KEYS])
        probs_t = sb("probs_t", [P, 2, CHUNKS, P])
        edge_t = sb("edge_t", [(CHUNKS - 1) * WINDOW, CHUNKS - 1, 2 * WINDOW])
        o_tok = sb("o_tok", [P, CHUNKS, P])
        o_feat = sb("o_feat", [P, PAIRS, TOK])
        x_mid = sb("x_mid", [P, TOK])
        x_sh = sb("x_sh", [P, TOK])
        x_cen = sb("x_cen", [P, TOK])
        sq_f = sb("sq_f", [P, TOK])
        rstd_f = sb("rstd_f", [P, TOK])
        y_f = sq_f
        gates = sb("gates", [P, NF, TOK])
        values = sb("values", [P, NF, TOK])

        mask_raw = gates[:].rearrange("p a t -> p (a t)")[:, 0:3 * KEYS + 2 * P]
        wkqv_sb = values[:, 0, 0:3 * P]
        wq_pad = o_feat[:, 0, :]
        wk_pad = o_feat[:, 1, :]
        m_hi = r_norm[1][:, 0:GROUP]
        m_lo = r_norm[1][:, GROUP:2 * GROUP]
        m_cols = r_norm[1][:, 16:16 + 4 * GROUP]
        add_q = o_feat[:, 2:2 + GROUP, :]
        add_k = probs[:].rearrange("p a c h k -> p (a c h k)")[:, 0:GROUP * TOK].rearrange("p (g t) -> p g t", g=GROUP)
        qa = parts_sb
        ka = sb("ka", [P, GROUP, TOK], F32R)
        m_round = sb("m_round", [P, GROUP], F32R)
        stats = sq[0][:, 0:CHUNKS * 6].rearrange("p (c k) -> p c k", k=6)
        mean_var = sq[1][:, 0:CHUNKS * 2].rearrange("p (c k) -> p c k", k=2)
        rstd = r_norm[0][:, 0:CHUNKS]
        x_nrm = x_mid[:, :].rearrange("p (c d) -> p c d", c=CHUNKS)
        xn_t = x_sh
        part_hi = t_cos[0]
        scaled = t_sin[0]
        va = rotated[0][:, :].rearrange("p (c d) -> p c d", c=CHUNKS)
        p_glob = v_sb[:, :, 0:TOK]
        pt_glob = v_sb[:, :, TOK:2 * TOK]
        g_max = sb("g_max", [P, HEADS * CHUNKS])
        g_sum = sb("g_sum", [P, CHUNKS, HEADS])
        g_inv = sb("g_inv", [P, CHUNKS, HEADS])
        o_glob = o_tok

        s_const = sem("const_loaded")
        s_par = sem("params_loaded")
        s_zero = sem("zeroed")
        s_x = sem("x_loaded")
        s_raw = [sem(f"qkv_raw{i}_loaded") for i in range(2)]
        s_w = sem("qkv_split")
        p_hi = sem("pool_hi")
        p_lo = sem("pool_lo")
        p_w1 = sem("pool_w1")
        v0 = sem("dve_setup")
        s_wo = sem("wo_loaded")
        s_w1 = sem("w1_loaded")
        s_w1s = sem("w1_split")
        s_w2 = sem("w2_loaded")
        a_m = sem("a_m")
        a_stat = sem("a_stat")
        a_mv = sem("a_mv")
        a_ln = sem("a_ln")
        a_rstd = sem("a_rstd")
        a_xn = sem("a_xn")
        a_xt = sem("a_xt")
        a_xte = sem("a_xte")
        a_proj = sem("a_proj")
        a_scl = sem("a_scaled")
        a_hi = sem("a_hi")
        a_mix = sem("a_mix")
        a_qk = sem("a_qk")
        a_v = sem("a_v")
        a_ve = sem("a_ve")
        a_s = sem("a_scores")
        a_max = sem("a_max")
        a_exp = sem("a_exp")
        a_pt = sem("a_pt")
        a_pte = sem("a_pte")
        a_o = sem("a_o")
        a_inv = sem("a_inv")
        a_oe = sem("a_oe")
        a_x1 = sem("a_x1")
        a_yt = sem("a_yt")
        a_state = sem("a_state")
        s_xs = sem("xs_ready")
        s_xhi = sem("xs_hi_written")
        s_p = [sem("q_proj"), sem("k_proj")]
        s_sq = [sem("q_squared"), sem("k_squared")]
        s_mul = [sem("q_times_tables"), sem("k_times_tables")]
        s_rot = [sem("q_rotated"), sem("k_rotated")]
        s_n2 = [sem("q_norm2"), sem("k_norm2")]
        s_ln = [sem("q_ln"), sem("k_ln")]
        s_r = [sem("q_rnorm"), sem("k_rnorm")]
        s_fin = [sem("q_final"), sem("k_final")]
        s_v = sem("v_proj")
        s_ve = [sem("v_even_out"), sem("v_odd_out")]
        s_s = sem("scores")
        s_mx = sem("max_ready")
        s_e = sem("probs_ready")
        s_pt = sem("probs_turned")
        s_pte = [sem("probs_t0_out"), sem("probs_t1_out")]
        s_pp = sem("edge_turned")
        s_ppe = sem("edge_out")
        s_o = sem("attended")
        s_ri = sem("inv_sum_ready")
        s_oe = sem("o_tok_ready")
        s_ot = sem("o_turned")
        s_ote = sem("o_feat_ready")
        f_wo = sem("f_wo")
        f_mid = sem("f_mid")
        f_sh = sem("f_sh")
        f_mean = sem("f_mean")
        f_cen = sem("f_cen")
        f_sq = sem("f_sq")
        f_var = sem("f_var")
        f_ln = sem("f_ln")
        f_rstd = sem("f_rstd")
        f_n = sem("f_n")
        f_y = sem("f_y")
        f_yhi = sem("f_yhi")
        f_ylo = sem("f_ylo")
        f_h = sem("f_h")
        f_he = sem("f_he")
        f_gelu = sem("f_gelu")
        f_prod = sem("f_prod")
        f_w2 = sem("f_w2")
        f_x = sem("f_x")
        o_t = sem("o_t")
        o_e = sem("o_e")
        s_out = sem("out_stored")

        UNITS = HEADS * CHUNKS
        block = ctx.enter_context(nc.Block())

        @block.sync
        def _(sp):
            sp.dma_start(x_tok[:], x.rearrange("b (c p) d -> p (b c) d", p=P)).then_inc(s_x, 16)
            sp.dma_start(wide_sb[:], wide).then_inc(s_const, 16)
            sp.dma_start(mask_raw, masks).then_inc(s_const, 16)
            sp.dma_start(wkqv_sb, w_kqv).then_inc(s_const, 16)
            sp.wait_ge(s_zero, 1)
            for g in range(GROUP):
                for r in range(3 * GLOBAL_DIM, 3 * GLOBAL_DIM + 4):
                    sp.dma_start(m_col[r:r + SLOT * (GROUP - 1) + 1:SLOT, g:g + 1],
                                 m.rearrange("(g h) a b -> g h (a b)", g=GROUP)[g]).then_inc(s_const, 16)
            sp.dma_start(rot_sb[:], rotary).then_inc(s_par, 16)

            def load_pair(l, pair):
                sp.dma_start(w_raw[:, pair % 2, :, :],
                             w_qkv[l, :, :].rearrange("d (t n) -> d t n", t=3)[:, :, pair * P:(pair + 1) * P]
                             ).then_inc(s_raw[pair % 2], 16)

            def load_rest(l):
                if not isinstance(l, int):
                    sp.wait_ge(f_wo, SEQS * l)
                    sp.wait_ge(s_w1s, l)
                    sp.wait_ge(f_w2, SEQS * l)
                sp.dma_start(wo_sb[:], w_o[l, :, :].rearrange("(a p) n -> p a n", p=P)).then_inc(s_wo, 16)
                sp.dma_start(w1_raw[:], w_1[l, :, :]).then_inc(s_w1, 16)
                sp.dma_start(w2_sb[:, 0:NF - 1, :], w_2[l, 0:(NF - 1) * P, :].rearrange("(a p) n -> p a n", p=P)
                             ).then_inc(s_w2, 16)
                sp.dma_start(w2_sb[0:FFN_TILES[-1][1], NF - 1, :], w_2[l, (NF - 1) * P:FFN, :]).then_inc(s_w2, 16)

            for pair in range(PAIRS):
                if pair >= 2:
                    sp.wait_ge(s_w, pair - 1)
                load_pair(0, pair)
            with nc.allow_non_contiguous_dma("per-feature parameters, once"):
                half = DIM_HEAD // 2
                for i, src in enumerate((q_scale, k_scale)):
                    cols = src.rearrange("l d -> d l")
                    for h in range(2):
                        base = h * DIM_HEAD
                        sp.dma_start(scales[base:base + DIM_HEAD, 2 * i, :], cols).then_inc(s_par, 16)
                        sp.dma_start(scales[base:base + half, 2 * i + 1, :], cols[half:, :]).then_inc(s_par, 16)
                        sp.dma_start(scales[base + half:base + DIM_HEAD, 2 * i + 1, :], cols[:half, :]
                                     ).then_inc(s_par, 16)
                for i, src in enumerate((ln_g, ln_b, b_2)):
                    sp.dma_start(vecs[:, i, :], src.rearrange("l d -> d l")).then_inc(s_par, 16)
                for k, off in enumerate((FFN, 0)):
                    for j, (at, n) in enumerate(FFN_TILES):
                        sp.dma_start(b1_sb[0:n, k * NF + j, :], b_1[:, off + at:off + at + n].rearrange("l d -> d l")
                                     ).then_inc(s_par, 16)
            load_rest(0)
            with sp.Fori(1, DEPTH) as l:
                for pair in range(PAIRS):
                    sp.wait_ge(s_w, PAIRS * l + pair - 1)
                    load_pair(l, pair)
                load_rest(l)
            for s in range(SEQS):
                for c in range(CHUNKS):
                    i = s * CHUNKS + c
                    sp.wait_ge(o_e, i + 1)
                    sp.dma_start(out[s, c * P:(c + 1) * P, :], x_tok[:, i, :]).then_inc(s_out, 16)
            sp.wait_ge(s_out, 16 * SEQS * CHUNKS)

        PARAM_LOADS = 1 + 12 + 3 + 2 * NF
        CONST_LOADS = 3 + 4 * GROUP

        @block.gpsimd
        def _(pool):
            pool.memset(m_col[:], 0.0).then_inc(s_zero, 1)

            def split_pair(l, pair):
                loads = 16 * (PAIRS // 2 * l + pair // 2 + 1)
                split = PAIRS * l + pair + 1
                pool.wait_ge(s_raw[pair % 2], loads)
                hi, lo = w_hi[:, :, pair, :], w_lo[:, :, pair, :]
                raw = w_raw[:, pair % 2, :, :]
                pool.tensor_tensor(hi[:, 0:5:2, :], raw, zero.unsqueeze(2).to_broadcast([P, 3, P]), ALU.add
                                   ).then_inc(p_hi, 1)
                pool.wait_ge(p_hi, split)
                pool.tensor_tensor(lo[:, 0:5:2, :], raw, hi[:, 0:5:2, :].bitcast(F32), ALU.subtract).then_inc(p_lo, 1)
                pool.wait_ge(p_lo, split)
                last = None
                for part in (hi, lo):
                    for a in range(2):
                        view = part[:, 0:4, :].rearrange("p (t b) (h a d) -> p t b h a d", b=2, a=2, h=2)
                        last = pool.tensor_tensor(view[:, :, 1, :, a, :], view[:, :, 0, :, 1 - a, :].bitcast(F32),
                                                  zero.unsqueeze(2).unsqueeze(3).to_broadcast([P, 2, 2, DIM_HEAD // 2]), ALU.add)
                last.then_inc(s_w, 1)

            def add(n, i):
                pool.wait_ge(s_mul[i], n + 1)
                if not (isinstance(n, int) and n == 0):
                    pool.wait_ge(s_fin[i], n)
                pool.tensor_tensor(rotated[i][:], t_cos[i][:], t_sin[i][:], ALU.add).then_inc(s_rot[i], 1)

            def split_w1(l):
                pool.wait_ge(s_w1, 16 * (l + 1))
                pool.wait_ge(f_x, SEQS * l + 1)
                pool.tensor_tensor(w1_hi[:], w1_raw[:], zero.to_broadcast([P, 2 * FFN]), ALU.add).then_inc(p_w1, 1)
                pool.wait_ge(p_w1, l + 1)
                pool.tensor_tensor(w1_lo[:], w1_raw[:], w1_hi[:].bitcast(F32), ALU.subtract).then_inc(s_w1s, 1)

            def body(g, l_next=None, last=False):
                for p in range(PAIRS):
                    if not (last and p == PAIRS - 1):
                        add(PAIRS * g + p + 1, 0)
                        add(PAIRS * g + p + 1, 1)
                    if l_next is not None:
                        pool.wait_ge(s_p[1], PAIRS * g + p + 1)
                        pool.wait_ge(s_v, V_TILES * (g + 1))
                        split_pair(l_next, p)

            pool.wait_ge(s_const, 16 * CONST_LOADS)
            for pair in range(PAIRS):
                split_pair(0, pair)
            pool.wait_ge(a_o, UNITS * SEQS)
            add(0, 0)
            add(0, 1)

            def layer(l, last):
                body(SEQS * l)
                split_w1(l)
                with pool.Fori(1, SEQS - 1) as s:
                    body(SEQS * l + s)
                body(SEQS * l + SEQS - 1, None if last else l + 1, last)

            with pool.Fori(0, DEPTH - 1) as l:
                layer(l, False)
            layer(DEPTH - 1, True)

        @block.tensor
        def _(pe):
            def three(dst, lhs, rhs, stop=True):
                (lh, ll), (rh, rl) = lhs, rhs
                pe.matmul(dst, lh, rh, start=True, stop=False)
                pe.matmul(dst, lh, rl, start=False, stop=False)
                return pe.matmul(dst, ll, rh, start=False, stop=True)

            pe.wait_ge(s_const, 16 * CONST_LOADS)
            with pe.Fori(0, SEQS) as s:
                pe.wait_ge(a_xn, 2 * s + 1)
                for c in range(CHUNKS):
                    mm = pe.transpose(bank[0][:, c * P:(c + 1) * P], x_nrm[:, c, :], eye)
                mm.then_inc(a_xt, 1)
                pe.wait_ge(a_xte, s + 1)
                for i in range(2 * GROUP):
                    w = (wq_pad, wk_pad)[i % 2]
                    if i >= 2:
                        pe.wait_ge(a_qk, 2 * GROUP * s + i - 1)
                    elif i == 0:
                        pe.wait_ge(a_m, 1)
                    pe.matmul(bank[1 + i % 2][:], w[:, (i // 2) * P:(i // 2 + 1) * P], xn_t[:],
                              start=True, stop=True).then_inc(a_proj, 1)
                for c in range(CHUNKS):
                    mm = pe.matmul(bank[0][:, c * P:(c + 1) * P], xn_t[:, c * P:(c + 1) * P],
                                   wkqv_sb[:, 2 * P:3 * P], start=True, stop=True)
                mm.then_inc(a_v, 1)

                def scores(u):
                    h, c = divmod(u, CHUNKS)
                    grp, r = divmod(h, GROUP)
                    n = (c + 1) * P
                    dst = bank[3 + u % 2]
                    if u < 2:
                        pe.wait_ge(a_qk, 2 * GROUP * (s + 1))
                    if u >= 2:
                        pe.wait_ge(a_exp, UNITS * s + u - 1)
                    rows = slice(SLOT * r, SLOT * (r + 1))
                    pe.matmul(dst[:, 0:n], qa[rows, grp, c * P:(c + 1) * P], ka[rows, grp, 0:n],
                              start=True, stop=False)
                    pe.matmul(dst[:, n - P:n], eye16, causal_mask, start=False, stop=True).then_inc(a_s, 1)

                def turn(u):
                    h, c = divmod(u, CHUNKS)
                    pe.wait_ge(a_exp, UNITS * s + u + 1)
                    if u >= 2:
                        pe.wait_ge(a_pte, UNITS * s + u - 1)
                    for b in range(c + 1):
                        mm = pe.transpose(bank[5 + u % 2][:, b * P:(b + 1) * P], p_glob[:, u % 2, b * P:(b + 1) * P],
                                          eye)
                    mm.then_inc(a_pt, 1)

                def attend(u):
                    h, c = divmod(u, CHUNKS)
                    pe.wait_ge(a_pte, UNITS * s + u + 1)
                    if u == 0:
                        pe.wait_ge(a_ve, s + 1)
                    at = c * P + h * GLOBAL_DIM
                    for b in range(c + 1):
                        mm = pe.matmul(bank[7][:, at:at + GLOBAL_DIM], pt_glob[:, u % 2, b * P:(b + 1) * P],
                                       va[:, b, h * GLOBAL_DIM:(h + 1) * GLOBAL_DIM], start=(b == 0), stop=(b == c),
                                       skip_group_check=True)
                    mm.then_inc(a_o, 1)

                for u in range(UNITS + 2):
                    if u < UNITS:
                        scores(u)
                    if 1 <= u <= UNITS:
                        turn(u - 1)
                    if u >= 2:
                        attend(u - 2)
                pe.wait_ge(a_xn, 2 * s + 2)
                for c in range(CHUNKS):
                    mm = pe.transpose(bank[0][:, c * P:(c + 1) * P], x_nrm[:, c, :], eye)
                mm.then_inc(a_yt, 1)

            def project(n, g, p, i):
                if i == 0:
                    pe.wait_ge(s_w, PAIRS * (g // SEQS) + p + 1)
                    if p == 0:
                        pe.wait_ge(s_xs, g + 1)
                    if not (isinstance(n, int) and n == 0):
                        pe.wait_ge(s_mul[1], n)
                else:
                    pe.wait_ge(s_mul[0], n + 1)
                for b in range(2):
                    mm = three(bank[b][:], (w_hi[:, 2 * i + b, p, :], w_lo[:, 2 * i + b, p, :]), (xs_hi, xs_lo))
                mm.then_inc(s_p[i], 1)

            def norm2(n, i):
                pe.wait_ge(s_sq[i], n + 1)
                if i == 1:
                    pe.wait_ge(s_ln[0], n + 1)
                pe.matmul(bank[6][:], pair_ones, sq[i][:], start=True, stop=True).then_inc(s_n2[i], 1)

            def value_tiles(g, n):
                pe.wait_ge(s_w, PAIRS * (g // SEQS + 1))
                for t in range(V_TILES):
                    c, half = divmod(t, 2)
                    if t == 0:
                        pe.wait_ge(s_ln[1], n + 1)
                    elif t == 1:
                        if not (isinstance(g, int) and g == 0):
                            pe.wait_ge(f_x, g)
                    else:
                        pe.wait_ge(s_ve[t % 2], V_TILES // 2 * g + t // 2)
                    if c < CHUNKS:
                        lhs = (xs_hi[:, c * P:(c + 1) * P], xs_lo[:, c * P:(c + 1) * P])
                        dst = bank[6 + t % 2][:]
                    else:
                        lhs = (xe_hi[:], xe_lo[:])
                        dst = bank[6 + t % 2][0:(CHUNKS - 1) * WINDOW, :]
                    w = slice(half * PAIRS // 2, (half + 1) * PAIRS // 2)
                    three(dst, lhs, (w_hi[:, V_W, w, :], w_lo[:, V_W, w, :])).then_inc(s_v, 1)

            def local_scores(n, h):
                if h == 0:
                    pe.wait_ge(s_fin[0], n + 1)
                    pe.wait_ge(s_fin[1], n + 1)
                rows = slice(DIM_HEAD * h, DIM_HEAD * (h + 1))
                for b in range(2):
                    if h == 1:
                        pe.wait_ge(s_e, 4 * n + b + 1)
                    elif not (isinstance(n, int) and n == 0):
                        pe.wait_ge(s_e, 4 * n + b - 1)
                    dst = bank[2 + b]
                    pe.matmul(dst[:, 0:2 * KEYS], eye16, local_mask[:, b * KEYS:(b + 2) * KEYS], start=True, stop=False)
                    for c in range(2 * b, 2 * b + 2):
                        mm = pe.matmul(dst[:, (c % 2) * KEYS:(c % 2 + 1) * KEYS], q_fin[rows, c * P:(c + 1) * P],
                                       k_fin[rows, c * P:c * P + KEYS], start=False, stop=(c % 2 == 1))
                    mm.then_inc(s_s, 1)

            def turn_probs(n, g, p, h):
                pe.wait_ge(s_e, 4 * n + 2 * h + 2)
                if h == 0:
                    if not (isinstance(n, int) and n == 0):
                        pe.wait_ge(s_ote, n)
                else:
                    if p == 0:
                        pe.wait_ge(s_ve[0], V_TILES // 2 * (g + 1))
                    else:
                        pe.wait_ge(s_ln[1], n + 1)
                    pe.wait_ge(s_pte[0], n + 1)
                for c in range(CHUNKS):
                    mm = pe.transpose(bank[4][:, c * P:(c + 1) * P], probs[:, p % 2, c, h, WINDOW:KEYS], eye)
                mm.then_inc(s_pt, 1)

            def turn_edges(n, p):
                for h in range(2):
                    for c in range(1, CHUNKS):
                        rows = slice(WINDOW * (c - 1), WINDOW * c)
                        mm = pe.matmul(bank[6][rows, h * WINDOW:(h + 1) * WINDOW],
                                       probs[0:WINDOW, p % 2, c, h, 0:WINDOW], eye[0:WINDOW, 0:WINDOW],
                                       start=True, stop=True, skip_group_check=True)
                mm.then_inc(s_pp, 1)

            def attend_local(n, g, p, h):
                if h == 0:
                    pe.wait_ge(s_ppe, n + 1)
                    if p == 0:
                        pe.wait_ge(s_ve[0], V_TILES // 2 * (g + 1))
                        pe.wait_ge(s_ve[1], V_TILES // 2 * (g + 1))
                    if not (isinstance(n, int) and n == 0):
                        pe.wait_ge(s_oe, n)
                pe.wait_ge(s_pte[h], n + 1)
                cols = slice(p * P + h * DIM_HEAD, p * P + (h + 1) * DIM_HEAD)
                for c in range(CHUNKS):
                    at = c * P + h * DIM_HEAD
                    mm = pe.matmul(bank[5][:, at:at + DIM_HEAD], probs_t[:, h, c, :], v_sb[:, c, cols],
                                   start=True, stop=(c == 0), skip_group_check=True)
                    if c > 0:
                        mm = pe.matmul(bank[5][0:WINDOW, at:at + DIM_HEAD],
                                       edge_t[:, c - 1, h * WINDOW:(h + 1) * WINDOW], v_edge[:, cols],
                                       start=False, stop=True, skip_group_check=True)
                if h == 1:
                    mm.then_inc(s_o, 1)

            def turn_o(n):
                pe.wait_ge(s_oe, n + 1)
                pe.wait_ge(s_pte[1], n + 1)
                for c in range(CHUNKS):
                    mm = pe.transpose(bank[4][:, c * P:(c + 1) * P], o_tok[:, c, :], eye)
                mm.then_inc(s_ot, 1)

            def ffn_parts(f, after_values):
                l = f // SEQS

                def out_proj():
                    pe.wait_ge(s_ote, PAIRS * (f + 1))
                    pe.wait_ge(s_wo, 16 * (l + 1))
                    if after_values:
                        pe.wait_ge(s_ve[1], V_TILES // 2 * (f + 2))
                    else:
                        pe.wait_ge(f_x, f + 1)
                    for a in range(PAIRS):
                        mm = pe.matmul(bank[7][:], wo_sb[:, a, :], o_feat[:, a, :], start=(a == 0),
                                       stop=(a == PAIRS - 1))
                    mm.then_inc(f_wo, 1)

                def mean():
                    pe.wait_ge(f_sh, f + 1)
                    pe.matmul(bank[7][:], mean_w, x_sh[:], start=True, stop=True).then_inc(f_mean, 1)

                def var():
                    pe.wait_ge(f_sq, f + 1)
                    pe.matmul(bank[7][:], mean_w, sq_f[:], start=True, stop=True).then_inc(f_var, 1)

                def up(i):
                    def run():
                        at, n = FFN_TILES[i % NF]
                        off = at + (FFN if i < NF else 0)
                        if i == 0:
                            pe.wait_ge(f_ylo, f + 1)
                            pe.wait_ge(s_w1s, l + 1)
                        else:
                            pe.wait_ge(f_he, 2 * NF * f + i)
                        three(bank[7][0:n, :], (w1_hi[:, off:off + n], w1_lo[:, off:off + n]), (y_hi, y_lo)
                              ).then_inc(f_h, 1)
                    return run

                def down():
                    pe.wait_ge(f_prod, f + 1)
                    pe.wait_ge(s_w2, 32 * (l + 1))
                    for j, (_, n) in enumerate(FFN_TILES):
                        mm = pe.matmul(bank[7][:], w2_sb[0:n, j, :], gates[0:n, j, :], start=(j == 0),
                                       stop=(j == NF - 1))
                    mm.then_inc(f_w2, 1)

                return {(0, 1): out_proj, (1, 1): mean, (2, 1): var, (3, 0): up(0), (3, 1): up(1), (4, 0): up(2),
                        (4, 1): up(3), (5, 0): up(4), (5, 1): up(5), (6, 1): down}

            def body(g, first=False, last=False):
                parts = {} if first else ffn_parts(g - 1, True)
                for p in range(PAIRS):
                    n = PAIRS * g + p
                    nxt = not (last and p == PAIRS - 1)
                    gn, pn = (g, p + 1) if p + 1 < PAIRS else (g + 1, 0)
                    local_scores(n, 0)
                    if nxt:
                        project(n + 1, gn, pn, 0)
                    local_scores(n, 1)
                    if p == 0:
                        value_tiles(g, n)
                    if (p, 0) in parts:
                        parts[(p, 0)]()
                    turn_probs(n, g, p, 0)
                    if nxt:
                        project(n + 1, gn, pn, 1)
                    turn_probs(n, g, p, 1)
                    turn_edges(n, p)
                    if nxt:
                        pe.wait_ge(s_ppe, n + 1)
                        norm2(n + 1, 0)
                    attend_local(n, g, p, 0)
                    if (p, 1) in parts:
                        parts[(p, 1)]()
                    attend_local(n, g, p, 1)
                    if nxt:
                        norm2(n + 1, 1)
                    turn_o(n)

            project(0, 0, 0, 0)
            project(0, 0, 0, 1)
            norm2(0, 0)
            norm2(0, 1)
            body(0, first=True)
            with pe.Fori(1, BODIES - 1) as g:
                body(g)
            body(BODIES - 1, last=True)
            tail = ffn_parts(BODIES - 1, False)
            for key in sorted(tail):
                tail[key]()
            pe.wait_ge(f_x, BODIES + 1)
            for i in range(SEQS * CHUNKS // 4):
                if i >= 2:
                    pe.wait_ge(o_e, 4 * (i - 1))
                for c in range(4):
                    mm = pe.transpose(bank[i % 2][:, c * P:(c + 1) * P], state[:, (4 * i + c) * P:(4 * i + c + 1) * P],
                                      eye)
                mm.then_inc(o_t, 1)

        @block.scalar
        def _(act):
            def rstd_of(s, k):
                act.wait_ge(a_mv, 2 * s + k + 1)
                act.activation(rstd, mean_var[:, :, 1], ACT.Ln, bias=const(C_EPS)).then_inc(a_ln, 1)
                act.wait_ge(a_ln, 2 * s + k + 1)
                act.activation(rstd, rstd, ACT.Exp, scale=-0.5).then_inc(a_rstd, 1)

            act.preload_act_table_set(LN_EXP)
            act.wait_ge(s_const, 16 * CONST_LOADS)
            with act.Fori(0, SEQS) as s:
                rstd_of(s, 0)
                act.wait_ge(a_xt, s + 1)
                act.activation(xn_t[:], bank[0][:], ACT.Copy).then_inc(a_xte, 1)
                act.wait_ge(a_v, s + 1)
                act.activation(va, bank[0][:].rearrange("p (c d) -> p c d", c=CHUNKS), ACT.Copy).then_inc(a_ve, 1)
                for u in range(UNITS):
                    h, c = divmod(u, CHUNKS)
                    n = (c + 1) * P
                    act.wait_ge(a_max, UNITS * s + u + 1)
                    if u >= 2:
                        act.wait_ge(a_pt, UNITS * s + u - 1)
                    act.activation(p_glob[:, u % 2, 0:n], bank[3 + u % 2][:, 0:n], ACT.Exp,
                                   bias=g_max[:, u:u + 1], accum_out=g_sum[:, c, h:h + 1]).then_inc(a_exp, 1)
                rstd_of(s, 1)
                act.wait_ge(a_yt, s + 1)
                act.activation(state[:, bass.ds(s * TOK, TOK)], bank[0][:], ACT.Copy).then_inc(a_state, 1)

            def square(n, i):
                act.wait_ge(s_p[i], n + 1)
                if not (isinstance(n, int) and n == 0):
                    act.wait_ge(s_n2[i], n)
                act.activation(sq[i][:], bank[0][:], ACT.Square).then_inc(s_sq[i], 1)

            def rnorm(n, i):
                act.wait_ge(s_n2[i], n + 1)
                if not (isinstance(n, int) and n == 0):
                    act.wait_ge(s_fin[i], n)
                act.activation(r_norm[i][:], bank[6][:], ACT.Ln, bias=const(C_TINY),
                               scale=float(2 ** NORM_SHIFT)).then_inc(s_ln[i], 1)
                act.wait_ge(s_ln[i], n + 1)
                act.activation(r_norm[i][:], r_norm[i][:], ACT.Exp, bias=const(C_SHIFT), scale=-0.5).then_inc(s_r[i], 1)

            def exps(n, p, h):
                for b in range(2):
                    act.wait_ge(s_mx, 4 * n + 2 * h + b + 1)
                    if h == 0 and b == 0 and not (isinstance(n, int) and n < 2):
                        act.wait_ge(s_pp, n - 1)
                    for c in range(2 * b, 2 * b + 2):
                        at = (c % 2) * KEYS
                        one = act.activation(probs[:, p % 2, c, h, :], bank[2 + b][:, at:at + KEYS], ACT.Exp,
                                             bias=neg_max[:, h, c:c + 1],
                                             accum_out=row_sum[:, p % 2, 2 * c + h:2 * c + h + 1])
                    one.then_inc(s_e, 1)

            def ffn_parts(f):
                def square_f():
                    act.wait_ge(f_cen, f + 1)
                    act.activation(sq_f[:], x_cen[:], ACT.Square).then_inc(f_sq, 1)

                def rstd_f_():
                    act.wait_ge(f_var, f + 1)
                    act.activation(rstd_f[:], bank[7][:], ACT.Ln, bias=const(C_EPS)).then_inc(f_ln, 1)
                    act.wait_ge(f_ln, f + 1)
                    act.activation(rstd_f[:], rstd_f[:], ACT.Exp, scale=-0.5).then_inc(f_rstd, 1)

                def gelu():
                    act.preload_act_table(ACT.Gelu)
                    act.wait_ge(f_he, 2 * NF * f + NF)
                    n = FFN_TILES[-1][1]
                    act.activation(gates[:, 0:NF - 1, :], gates[:, 0:NF - 1, :], ACT.Gelu)
                    act.activation(gates[0:n, NF - 1, :], gates[0:n, NF - 1, :], ACT.Gelu).then_inc(f_gelu, 1)
                    act.preload_act_table_set(LN_EXP)

                return {1: square_f, 2: rstd_f_, 5: gelu}

            def body(g, first=False, last=False):
                parts = {} if first else ffn_parts(g - 1)
                for p in range(PAIRS):
                    n = PAIRS * g + p
                    nxt = not (last and p == PAIRS - 1)
                    exps(n, p, 0)
                    if nxt:
                        square(n + 1, 0)
                    if p == 0:
                        if not first:
                            act.wait_ge(s_o, PAIRS * g)
                        for t in range(0, V_TILES, 2):
                            act.wait_ge(s_v, V_TILES * g + t + 1)
                            c, half = divmod(t, 2)
                            cols = slice(half * INNER // 2, (half + 1) * INNER // 2)
                            if c < CHUNKS:
                                act.activation(v_sb[:, c, cols], bank[6][:], ACT.Copy).then_inc(s_ve[0], 1)
                            else:
                                act.activation(v_edge[:, cols], bank[6][0:(CHUNKS - 1) * WINDOW, :], ACT.Copy
                                               ).then_inc(s_ve[0], 1)
                    exps(n, p, 1)
                    if nxt:
                        square(n + 1, 1)
                    act.wait_ge(s_pt, 2 * n + 2)
                    if not (isinstance(n, int) and n == 0):
                        act.wait_ge(s_o, n)
                    act.activation(probs_t[:, 1, :, :], bank[4][:].rearrange("p (c q) -> p c q", c=CHUNKS), ACT.Copy
                                   ).then_inc(s_pte[1], 1)
                    if nxt:
                        rnorm(n + 1, 0)
                    if p in parts:
                        parts[p]()
                    if nxt:
                        rnorm(n + 1, 1)
                    act.wait_ge(s_ot, n + 1)
                    if p == 0 and not first:
                        act.wait_ge(f_wo, g)
                    act.activation(o_feat[:, p, :], bank[4][:], ACT.Copy).then_inc(s_ote, 1)

            square(0, 0)
            square(0, 1)
            rnorm(0, 0)
            rnorm(0, 1)
            body(0, first=True)
            with act.Fori(1, BODIES - 1) as g:
                body(g)
            body(BODIES - 1, last=True)
            tail = ffn_parts(BODIES - 1)
            for key in sorted(tail):
                tail[key]()

        @block.vector
        def _(dve):
            dve.memset(wq_pad[:], 0.0).then_inc(v0, 1)
            dve.memset(wk_pad[:], 0.0).then_inc(v0, 1)
            dve.memset(k_fin[:, 0:WINDOW], 0.0).then_inc(v0, 1)
            dve.memset(edge_t[:], 0.0).then_inc(v0, 1)
            dve.wait_ge(s_const, 16 * CONST_LOADS)
            dve.wait_ge(v0, 4)
            dve.tensor_copy(mask_sb[:], mask_raw).then_inc(v0, 1)
            n = GLOBAL_DIM
            for w, at in ((wq_pad, P), (wk_pad, 0)):
                for k in range(3):
                    dst = w.rearrange("p (h r) -> p h r", r=SLOT)[:, :, k * n:(k + 1) * n]
                    dve.tensor_copy(dst, wkqv_sb[:, at:at + P].rearrange("p (h r) -> p h r", r=n)).then_inc(v0, 1)
            dve.tensor_copy(m_round[:], m_col[:]).then_inc(v0, 1)
            dve.wait_ge(v0, 12)
            dve.tensor_tensor(m_lo, m_col[:], m_round[:].bitcast(F32), ALU.subtract).then_inc(v0, 1)
            dve.wait_ge(v0, 13)
            k = 13
            for i, (hi_row, lo_row) in enumerate(((M_HI_Q, M_LO_Q), (M_HI_K, M_LO_K))):
                dve.tensor_scalar(m_cols[:, 4 * i:4 * i + 4], m_lo, const(lo_row), None, ALU.mult).then_inc(v0, 1)
                k += 1
                dve.wait_ge(v0, k)
                dve.scalar_tensor_tensor(out=m_cols[:, 4 * i:4 * i + 4], in0=m_round[:].bitcast(F32),
                                         scalar=const(hi_row), in1=m_cols[:, 4 * i:4 * i + 4],
                                         op0=ALU.mult, op1=ALU.add).then_inc(v0, 1)
                k += 1
                dve.wait_ge(v0, k)
            for i, (dst, pos) in enumerate(((add_q, q_pos), (add_k, k_pos))):
                for grp in range(GROUP):
                    one = dve.tensor_scalar(dst[:, grp, :], pos, m_cols[:, 4 * i + grp:4 * i + grp + 1], None, ALU.add)
            one.then_inc(a_m, 1)
            dve.wait_ge(a_m, 1)
            dve.wait_ge(s_x, 16)

            def normalise(s, k, after_sum=False):
                if after_sum:
                    dve.wait_ge(a_x1, s + 1)
                    dve.memset(scratch[:, 0:1], 0.0)
                for c in range(CHUNKS):
                    one = dve.bn_stats(stats[:, c, :], x_tok[:, bass.ds(s * CHUNKS + c, 1), :].rearrange("p a d -> p (a d)"))
                one.then_inc(a_stat, 1)
                dve.wait_ge(a_stat, 2 * s + k + 1)
                dve.memset(scratch[:, 1:2], 0.0)
                for c in range(CHUNKS):
                    one = dve.bn_aggr(mean_var[:, c, :], stats[:, c, :])
                one.then_inc(a_mv, 1)
                dve.wait_ge(a_rstd, 2 * s + k + 1)
                for c in range(CHUNKS):
                    one = dve.tensor_scalar(x_nrm[:, c, :], x_tok[:, bass.ds(s * CHUNKS + c, 1), :].rearrange("p a d -> p (a d)"),
                                            mean_var[:, c, 0:1], rstd[:, c:c + 1], ALU.subtract, ALU.mult)
                one.then_inc(a_xn, 1)

            with dve.Fori(0, SEQS) as s:
                normalise(s, 0)
                for i in range(2 * GROUP):
                    grp, k = divmod(i, 2)
                    j = 2 * GROUP * s + i
                    dve.wait_ge(a_proj, j + 1)
                    if i > 0:
                        dve.wait_ge(a_qk, j)
                    src = bank[1 + k]
                    dve.tensor_scalar(scaled[:], src[:], (float(D) ** -0.5, 1.0)[k], None, ALU.mult).then_inc(a_scl, 1)
                    dve.wait_ge(a_scl, j + 1)
                    dve.tensor_copy(part_hi[:].bitcast(F32R), scaled[:]).then_inc(a_hi, 1)
                    dve.wait_ge(a_hi, j + 1)
                    dve.scalar_tensor_tensor(out=part_hi[:], in0=part_hi[:], scalar=const((SIGN_Q, SIGN_K)[k]),
                                             in1=(add_q, add_k)[k][:, grp, :], op0=ALU.mult, op1=ALU.add
                                             ).then_inc(a_mix, 1)
                    dve.wait_ge(a_mix, j + 1)
                    dve.scalar_tensor_tensor(out=(qa, ka)[k][:, grp, :], in0=scaled[:],
                                             scalar=const((LOW_Q, LOW_K)[k]), in1=part_hi[:],
                                             op0=ALU.mult, op1=ALU.add).then_inc(a_qk, 1)

                def turned(u):
                    h, c = divmod(u, CHUNKS)
                    m_ = (c + 1) * P
                    dve.wait_ge(a_pt, UNITS * s + u + 1)
                    if u >= 2:
                        dve.wait_ge(a_o, UNITS * s + u - 1)
                    dve.tensor_copy(pt_glob[:, u % 2, 0:m_], bank[5 + u % 2][:, 0:m_]).then_inc(a_pte, 1)

                for u in range(UNITS + 1):
                    if u < UNITS:
                        m_ = (u % CHUNKS + 1) * P
                        dve.wait_ge(a_s, UNITS * s + u + 1)
                        dve.tensor_reduce(g_max[:, u:u + 1], bank[3 + u % 2][:, 0:m_], AX_X, ALU.max,
                                          negate=True).then_inc(a_max, 1)
                    if u >= 1:
                        turned(u - 1)
                dve.wait_ge(a_exp, UNITS * (s + 1))
                dve.reciprocal(g_inv[:], g_sum[:]).then_inc(a_inv, 1)
                dve.wait_ge(a_inv, s + 1)
                dve.wait_ge(a_o, UNITS * (s + 1))
                dve.tensor_tensor(o_glob[:].rearrange("p c (h d) -> p c h d", h=HEADS),
                                  bank[7][:].rearrange("p (c h d) -> p c h d", c=CHUNKS, h=HEADS),
                                  g_inv[:].unsqueeze(3).to_broadcast([P, CHUNKS, HEADS, GLOBAL_DIM]),
                                  ALU.mult).then_inc(a_oe, 1)
                dve.wait_ge(a_oe, s + 1)
                xs_ = x_tok[:, bass.ds(s * CHUNKS, CHUNKS), :]
                dve.tensor_tensor(xs_, xs_, o_glob[:], ALU.add).then_inc(a_x1, 1)
                normalise(s, 1, True)

            dve.memset(xs_hi[DIM_HEAD:P, 0:1].bitcast(F32), 0.0).then_inc(v0, 1)
            dve.memset(xs_lo[DIM_HEAD:P, 0:1].bitcast(F32), 0.0).then_inc(v0, 1)
            dve.memset(x_sh[DIM_HEAD:P, 0:1], 0.0).then_inc(v0, 1)
            dve.wait_ge(v0, 20)
            HALF = D // 2

            def shifted_input(g, ready=None):
                at = (g % SEQS) * TOK
                if not (isinstance(g, int) and g < 2):
                    dve.wait_ge(f_x, g - 1)
                if not (isinstance(g, int) and g == 0):
                    dve.wait_ge(s_xs, g)
                src = (state[0:HALF, bass.ds(at, TOK)], state[HALF:P, bass.ds(at, TOK - 1)])
                dve.tensor_copy(xs_hi[0:HALF, :], src[0])
                dve.tensor_copy(xs_hi[HALF:P, 1:TOK], src[1]).then_inc(s_xhi, 1)
                dve.wait_ge(s_xhi, 2 * g + 1)
                dve.tensor_tensor(xs_lo[0:HALF, :], src[0], xs_hi[0:HALF, :].bitcast(F32), ALU.subtract)
                dve.tensor_tensor(xs_lo[HALF:P, 1:TOK], src[1], xs_hi[HALF:P, 1:TOK].bitcast(F32), ALU.subtract
                                  ).then_inc(s_xhi, 1)
                dve.wait_ge(s_xhi, 2 * g + 2)
                for full, edge in ((xs_hi, xe_hi), (xs_lo, xe_lo)):
                    view = full.bitcast(F32).rearrange("p (c t) -> p c t", t=P)[:, 0:CHUNKS - 1, P - WINDOW:P]
                    one = dve.tensor_copy(edge[:].rearrange("p (c t) -> p c t", t=WINDOW), view)
                one.then_inc(s_xs, 1)

            def times_tables(n, l, i):
                dve.wait_ge(s_p[i], n + 1)
                if not (isinstance(n, int) and n == 0):
                    dve.wait_ge(s_rot[i], n)
                dve.scalar_tensor_tensor(out=t_sin[i][:], in0=bank[1][:], scalar=scales[:, 2 * i + 1, bass.ds(l, 1)],
                                         in1=rot_sb[:, 2 * i + 1, :], op0=ALU.mult, op1=ALU.mult)
                dve.wait_ge(s_sq[i], n + 1)
                dve.scalar_tensor_tensor(out=t_cos[i][:], in0=bank[0][:], scalar=scales[:, 2 * i, bass.ds(l, 1)],
                                         in1=rot_sb[:, 2 * i, :], op0=ALU.mult, op1=ALU.mult).then_inc(s_mul[i], 1)

            def final(n, i):
                dve.wait_ge(s_r[i], n + 1)
                dve.wait_ge(s_rot[i], n + 1)
                if not (isinstance(n, int) and n == 0):
                    dve.wait_ge(s_s, 4 * n)
                dst = q_fin[:] if i == 0 else k_fin[:, WINDOW:]
                dve.scalar_tensor_tensor(out=dst, in0=r_norm[i][:], scalar=NORM_CAP, in1=rotated[i][:],
                                         op0=ALU.min, op1=ALU.mult).then_inc(s_fin[i], 1)

            def maxima(n, h):
                for b in range(2):
                    dve.wait_ge(s_s, 4 * n + 2 * h + b + 1)
                    if b == 0 and not (isinstance(n, int) and n == 0):
                        dve.wait_ge(s_e, 4 * n - 2 + 2 * h)
                    dve.tensor_reduce(neg_max[:, h, 2 * b:2 * b + 2],
                                      bank[2 + b][:, 0:2 * KEYS].rearrange("p (c k) -> p c k", c=2),
                                      AX_X, ALU.max, negate=True).then_inc(s_mx, 1)

            def ffn_parts(f):
                l = f // SEQS
                at = (f % SEQS) * TOK

                def mid():
                    dve.wait_ge(f_wo, f + 1)
                    dve.wait_ge(f_x, f + 1)
                    dve.tensor_tensor(x_mid[:], bank[7][:], state[:, bass.ds(at, TOK)], ALU.add).then_inc(f_mid, 1)
                    dve.wait_ge(f_mid, f + 1)
                    dve.tensor_copy(x_sh[0:HALF, :], x_mid[0:HALF, :])
                    dve.tensor_copy(x_sh[HALF:P, 1:TOK], x_mid[HALF:P, 0:TOK - 1]).then_inc(f_sh, 1)

                def centre():
                    dve.wait_ge(f_mean, f + 1)
                    dve.tensor_tensor(x_cen[:], x_sh[:], bank[7][:], ALU.subtract).then_inc(f_cen, 1)

                def norm():
                    dve.wait_ge(f_rstd, f + 1)
                    dve.tensor_tensor(x_cen[:], x_cen[:], rstd_f[:], ALU.mult).then_inc(f_n, 1)
                    dve.wait_ge(f_n, f + 1)
                    dve.tensor_scalar(y_f[:], x_cen[:], vecs[:, 0, bass.ds(l, 1)], vecs[:, 1, bass.ds(l, 1)],
                                      ALU.mult, ALU.add).then_inc(f_y, 1)
                    dve.wait_ge(f_y, f + 1)
                    dve.tensor_copy(y_hi, y_f[:]).then_inc(f_yhi, 1)
                    dve.wait_ge(f_yhi, f + 1)
                    dve.tensor_tensor(y_lo, y_f[:], y_hi.bitcast(F32), ALU.subtract).then_inc(f_ylo, 1)

                def up(i):
                    def run():
                        n = FFN_TILES[i % NF][1]
                        dve.wait_ge(f_h, 2 * NF * f + i + 1)
                        dst = (gates if i < NF else values)[0:n, i % NF, :]
                        dve.tensor_scalar(dst, bank[7][0:n, :], b1_sb[0:n, i, bass.ds(l, 1)], None, ALU.add
                                          ).then_inc(f_he, 1)
                    return run

                def product():
                    n = FFN_TILES[-1][1]
                    dve.wait_ge(f_gelu, f + 1)
                    dve.wait_ge(f_he, 2 * NF * (f + 1))
                    dve.tensor_tensor(gates[:, 0:NF - 1, :], gates[:, 0:NF - 1, :], values[:, 0:NF - 1, :], ALU.mult)
                    dve.tensor_tensor(gates[0:n, NF - 1, :], gates[0:n, NF - 1, :], values[0:n, NF - 1, :], ALU.mult
                                      ).then_inc(f_prod, 1)

                def residual():
                    dve.wait_ge(f_w2, f + 1)
                    dve.scalar_tensor_tensor(out=state[:, bass.ds(at, TOK)], in0=bank[7][:],
                                             scalar=vecs[:, 2, bass.ds(l, 1)], in1=x_mid[:],
                                             op0=ALU.add, op1=ALU.add).then_inc(f_x, 1)

                return {(0, 1): mid, (1, 1): centre, (2, 1): norm, (3, 0): up(0), (3, 1): up(1), (4, 0): up(2),
                        (4, 1): up(3), (5, 0): up(4), (5, 1): up(5), (6, 0): product, (6, 1): residual}

            def body(g, first=False, last=False):
                parts = {} if first else ffn_parts(g - 1)
                for p in range(PAIRS):
                    n = PAIRS * g + p
                    nxt = not (last and p == PAIRS - 1)
                    l = (g if p + 1 < PAIRS else g + 1) // SEQS
                    maxima(n, 0)
                    if nxt:
                        times_tables(n + 1, l, 0)
                    maxima(n, 1)
                    if p == 0:
                        if not first:
                            dve.wait_ge(s_o, PAIRS * g)
                        for t in range(1, V_TILES, 2):
                            dve.wait_ge(s_v, V_TILES * g + t + 1)
                            c, half = divmod(t, 2)
                            cols = slice(half * INNER // 2, (half + 1) * INNER // 2)
                            if c < CHUNKS:
                                dve.tensor_copy(v_sb[:, c, cols], bank[7][:]).then_inc(s_ve[1], 1)
                            else:
                                dve.tensor_copy(v_edge[:, cols], bank[7][0:(CHUNKS - 1) * WINDOW, :]
                                                ).then_inc(s_ve[1], 1)
                    if (p, 0) in parts:
                        parts[(p, 0)]()
                    dve.wait_ge(s_pt, 2 * n + 1)
                    if not (isinstance(n, int) and n == 0):
                        dve.wait_ge(s_o, n)
                    dve.tensor_copy(probs_t[:, 0, :, :], bank[4][:].rearrange("p (c q) -> p c q", c=CHUNKS)
                                    ).then_inc(s_pte[0], 1)
                    if nxt:
                        times_tables(n + 1, l, 1)
                    dve.wait_ge(s_pp, n + 1)
                    for c in range(CHUNKS - 1):
                        rows = slice(WINDOW * c, WINDOW * (c + 1))
                        one = dve.tensor_copy(edge_t[rows, c, :], bank[6][rows, 0:2 * WINDOW])
                    one.then_inc(s_ppe, 1)
                    dve.wait_ge(s_e, 4 * n + 4)
                    if not (isinstance(n, int) and n == 0):
                        dve.wait_ge(s_oe, n)
                    dve.reciprocal(inv_sum[:], row_sum[:, p % 2, :]).then_inc(s_ri, 1)
                    if nxt:
                        final(n + 1, 0)
                    if p == PAIRS - 2 and not last:
                        dve.wait_ge(s_p[1], PAIRS * (g + 1))
                        dve.wait_ge(s_v, V_TILES * (g + 1))
                        shifted_input(g + 1)
                    if (p, 1) in parts:
                        parts[(p, 1)]()
                    dve.wait_ge(s_o, n + 1)
                    dve.wait_ge(s_ri, n + 1)
                    if not (isinstance(n, int) and n == 0):
                        dve.wait_ge(s_ot, n)
                    dve.tensor_tensor(o_tok[:].rearrange("p c (h d) -> p (c h) d", h=2),
                                      bank[5][:].rearrange("p (c d) -> p c d", d=DIM_HEAD),
                                      inv_sum[:].unsqueeze(2).to_broadcast([P, 2 * CHUNKS, DIM_HEAD]), ALU.mult
                                      ).then_inc(s_oe, 1)
                    if nxt:
                        final(n + 1, 1)

            dve.wait_ge(s_par, 16 * PARAM_LOADS)
            dve.wait_ge(a_state, SEQS)
            dve.memset(scratch[:, 0:1], 0.0).then_inc(f_x, 1)
            shifted_input(0)
            times_tables(0, 0, 0)
            times_tables(0, 0, 1)
            final(0, 0)
            final(0, 1)
            body(0, first=True)
            with dve.Fori(1, BODIES - 1) as g:
                body(g)
            body(BODIES - 1, last=True)
            tail = ffn_parts(BODIES - 1)
            for key in sorted(tail):
                tail[key]()
            for i in range(SEQS * CHUNKS):
                dve.wait_ge(o_t, i // 4 + 1)
                dve.tensor_tensor(x_tok[:, i, :], x_tok[:, i, :], bank[(i // 4) % 2][:, (i % 4) * P:(i % 4 + 1) * P],
                                  ALU.add).then_inc(o_e, 1)


_INS = ['L0_attn_x', 'L0_attn_W_kqv', 'L0_attn_m', 'L0_ffn_Wqkv', 'L0_ffn_q_scale', 'L0_ffn_k_scale', 'L0_ffn_Wo',
        'L0_ffn_ln_g', 'L0_ffn_ln_b', 'L0_ffn_W1', 'L0_ffn_b1', 'L0_ffn_W2', 'L0_ffn_b2']


def kernel(**inputs):
    import concourse.bacc as bacc
    from concourse.bass_utils import run_bass_kernel_spmd

    nc = bacc.Bacc("TRN2", target_bir_lowering=False, num_devices=1)
    arrays, args = {}, []
    masks, wide = shape_constants()
    host = [(name, np.ascontiguousarray(inputs[name])) for name in _INS]
    host += [("rotary", rotary_constants()), ("masks", masks), ("wide", wide)]
    for name, a in host:
        arrays[f"in_{name}"] = a
        args.append(nc.dram_tensor(f"in_{name}", a.shape, mybir.dt.from_np(a.dtype), kind="ExternalInput").ap())
    out = nc.dram_tensor("out_0", (SEQS, TOK, D), F32, kind="ExternalOutput").ap()
    build_program(nc, *args, out)
    r = run_bass_kernel_spmd(nc, [arrays], core_ids=[0])
    return r.results[0]["out_0"]
```

```python
from contextlib import ExitStack

import numpy as np

import concourse.bass as bass
from concourse import mybir

F32 = mybir.dt.float32
F32R = mybir.dt.float32r
BF16 = mybir.dt.bfloat16
ALU = mybir.AluOpType
ACT = mybir.ActivationFunctionType
AX_X = mybir.AxisListType.X

P = 128
SEQS, TOK, D = 4, 512, 128
CHUNKS = TOK // P
HEADS = 16
GLOBAL_DIM = D // HEADS
GROUP = 4
SLOT = P // GROUP
DEPTH = 6
DIM_HEAD = 64
INNER = HEADS * DIM_HEAD
PAIRS = INNER // P
WINDOW = 32
QK_SCALE = 8.0
KEYS = WINDOW + P
FFN = int(D * 4 * 2 / 3)
FFN_TILES = [(j * P, min(P, FFN - j * P)) for j in range(-(-FFN // P))]
NF = len(FFN_TILES)
BODIES = DEPTH * SEQS
LN_EPS = 1e-5
MASKED = -1e30
NORM_SHIFT = 20
NORM_CAP = 1e12
LN_EXP = "natural_log_exp_and_others"
V_TILES = 2 * CHUNKS
SPAN = 3 * DIM_HEAD
Q_A, Q_B, K_A, K_B, V_W = range(5)


def rotary_constants():
    half = np.arange(0, DIM_HEAD, 2, dtype=np.float32)
    inv_freq = (1.0 / np.float32(10000.0) ** (half / DIM_HEAD)).astype(np.float32)
    t = np.arange(TOK, dtype=np.float32)
    freqs = t[:, None] * inv_freq[None, :]
    freqs = np.concatenate([freqs, freqs], -1)
    base = ((half + np.float32(0.4 * DIM_HEAD)) / np.float32(1.4 * DIM_HEAD)).astype(np.float32)
    power = ((t - TOK // 2) / np.float32(WINDOW // 2)).astype(np.float32)
    scale = base[None, :] ** power[:, None]
    scale = np.concatenate([scale, scale], -1).astype(np.float32)
    sign = np.where(np.arange(DIM_HEAD) < DIM_HEAD // 2, -1.0, 1.0).astype(np.float32)
    inv = np.float32(1.0) / scale
    tables = [np.cos(freqs) * scale * np.float32(QK_SCALE), np.sin(freqs) * sign * scale * np.float32(QK_SCALE),
              np.cos(freqs) * inv, np.sin(freqs) * sign * inv]
    return np.stack([np.concatenate([x.T, x.T], 0) for x in tables], 1).astype(np.float32)


def shape_constants():
    i = np.arange(P)[:, None]
    j = np.arange(KEYS)[None, :] - WINDOW
    seen = (j <= i) & (j >= i - WINDOW)
    local = np.stack([np.where(seen & (j >= 0), 0.0, MASKED), np.where(seen, 0.0, MASKED),
                      np.where(seen, 0.0, MASKED)], 1)
    key, query = np.arange(P)[:, None], np.arange(KEYS)[None, :]
    turned = np.where((query >= key) & (query <= key + WINDOW), 0.0, MASKED)
    causal = np.where(np.arange(P)[None, :] <= i, 0.0, MASKED)
    masks = np.concatenate([local.reshape(P, -1), turned, turned, causal, np.eye(P)], 1).astype(np.float32)
    eye = np.eye(P, dtype=np.float32)
    mean = np.full((P, P), 1.0 / D, np.float32)
    pair = (np.arange(P)[:, None] // DIM_HEAD == np.arange(P)[None, :] // DIM_HEAD).astype(np.float32)
    squares = np.concatenate([eye, mean, pair], 1)
    row = np.arange(P) % SLOT
    n = GLOBAL_DIM
    pos = np.arange(TOK, dtype=np.float32)[None, :]
    low_q = ((row >= n) & (row < 2 * n)).astype(np.float32)
    low_k = ((row >= 2 * n) & (row < 3 * n)).astype(np.float32)
    real = (row < 3 * n).astype(np.float32)
    q_pos = ((row == 3 * n + 2) | (row == 3 * n + 3))[:, None] * pos
    k_pos = ((row == 3 * n) | (row == 3 * n + 1))[:, None] * pos
    q_m_hi, q_m_lo = (row == 3 * n), (row == 3 * n + 1)
    k_m_hi, k_m_lo = (row == 3 * n + 2), (row == 3 * n + 3)
    cols = np.stack([low_q, low_k, real - 2 * low_q, real - 2 * low_k, q_m_hi, q_m_lo,
                     -1.0 * k_m_hi, -1.0 * k_m_lo,
                     np.full(P, LN_EPS), np.full(P, 2.0 ** -64), np.full(P, 0.5 * NORM_SHIFT * np.log(2.0)),
                     np.zeros(P)], 1).astype(np.float32)
    wide = np.concatenate([squares, q_pos, k_pos, cols], 1).astype(np.float32)
    return masks, np.ascontiguousarray(wide)


LOW_Q, LOW_K, SIGN_Q, SIGN_K, M_HI_Q, M_LO_Q, M_HI_K, M_LO_K, C_EPS, C_TINY, C_SHIFT, C_ZERO = range(12)


def build_program(nc, x, w_kqv, m, w_qkv, q_scale, k_scale, w_o, ln_g, ln_b, w_1, b_1, w_2, b_2,
                  rotary, masks, wide, out):
    with ExitStack() as ctx:
        def sb(name, shape, dt=F32):
            return ctx.enter_context(nc.sbuf_tensor(name, shape, dt))

        def sem(name):
            return ctx.enter_context(nc.semaphore(name))

        bank = [ctx.enter_context(nc.psum_tensor(f"bank{i}", [P, 512], F32)) for i in range(8)]

        mask_sb = sb("mask_sb", [P, 5 * KEYS + 2 * P], BF16)
        local_mask = mask_sb[:, 0:3 * KEYS]
        local_mask_t = mask_sb[:, 3 * KEYS:5 * KEYS]
        causal_mask = mask_sb[:, 5 * KEYS:5 * KEYS + P]
        eye16 = mask_sb[:, 5 * KEYS + P:5 * KEYS + 2 * P]
        ones16 = sb("ones16", [1, P], BF16)
        wide_sb = sb("wide_sb", [P, 3 * P + 2 * TOK + 12])
        eye, mean_w, pair_ones = (wide_sb[:, i * P:(i + 1) * P] for i in range(3))
        q_pos = wide_sb[:, 3 * P:3 * P + TOK]
        k_pos = wide_sb[:, 3 * P + TOK:3 * P + 2 * TOK]

        def const(i, rows=P):
            return wide_sb[0:rows, 3 * P + 2 * TOK + i:3 * P + 2 * TOK + i + 1]

        zero = const(C_ZERO)
        scratch = sb("scratch", [P, 2])

        rot_sb = sb("rot_sb", [P, 4, TOK])
        scales = sb("scales", [P, 4, DEPTH])
        vecs = sb("vecs", [P, 3, DEPTH])
        b1_sb = sb("b1_sb", [P, 2 * NF, DEPTH])
        m_col = sb("m_col", [P, GROUP])

        x_tok = sb("x_tok", [P, SEQS * CHUNKS, D])
        state = sb("state", [P, SEQS * TOK])

        w_hi = sb("w_hi", [P, 5, PAIRS, P], F32R)
        w_lo = sb("w_lo", [P, 5, PAIRS, P], F32R)
        w_raw = sb("w_raw", [P, 2, 3, P])
        wo_sb = sb("wo_sb", [P, PAIRS, D])
        w1_raw = sb("w1_raw", [P, 2 * FFN])
        w1_hi = sb("w1_hi", [P, 2 * FFN], F32R)
        w1_lo = sb("w1_lo", [P, 2 * FFN], F32R)
        w2_sb = sb("w2_sb", [P, NF, D])

        parts_sb = sb("parts_sb", [P, 4, TOK], F32R)
        xs_hi, xs_lo, y_hi, y_lo = (parts_sb[:, i, :] for i in range(4))
        v_sb = sb("v_sb", [P, CHUNKS, PAIRS, SPAN])
        sq = [sb("sq_q", [P, TOK]), sb("sq_k", [P, TOK])]
        r_norm = [sb("r_q", [P, TOK]), sb("r_k", [P, TOK])]
        t_cos = [sb("tc_q", [P, TOK]), sb("tc_k", [P, TOK])]
        t_sin = [sb("ts_q", [P, TOK]), sb("ts_k", [P, TOK])]
        rotated = [sb("rot_q", [P, TOK]), sb("rot_k", [P, TOK])]
        fin = sb("fin", [P, 4, TOK])
        q_fin, k_fin = fin[:, 0:2, :], fin[:, 2:4, :]
        q16 = sb("q16", [P, 2, TOK], BF16)
        k16 = sb("k16", [P, 2, WINDOW + TOK], BF16)
        neg_max = sb("neg_max", [P, 2, CHUNKS], BF16)
        neg_row = sb("neg_row", [1, 2, TOK], BF16)
        probs_t = sb("probs_t", [P, 2, CHUNKS * KEYS - WINDOW])
        inv_sums = sb("inv_sums", [P, TOK])
        o_feat = sb("o_feat", [P, PAIRS, TOK])
        x_mid = sb("x_mid", [P, TOK])
        x_sh = sb("x_sh", [P, TOK])
        x_cen = sb("x_cen", [P, TOK])
        sq_f = sb("sq_f", [P, TOK])
        rstd_f = sb("rstd_f", [P, TOK])
        y_f = sq_f
        gates = sb("gates", [P, NF, TOK])
        values = sb("values", [P, NF, TOK])

        mask_raw = gates[:].rearrange("p a t -> p (a t)")[:, 0:5 * KEYS + 2 * P]
        wkqv_sb = values[:, 0, 0:3 * P]
        wq_pad = o_feat[:, 0, :]
        wk_pad = o_feat[:, 1, :]
        m_hi = r_norm[1][:, 0:GROUP]
        m_lo = r_norm[1][:, GROUP:2 * GROUP]
        m_cols = r_norm[1][:, 16:16 + 4 * GROUP]
        add_q = o_feat[:, 2:2 + GROUP, :]
        add_k = fin
        qa = parts_sb
        m_round = sb("m_round", [P, GROUP], F32R)
        stats = sq[0][:, 0:CHUNKS * 6].rearrange("p (c k) -> p c k", k=6)
        mean_var = sq[1][:, 0:CHUNKS * 2].rearrange("p (c k) -> p c k", k=2)
        rstd = r_norm[0][:, 0:CHUNKS]
        x_nrm = x_mid[:, :].rearrange("p (c d) -> p c d", c=CHUNKS)
        xn_t = x_sh
        part_hi = t_cos[0]
        scaled = t_sin[0]
        va = rotated[0][:, :].rearrange("p (c d) -> p c d", c=CHUNKS)
        v_flat = v_sb[:].rearrange("p c a d -> p c (a d)")
        p_glob = v_flat[:, :, 0:TOK]
        pt_glob = v_flat[:, :, TOK:2 * TOK]
        ka_rest = sb("ka_rest", [P, GROUP - 2, TOK], F32R)
        ka = [w1_hi[:, 0:TOK], w1_lo[:, 0:TOK]] + [ka_rest[:, i, :] for i in range(GROUP - 2)]
        g_max = sb("g_max", [P, HEADS * CHUNKS])
        g_sum = sb("g_sum", [P, CHUNKS, HEADS])
        g_inv = sb("g_inv", [P, CHUNKS, HEADS])
        o_glob = rotated[1][:, :].rearrange("p (c d) -> p c d", c=CHUNKS)

        s_const = sem("const_loaded")
        s_par = sem("params_loaded")
        s_zero = sem("zeroed")
        s_x = sem("x_loaded")
        s_raw = [sem(f"qkv_raw{i}_loaded") for i in range(2)]
        s_w = sem("qkv_split")
        p_hi = sem("pool_hi")
        p_lo = sem("pool_lo")
        p_w1 = sem("pool_w1")
        v0 = sem("dve_setup")
        s_wo = sem("wo_loaded")
        s_w1 = sem("w1_loaded")
        s_w1s = sem("w1_split")
        s_w2 = sem("w2_loaded")
        a_m = sem("a_m")
        a_stat = sem("a_stat")
        a_mv = sem("a_mv")
        a_ln = sem("a_ln")
        a_rstd = sem("a_rstd")
        a_xn = sem("a_xn")
        a_xt = sem("a_xt")
        a_xte = sem("a_xte")
        a_proj = sem("a_proj")
        a_hi = sem("a_hi")
        a_mix = sem("a_mix")
        a_qk = sem("a_qk")
        a_v = sem("a_v")
        a_ve = sem("a_ve")
        a_s = sem("a_scores")
        a_max = sem("a_max")
        a_exp = sem("a_exp")
        a_pt = sem("a_pt")
        a_pte = sem("a_pte")
        a_o = sem("a_o")
        a_inv = sem("a_inv")
        a_oe = sem("a_oe")
        a_x1 = sem("a_x1")
        a_yt = sem("a_yt")
        a_state = sem("a_state")
        s_xs = sem("xs_ready")
        s_xhi = sem("xs_hi_written")
        s_p = [sem("q_proj"), sem("k_proj")]
        s_sq = [sem("q_squared"), sem("k_squared")]
        s_mul = [sem("q_times_tables"), sem("k_times_tables")]
        s_rot = [sem("q_rotated"), sem("k_rotated")]
        s_n2 = [sem("q_norm2"), sem("k_norm2")]
        s_ln = [sem("q_ln"), sem("k_ln")]
        s_r = [sem("q_rnorm"), sem("k_rnorm")]
        s_fin = [sem("q_final"), sem("k_final")]
        s_v = sem("v_proj")
        s_ve = [sem("v_even_out"), sem("v_odd_out")]
        s_16 = [sem("q_rounded"), sem("k_rounded")]
        s_s = sem("rounded_scores")
        s_mx = sem("max_ready")
        s_tm = sem("max_turned")
        s_nm = sem("max_row_ready")
        s_st = sem("turned_scores")
        s_e = sem("probs_ready")
        s_o = sem("attended")
        s_lns = sem("sums_ln")
        s_sum = sem("inv_sums_ready")
        s_nrm = sem("o_feat_ready")
        f_wo = sem("f_wo")
        f_mid = sem("f_mid")
        f_sh = sem("f_sh")
        f_mean = sem("f_mean")
        f_cen = sem("f_cen")
        f_sq = sem("f_sq")
        f_var = sem("f_var")
        f_ln = sem("f_ln")
        f_rstd = sem("f_rstd")
        f_y = sem("f_y")
        f_yhi = sem("f_yhi")
        f_ylo = sem("f_ylo")
        f_h = sem("f_h")
        f_he = sem("f_he")
        f_gelu = sem("f_gelu")
        f_prod = sem("f_prod")
        f_w2 = sem("f_w2")
        f_x = sem("f_x")
        o_t = sem("o_t")
        o_e = sem("o_e")
        s_out = sem("out_stored")

        UNITS = HEADS * CHUNKS
        SCORE_BANKS, TURN_BANKS = (3, 4, 0), (5, 6, 2)
        PROJECT_AT = {(i // 2 - 1) * GROUP * CHUNKS + 4 + 5 * (i % 2): i for i in range(2, 2 * GROUP)}

        def value_place(t):
            c, half = divmod(t, 2)
            pairs = slice(half * PAIRS // 2, (half + 1) * PAIRS // 2)
            return v_sb[:, c, pairs, :].rearrange("p a (x d) -> p a x d", d=DIM_HEAD)[:, :, 0:3:2, :]

        def value_source(t):
            return bank[6 + t % 2][:].rearrange("p (a x d) -> p a x d", x=2, d=DIM_HEAD)

        block = ctx.enter_context(nc.Block())

        @block.sync
        def _(sp):
            sp.dma_start(x_tok[:], x.rearrange("b (c p) d -> p (b c) d", p=P)).then_inc(s_x, 16)
            sp.dma_start(wide_sb[:], wide).then_inc(s_const, 16)
            sp.dma_start(mask_raw, masks).then_inc(s_const, 16)
            sp.dma_start(wkqv_sb, w_kqv).then_inc(s_const, 16)
            sp.wait_ge(s_zero, 1)
            for g in range(GROUP):
                for r in range(3 * GLOBAL_DIM, 3 * GLOBAL_DIM + 4):
                    sp.dma_start(m_col[r:r + SLOT * (GROUP - 1) + 1:SLOT, g:g + 1],
                                 m.rearrange("(g h) a b -> g h (a b)", g=GROUP)[g]).then_inc(s_const, 16)
            sp.dma_start(rot_sb[:], rotary).then_inc(s_par, 16)

            def load_pair(l, pair):
                sp.dma_start(w_raw[:, pair % 2, :, :],
                             w_qkv[l, :, :].rearrange("d (t n) -> d t n", t=3)[:, :, pair * P:(pair + 1) * P]
                             ).then_inc(s_raw[pair % 2], 16)

            def load_rest(l):
                if not isinstance(l, int):
                    sp.wait_ge(f_wo, SEQS * l)
                    sp.wait_ge(s_w1s, l)
                    sp.wait_ge(f_w2, SEQS * l)
                sp.dma_start(wo_sb[:], w_o[l, :, :].rearrange("(a p) n -> p a n", p=P)).then_inc(s_wo, 16)
                sp.dma_start(w1_raw[:], w_1[l, :, :]).then_inc(s_w1, 16)
                sp.dma_start(w2_sb[:, 0:NF - 1, :], w_2[l, 0:(NF - 1) * P, :].rearrange("(a p) n -> p a n", p=P)
                             ).then_inc(s_w2, 16)
                sp.dma_start(w2_sb[0:FFN_TILES[-1][1], NF - 1, :], w_2[l, (NF - 1) * P:FFN, :]).then_inc(s_w2, 16)

            for pair in range(PAIRS):
                if pair >= 2:
                    sp.wait_ge(s_w, pair - 1)
                load_pair(0, pair)
            with nc.allow_non_contiguous_dma("per-feature parameters, once"):
                half = DIM_HEAD // 2
                for i, src in enumerate((q_scale, k_scale)):
                    cols = src.rearrange("l d -> d l")
                    for h in range(2):
                        base = h * DIM_HEAD
                        sp.dma_start(scales[base:base + DIM_HEAD, 2 * i, :], cols).then_inc(s_par, 16)
                        sp.dma_start(scales[base:base + half, 2 * i + 1, :], cols[half:, :]).then_inc(s_par, 16)
                        sp.dma_start(scales[base + half:base + DIM_HEAD, 2 * i + 1, :], cols[:half, :]
                                     ).then_inc(s_par, 16)
                for i, src in enumerate((ln_g, ln_b, b_2)):
                    sp.dma_start(vecs[:, i, :], src.rearrange("l d -> d l")).then_inc(s_par, 16)
                for k, off in enumerate((FFN, 0)):
                    for j, (at, n) in enumerate(FFN_TILES):
                        sp.dma_start(b1_sb[0:n, k * NF + j, :], b_1[:, off + at:off + at + n].rearrange("l d -> d l")
                                     ).then_inc(s_par, 16)
            load_rest(0)
            with sp.Fori(1, DEPTH) as l:
                for pair in range(PAIRS):
                    sp.wait_ge(s_w, PAIRS * l + pair - 1)
                    load_pair(l, pair)
                load_rest(l)
            for s in range(SEQS):
                for c in range(CHUNKS):
                    i = s * CHUNKS + c
                    sp.wait_ge(o_e, i + 1)
                    sp.dma_start(out[s, c * P:(c + 1) * P, :], x_tok[:, i, :]).then_inc(s_out, 16)
            sp.wait_ge(s_out, 16 * SEQS * CHUNKS)

        PARAM_LOADS = 1 + 12 + 3 + 2 * NF
        CONST_LOADS = 3 + 4 * GROUP

        @block.gpsimd
        def _(pool):
            pool.memset(m_col[:], 0.0).then_inc(s_zero, 1)

            def split_pair(l, pair):
                loads = 16 * (PAIRS // 2 * l + pair // 2 + 1)
                split = PAIRS * l + pair + 1
                pool.wait_ge(s_raw[pair % 2], loads)
                hi, lo = w_hi[:, :, pair, :], w_lo[:, :, pair, :]
                raw = w_raw[:, pair % 2, :, :]
                pool.tensor_tensor(hi[:, 0:5:2, :], raw, zero.unsqueeze(2).to_broadcast([P, 3, P]), ALU.add
                                   ).then_inc(p_hi, 1)
                pool.wait_ge(p_hi, split)
                pool.tensor_tensor(lo[:, 0:5:2, :], raw, hi[:, 0:5:2, :].bitcast(F32), ALU.subtract).then_inc(p_lo, 1)
                pool.wait_ge(p_lo, split)
                last = None
                for part in (hi, lo):
                    for a in range(2):
                        view = part[:, 0:4, :].rearrange("p (t b) (h a d) -> p t b h a d", b=2, a=2, h=2)
                        last = pool.tensor_tensor(view[:, :, 1, :, a, :], view[:, :, 0, :, 1 - a, :].bitcast(F32),
                                                  zero.unsqueeze(2).unsqueeze(3).to_broadcast([P, 2, 2, DIM_HEAD // 2]), ALU.add)
                last.then_inc(s_w, 1)

            def add(n, i):
                pool.wait_ge(s_mul[i], n + 1)
                if not (isinstance(n, int) and n == 0):
                    pool.wait_ge(s_fin[i], n)
                pool.tensor_tensor(rotated[i][:], t_cos[i][:], t_sin[i][:], ALU.add).then_inc(s_rot[i], 1)

            def split_w1(l):
                pool.wait_ge(s_w1, 16 * (l + 1))
                pool.wait_ge(f_x, SEQS * l + 1)
                pool.tensor_tensor(w1_hi[:], w1_raw[:], zero.to_broadcast([P, 2 * FFN]), ALU.add).then_inc(p_w1, 1)
                pool.wait_ge(p_w1, l + 1)
                pool.tensor_tensor(w1_lo[:], w1_raw[:], w1_hi[:].bitcast(F32), ALU.subtract).then_inc(s_w1s, 1)

            def body(g, l_next=None, last=False):
                for p in range(PAIRS):
                    if not (last and p == PAIRS - 1):
                        add(PAIRS * g + p + 1, 0)
                        add(PAIRS * g + p + 1, 1)
                    if l_next is not None:
                        pool.wait_ge(s_p[1], PAIRS * g + p + 1)
                        pool.wait_ge(s_v, V_TILES * (g + 1))
                        split_pair(l_next, p)

            pool.wait_ge(s_const, 16 * CONST_LOADS)
            for pair in range(PAIRS):
                split_pair(0, pair)
            pool.wait_ge(a_o, UNITS * SEQS)
            add(0, 0)
            add(0, 1)

            def layer(l, last):
                body(SEQS * l)
                split_w1(l)
                with pool.Fori(1, SEQS - 1) as s:
                    body(SEQS * l + s)
                body(SEQS * l + SEQS - 1, None if last else l + 1, last)

            with pool.Fori(0, DEPTH - 1) as l:
                layer(l, False)
            layer(DEPTH - 1, True)

        @block.tensor
        def _(pe):
            def three(dst, lhs, rhs, stop=True):
                (lh, ll), (rh, rl) = lhs, rhs
                pe.matmul(dst, lh, rh, start=True, stop=False)
                pe.matmul(dst, lh, rl, start=False, stop=False)
                return pe.matmul(dst, ll, rh, start=False, stop=True)

            pe.wait_ge(s_const, 16 * CONST_LOADS)
            with pe.Fori(0, SEQS) as s:
                pe.wait_ge(a_xn, 2 * s + 1)
                for c in range(CHUNKS):
                    mm = pe.transpose(bank[0][:, c * P:(c + 1) * P], x_nrm[:, c, :], eye)
                mm.then_inc(a_xt, 1)
                pe.wait_ge(a_xte, s + 1)
                def project_group(i):
                    w = (wq_pad, wk_pad)[i % 2]
                    if i >= 2:
                        pe.wait_ge(a_hi, 2 * GROUP * s + i)
                    elif i == 0:
                        pe.wait_ge(a_m, 1)
                    pe.matmul(bank[2 if i == 1 else 1][:], w[:, (i // 2) * P:(i // 2 + 1) * P], xn_t[:],
                              start=True, stop=True).then_inc(a_proj, 1)

                project_group(0)
                project_group(1)
                for c in range(CHUNKS):
                    mm = pe.matmul(bank[0][:, c * P:(c + 1) * P], xn_t[:, c * P:(c + 1) * P],
                                   wkqv_sb[:, 2 * P:3 * P], start=True, stop=True)
                mm.then_inc(a_v, 1)

                def scores(u):
                    h, c = divmod(u, CHUNKS)
                    grp, r = divmod(h, GROUP)
                    n = (c + 1) * P
                    dst = bank[SCORE_BANKS[u % 3]]
                    if u % (GROUP * CHUNKS) == 0:
                        pe.wait_ge(a_qk, 2 * GROUP * s + 2 * grp + 2)
                    if u == 2:
                        pe.wait_ge(a_ve, s + 1)
                    if u >= 3:
                        pe.wait_ge(a_exp, UNITS * s + u - 2)
                    rows = slice(SLOT * r, SLOT * (r + 1))
                    pe.matmul(dst[:, 0:n], qa[rows, grp, c * P:(c + 1) * P], ka[grp][rows, 0:n],
                              start=True, stop=False)
                    pe.matmul(dst[:, n - P:n], eye16, causal_mask, start=False, stop=True).then_inc(a_s, 1)

                def turn(u):
                    h, c = divmod(u, CHUNKS)
                    pe.wait_ge(a_exp, UNITS * s + u + 1)
                    if u >= 3:
                        pe.wait_ge(a_pte, UNITS * s + u - 2)
                    for b in range(c + 1):
                        mm = pe.transpose(bank[TURN_BANKS[u % 3]][:, b * P:(b + 1) * P], p_glob[:, u % 3, b * P:(b + 1) * P],
                                          eye)
                    mm.then_inc(a_pt, 1)

                def attend(u):
                    h, c = divmod(u, CHUNKS)
                    pe.wait_ge(a_pte, UNITS * s + u + 1)
                    if u == 0:
                        pe.wait_ge(a_ve, s + 1)
                    at = c * P + h * GLOBAL_DIM
                    for b in range(c + 1):
                        mm = pe.matmul(bank[7][:, at:at + GLOBAL_DIM], pt_glob[:, u % 3, b * P:(b + 1) * P],
                                       va[:, b, h * GLOBAL_DIM:(h + 1) * GLOBAL_DIM], start=(b == 0), stop=(b == c),
                                       skip_group_check=True)
                    mm.then_inc(a_o, 1)

                for u in range(UNITS + 3):
                    if u in PROJECT_AT:
                        project_group(PROJECT_AT[u])
                    if u < UNITS:
                        scores(u)
                    if 2 <= u < UNITS + 2:
                        turn(u - 2)
                    if u >= 3:
                        attend(u - 3)
                pe.wait_ge(a_xn, 2 * s + 2)
                for c in range(CHUNKS):
                    mm = pe.transpose(bank[0][:, c * P:(c + 1) * P], x_nrm[:, c, :], eye)
                mm.then_inc(a_yt, 1)

            def project(n, g, p, i):
                if i == 0:
                    pe.wait_ge(s_w, PAIRS * (g // SEQS) + p + 1)
                    if p == 0:
                        pe.wait_ge(s_xs, g + 1)
                    if not (isinstance(n, int) and n == 0):
                        pe.wait_ge(s_mul[1], n)
                else:
                    pe.wait_ge(s_mul[0], n + 1)
                for b in range(2):
                    mm = three(bank[b][:], (w_hi[:, 2 * i + b, p, :], w_lo[:, 2 * i + b, p, :]), (xs_hi, xs_lo))
                mm.then_inc(s_p[i], 1)

            def norm2(n, i, g=None):
                pe.wait_ge(s_sq[i], n + 1)
                if i == 0 and g is not None:
                    pe.wait_ge(s_ve[0], V_TILES // 2 * (g + 1))
                if i == 1:
                    pe.wait_ge(s_ln[0], n + 1)
                pe.matmul(bank[6][:], pair_ones, sq[i][:], start=True, stop=True).then_inc(s_n2[i], 1)

            def value_tiles(g, n):
                pe.wait_ge(s_w, PAIRS * (g // SEQS + 1))
                for t in range(V_TILES):
                    c, half = divmod(t, 2)
                    if t == 0:
                        pe.wait_ge(s_ln[1], n + 1)
                    elif t == 1:
                        if not (isinstance(g, int) and g == 0):
                            pe.wait_ge(f_x, g)
                    else:
                        pe.wait_ge(s_ve[t % 2], V_TILES // 2 * g + t // 2)
                    lhs = (xs_hi[:, c * P:(c + 1) * P], xs_lo[:, c * P:(c + 1) * P])
                    w = slice(half * PAIRS // 2, (half + 1) * PAIRS // 2)
                    three(bank[6 + t % 2][:], lhs, (w_hi[:, V_W, w, :], w_lo[:, V_W, w, :])).then_inc(s_v, 1)

            def max_scores(n, p, h):
                if h == 0:
                    pe.wait_ge(s_16[0], n + 1)
                    pe.wait_ge(s_16[1], n + 1)
                if not (isinstance(n, int) and n == 0):
                    pe.wait_ge(s_nrm, 2 * n - 1 + h)
                rows = slice(DIM_HEAD * h, DIM_HEAD * (h + 1))
                for b in range(2):
                    dst = bank[2 + 2 * h + b]
                    pe.matmul(dst[:, 0:2 * KEYS], eye16, local_mask[:, b * KEYS:(b + 2) * KEYS], start=True, stop=False)
                    for c in range(2 * b, 2 * b + 2):
                        mm = pe.matmul(dst[:, (c % 2) * KEYS:(c % 2 + 1) * KEYS], q16[rows, p % 2, c * P:(c + 1) * P],
                                       k16[rows, p % 2, c * P:c * P + KEYS], start=False, stop=(c % 2 == 1))
                    mm.then_inc(s_s, 1)

            def turn_max(n, h):
                pe.wait_ge(s_mx, 4 * n + 2 * h + 2)
                if h == 1:
                    pe.wait_ge(s_e, 4 * n + 2)
                for c in range(CHUNKS):
                    mm = pe.matmul(bank[5 - 2 * h][0:1, c * P:(c + 1) * P], neg_max[:, h, c:c + 1], eye16,
                                   start=True, stop=True, skip_group_check=True)
                mm.then_inc(s_tm, 1)

            def turned_scores(n, p, h):
                rows = slice(DIM_HEAD * h, DIM_HEAD * (h + 1))
                spans = [(bank[2 + 2 * h + c // 2], c, (c % 2) * KEYS, min(KEYS, TOK - c * P)) for c in range(CHUNKS)]
                for b in range(2):
                    width = min(2 * KEYS, CHUNKS * KEYS - WINDOW - 2 * b * KEYS)
                    pe.matmul(bank[2 + 2 * h + b][:, 0:width], eye16, local_mask_t[:, 0:width], start=True, stop=False)
                    for dst, c, at, q in spans[2 * b:2 * b + 2]:
                        pe.matmul(dst[:, at:at + q], k_fin[rows, p % 2, c * P:(c + 1) * P],
                                  q_fin[rows, p % 2, c * P:c * P + q], start=False, stop=False)
                pe.wait_ge(s_nm, 2 * n + h + 1)
                for b in range(2):
                    for dst, c, at, q in spans[2 * b:2 * b + 2]:
                        mm = pe.matmul(dst[:, at:at + q], ones16[:], neg_row[:, h, c * P:c * P + q],
                                       start=False, stop=(c % 2 == 1))
                    mm.then_inc(s_st, 1)

            def attend_local(n, g, p, h):
                if h == 0 and p == 0:
                    pe.wait_ge(s_ve[0], V_TILES // 2 * (g + 1))
                    pe.wait_ge(s_ve[1], V_TILES // 2 * (g + 1))
                pe.wait_ge(s_e, 4 * n + 2 * h + 2)
                dst = bank[2 + 2 * h]
                for c in range(CHUNKS):
                    q = min(KEYS, TOK - c * P)
                    mm = pe.matmul(dst[:, c * P:c * P + q], v_sb[:, c, p, h * DIM_HEAD:h * DIM_HEAD + P],
                                   probs_t[:, h, c * KEYS:c * KEYS + q], start=(c == 0), stop=(c == CHUNKS - 1),
                                   skip_group_check=True)
                mm.then_inc(s_o, 1)

            def ffn_parts(f, after_values):
                l = f // SEQS

                def out_proj():
                    pe.wait_ge(s_nrm, 2 * PAIRS * (f + 1))
                    pe.wait_ge(s_wo, 16 * (l + 1))
                    if after_values:
                        pe.wait_ge(s_ve[1], V_TILES // 2 * (f + 2))
                    else:
                        pe.wait_ge(f_x, f + 1)
                    for a in range(PAIRS):
                        mm = pe.matmul(bank[7][:], wo_sb[:, a, :], o_feat[:, a, :], start=(a == 0),
                                       stop=(a == PAIRS - 1))
                    mm.then_inc(f_wo, 1)

                def mean():
                    pe.wait_ge(f_sh, f + 1)
                    pe.matmul(bank[7][:], mean_w, x_sh[:], start=True, stop=True).then_inc(f_mean, 1)

                def var():
                    pe.wait_ge(f_sq, f + 1)
                    pe.matmul(bank[7][:], mean_w, sq_f[:], start=True, stop=True).then_inc(f_var, 1)

                def up(i):
                    def run():
                        at, n = FFN_TILES[i % NF]
                        off = at + (FFN if i < NF else 0)
                        if i == 0:
                            pe.wait_ge(f_ylo, f + 1)
                            pe.wait_ge(s_w1s, l + 1)
                        else:
                            pe.wait_ge(f_he, 2 * NF * f + i)
                        three(bank[7][0:n, :], (w1_hi[:, off:off + n], w1_lo[:, off:off + n]), (y_hi, y_lo)
                              ).then_inc(f_h, 1)
                    return run

                def down():
                    pe.wait_ge(f_prod, f + 1)
                    pe.wait_ge(s_w2, 32 * (l + 1))
                    for j, (_, n) in enumerate(FFN_TILES):
                        mm = pe.matmul(bank[7][:], w2_sb[0:n, j, :], gates[0:n, j, :], start=(j == 0),
                                       stop=(j == NF - 1))
                    mm.then_inc(f_w2, 1)

                return {(0, 0): out_proj, (1, 0): mean, (1, 1): var, (2, 1): up(0), (3, 0): up(1), (3, 1): up(2),
                        (4, 0): up(3), (4, 1): up(4), (5, 0): up(5), (6, 0): down}

            def body(g, first=False, last=False):
                parts = {} if first else ffn_parts(g - 1, True)
                for p in range(PAIRS):
                    n = PAIRS * g + p
                    nxt = not (last and p == PAIRS - 1)
                    gn, pn = (g, p + 1) if p + 1 < PAIRS else (g + 1, 0)
                    if nxt:
                        project(n + 1, gn, pn, 0)
                    max_scores(n, p, 0)
                    if not (first and p == 0):
                        attend_local(n - 1, g, (p - 1) % PAIRS, 1)
                    if nxt:
                        project(n + 1, gn, pn, 1)
                    turn_max(n, 0)
                    turned_scores(n, p, 0)
                    if p == 0:
                        value_tiles(g, n)
                    max_scores(n, p, 1)
                    if (p, 0) in parts:
                        parts[(p, 0)]()
                    if nxt:
                        norm2(n + 1, 0, g if p == 0 else None)
                    turn_max(n, 1)
                    attend_local(n, g, p, 0)
                    if nxt:
                        norm2(n + 1, 1)
                    turned_scores(n, p, 1)
                    if (p, 1) in parts:
                        parts[(p, 1)]()

            project(0, 0, 0, 0)
            project(0, 0, 0, 1)
            norm2(0, 0)
            norm2(0, 1)
            body(0, first=True)
            with pe.Fori(1, BODIES - 1) as g:
                body(g)
            body(BODIES - 1, last=True)
            attend_local(PAIRS * BODIES - 1, BODIES - 1, PAIRS - 1, 1)
            tail = ffn_parts(BODIES - 1, False)
            for key in sorted(tail):
                tail[key]()
            pe.wait_ge(f_x, BODIES + 1)
            for i in range(SEQS * CHUNKS // 4):
                if i >= 2:
                    pe.wait_ge(o_e, 4 * (i - 1))
                for c in range(4):
                    mm = pe.transpose(bank[i % 2][:, c * P:(c + 1) * P], state[:, (4 * i + c) * P:(4 * i + c + 1) * P],
                                      eye)
                mm.then_inc(o_t, 1)

        @block.scalar
        def _(act):
            def rstd_of(s, k):
                act.wait_ge(a_mv, 2 * s + k + 1)
                act.activation(rstd, mean_var[:, :, 1], ACT.Ln, bias=const(C_EPS)).then_inc(a_ln, 1)
                act.wait_ge(a_ln, 2 * s + k + 1)
                act.activation(rstd, rstd, ACT.Exp, scale=-0.5).then_inc(a_rstd, 1)

            act.preload_act_table_set(LN_EXP)
            act.wait_ge(s_const, 16 * CONST_LOADS)
            with act.Fori(0, SEQS) as s:
                rstd_of(s, 0)
                act.wait_ge(a_xt, s + 1)
                act.activation(xn_t[:], bank[0][:], ACT.Copy).then_inc(a_xte, 1)

                def scale_group(i):
                    j = 2 * GROUP * s + i
                    act.wait_ge(a_proj, j + 1)
                    if i > 0:
                        act.wait_ge(a_qk, j)
                    src = bank[2 if i == 1 else 1]
                    scale = (float(D) ** -0.5, 1.0)[i % 2]
                    act.activation(scaled[:], src[:], ACT.Copy, scale=scale)
                    act.activation(part_hi[:].bitcast(F32R), src[:], ACT.Copy, scale=scale).then_inc(a_hi, 1)

                scale_group(0)
                scale_group(1)
                act.wait_ge(a_v, s + 1)
                act.activation(va, bank[0][:].rearrange("p (c d) -> p c d", c=CHUNKS), ACT.Copy).then_inc(a_ve, 1)
                for u in range(UNITS):
                    h, c = divmod(u, CHUNKS)
                    n = (c + 1) * P
                    if u in PROJECT_AT:
                        scale_group(PROJECT_AT[u])
                    act.wait_ge(a_max, UNITS * s + u + 1)
                    if u >= 3:
                        act.wait_ge(a_pt, UNITS * s + u - 2)
                    act.activation(p_glob[:, u % 3, 0:n], bank[SCORE_BANKS[u % 3]][:, 0:n], ACT.Exp,
                                   bias=g_max[:, u:u + 1], accum_out=g_sum[:, c, h:h + 1]).then_inc(a_exp, 1)
                rstd_of(s, 1)
                act.wait_ge(a_yt, s + 1)
                act.activation(state[:, bass.ds(s * TOK, TOK)], bank[0][:], ACT.Copy).then_inc(a_state, 1)

            def square(n, i):
                act.wait_ge(s_p[i], n + 1)
                if not (isinstance(n, int) and n == 0):
                    act.wait_ge(s_n2[i], n)
                act.activation(sq[i][:], bank[0][:], ACT.Square).then_inc(s_sq[i], 1)

            def rnorm(n, i):
                act.wait_ge(s_n2[i], n + 1)
                if not (isinstance(n, int) and n == 0):
                    act.wait_ge(s_fin[i], n)
                act.activation(r_norm[i][:], bank[6][:], ACT.Ln, bias=const(C_TINY),
                               scale=float(2 ** NORM_SHIFT)).then_inc(s_ln[i], 1)
                act.wait_ge(s_ln[i], n + 1)
                act.activation(r_norm[i][:], r_norm[i][:], ACT.Exp, bias=const(C_SHIFT), scale=-0.5).then_inc(s_r[i], 1)

            def max_row(n, h):
                act.wait_ge(s_tm, 2 * n + h + 1)
                act.activation(neg_row[:, h, :], bank[5 - 2 * h][0:1, :], ACT.Copy).then_inc(s_nm, 1)

            def exps(n, h):
                for b in range(2):
                    width = min(2 * KEYS, CHUNKS * KEYS - WINDOW - 2 * b * KEYS)
                    act.wait_ge(s_st, 4 * n + 2 * h + b + 1)
                    if b == 0 and not (isinstance(n, int) and n == 0):
                        act.wait_ge(s_o, 2 * n - 1 + h)
                    act.activation(probs_t[:, h, 2 * b * KEYS:2 * b * KEYS + width], bank[2 + 2 * h + b][:, 0:width],
                                   ACT.Exp).then_inc(s_e, 1)

            def invert_sums(n, h):
                act.wait_ge(s_o, 2 * n + h + 1)
                if not (isinstance(n, int) and n == 0):
                    act.wait_ge(s_nrm, 2 * n - 1 + h)
                own = slice(DIM_HEAD * h, DIM_HEAD * (h + 1))
                other = slice(DIM_HEAD * (1 - h), DIM_HEAD * (2 - h))
                act.activation(inv_sums[own, :], bank[2 + 2 * h][other, :], ACT.Ln).then_inc(s_lns, 1)
                act.wait_ge(s_lns, 2 * n + h + 1)
                act.activation(inv_sums[own, :], inv_sums[own, :], ACT.Exp, scale=-1.0).then_inc(s_sum, 1)

            def ffn_parts(f):
                def square_f():
                    act.wait_ge(f_cen, f + 1)
                    act.activation(sq_f[:], x_cen[:], ACT.Square).then_inc(f_sq, 1)

                def rstd_f_():
                    act.wait_ge(f_var, f + 1)
                    act.activation(rstd_f[:], bank[7][:], ACT.Ln, bias=const(C_EPS)).then_inc(f_ln, 1)
                    act.wait_ge(f_ln, f + 1)
                    act.activation(rstd_f[:], rstd_f[:], ACT.Exp, scale=-0.5).then_inc(f_rstd, 1)

                def gelu():
                    act.preload_act_table(ACT.Gelu)
                    act.wait_ge(f_he, 2 * NF * f + NF)
                    act.activation(gates[:, 0:NF - 1, :], gates[:, 0:NF - 1, :], ACT.Gelu)

                def gelu_rest():
                    n = FFN_TILES[-1][1]
                    act.activation(gates[0:n, NF - 1, :], gates[0:n, NF - 1, :], ACT.Gelu).then_inc(f_gelu, 1)
                    act.preload_act_table_set(LN_EXP)

                return {(1, 0): square_f, (1, 1): rstd_f_, (4, 1): gelu, (5, -1): gelu_rest}

            def body(g, first=False, last=False):
                parts = {} if first else ffn_parts(g - 1)
                for p in range(PAIRS):
                    n = PAIRS * g + p
                    nxt = not (last and p == PAIRS - 1)
                    if nxt:
                        square(n + 1, 0)
                    if (p, -1) in parts:
                        parts[(p, -1)]()
                    if not (first and p == 0):
                        invert_sums(n - 1, 1)
                    if nxt:
                        square(n + 1, 1)
                    max_row(n, 0)
                    exps(n, 0)
                    if p == 0:
                        if not first:
                            act.wait_ge(s_o, 2 * PAIRS * g)
                        for t in range(0, V_TILES, 2):
                            act.wait_ge(s_v, V_TILES * g + t + 1)
                            act.activation(value_place(t), value_source(t), ACT.Copy).then_inc(s_ve[0], 1)
                    if (p, 0) in parts:
                        parts[(p, 0)]()
                    if nxt:
                        rnorm(n + 1, 0)
                    max_row(n, 1)
                    invert_sums(n, 0)
                    if nxt:
                        rnorm(n + 1, 1)
                    exps(n, 1)
                    if (p, 1) in parts:
                        parts[(p, 1)]()

            square(0, 0)
            square(0, 1)
            rnorm(0, 0)
            rnorm(0, 1)
            body(0, first=True)
            with act.Fori(1, BODIES - 1) as g:
                body(g)
            body(BODIES - 1, last=True)
            invert_sums(PAIRS * BODIES - 1, 1)
            tail = ffn_parts(BODIES - 1)
            for key in sorted(tail):
                tail[key]()

        @block.vector
        def _(dve):
            dve.memset(wq_pad[:], 0.0).then_inc(v0, 1)
            dve.memset(wk_pad[:], 0.0).then_inc(v0, 1)
            dve.memset(k16[:, :, 0:WINDOW], 0.0).then_inc(v0, 1)
            dve.memset(ones16[:], 1.0).then_inc(v0, 1)
            dve.wait_ge(s_const, 16 * CONST_LOADS)
            dve.wait_ge(v0, 4)
            dve.tensor_copy(mask_sb[:], mask_raw).then_inc(v0, 1)
            n = GLOBAL_DIM
            for w, at in ((wq_pad, P), (wk_pad, 0)):
                for k in range(3):
                    dst = w.rearrange("p (h r) -> p h r", r=SLOT)[:, :, k * n:(k + 1) * n]
                    dve.tensor_copy(dst, wkqv_sb[:, at:at + P].rearrange("p (h r) -> p h r", r=n)).then_inc(v0, 1)
            dve.tensor_copy(m_round[:], m_col[:]).then_inc(v0, 1)
            dve.wait_ge(v0, 12)
            dve.tensor_tensor(m_lo, m_col[:], m_round[:].bitcast(F32), ALU.subtract).then_inc(v0, 1)
            dve.wait_ge(v0, 13)
            k = 13
            for i, (hi_row, lo_row) in enumerate(((M_HI_Q, M_LO_Q), (M_HI_K, M_LO_K))):
                dve.tensor_scalar(m_cols[:, 4 * i:4 * i + 4], m_lo, const(lo_row), None, ALU.mult).then_inc(v0, 1)
                k += 1
                dve.wait_ge(v0, k)
                dve.scalar_tensor_tensor(out=m_cols[:, 4 * i:4 * i + 4], in0=m_round[:].bitcast(F32),
                                         scalar=const(hi_row), in1=m_cols[:, 4 * i:4 * i + 4],
                                         op0=ALU.mult, op1=ALU.add).then_inc(v0, 1)
                k += 1
                dve.wait_ge(v0, k)
            for i, (dst, pos) in enumerate(((add_q, q_pos), (add_k, k_pos))):
                for grp in range(GROUP):
                    one = dve.tensor_scalar(dst[:, grp, :], pos, m_cols[:, 4 * i + grp:4 * i + grp + 1], None, ALU.add)
            one.then_inc(a_m, 1)
            dve.wait_ge(a_m, 1)
            dve.wait_ge(s_x, 16)

            def normalise(s, k, after_sum=False):
                if after_sum:
                    dve.wait_ge(a_x1, s + 1)
                    dve.memset(scratch[:, 0:1], 0.0)
                for c in range(CHUNKS):
                    one = dve.bn_stats(stats[:, c, :], x_tok[:, bass.ds(s * CHUNKS + c, 1), :].rearrange("p a d -> p (a d)"))
                one.then_inc(a_stat, 1)
                dve.wait_ge(a_stat, 2 * s + k + 1)
                dve.memset(scratch[:, 1:2], 0.0)
                for c in range(CHUNKS):
                    one = dve.bn_aggr(mean_var[:, c, :], stats[:, c, :])
                one.then_inc(a_mv, 1)
                dve.wait_ge(a_rstd, 2 * s + k + 1)
                for c in range(CHUNKS):
                    one = dve.tensor_scalar(x_nrm[:, c, :], x_tok[:, bass.ds(s * CHUNKS + c, 1), :].rearrange("p a d -> p (a d)"),
                                            mean_var[:, c, 0:1], rstd[:, c:c + 1], ALU.subtract, ALU.mult)
                one.then_inc(a_xn, 1)

            with dve.Fori(0, SEQS) as s:
                normalise(s, 0)

                def split_group(i):
                    grp, k = divmod(i, 2)
                    j = 2 * GROUP * s + i
                    dve.wait_ge(a_hi, j + 1)
                    dve.scalar_tensor_tensor(out=part_hi[:], in0=part_hi[:], scalar=const((SIGN_Q, SIGN_K)[k]),
                                             in1=(add_q, add_k)[k][:, grp, :], op0=ALU.mult, op1=ALU.add
                                             ).then_inc(a_mix, 1)
                    dve.wait_ge(a_mix, j + 1)
                    dve.scalar_tensor_tensor(out=qa[:, grp, :] if k == 0 else ka[grp], in0=scaled[:],
                                             scalar=const((LOW_Q, LOW_K)[k]), in1=part_hi[:],
                                             op0=ALU.mult, op1=ALU.add).then_inc(a_qk, 1)

                split_group(0)
                split_group(1)

                def turned(u):
                    h, c = divmod(u, CHUNKS)
                    m_ = (c + 1) * P
                    dve.wait_ge(a_pt, UNITS * s + u + 1)
                    if u >= 3:
                        dve.wait_ge(a_o, UNITS * s + u - 2)
                    dve.tensor_copy(pt_glob[:, u % 3, 0:m_], bank[TURN_BANKS[u % 3]][:, 0:m_]).then_inc(a_pte, 1)

                for u in range(UNITS + 2):
                    if u < UNITS:
                        m_ = (u % CHUNKS + 1) * P
                        dve.wait_ge(a_s, UNITS * s + u + 1)
                        dve.tensor_reduce(g_max[:, u:u + 1], bank[SCORE_BANKS[u % 3]][:, 0:m_], AX_X, ALU.max,
                                          negate=True).then_inc(a_max, 1)
                    if u in PROJECT_AT:
                        split_group(PROJECT_AT[u])
                    if u >= 2:
                        turned(u - 2)
                dve.wait_ge(a_exp, UNITS * (s + 1))
                dve.reciprocal(g_inv[:], g_sum[:]).then_inc(a_inv, 1)
                dve.wait_ge(a_inv, s + 1)
                dve.wait_ge(a_o, UNITS * (s + 1))
                dve.tensor_tensor(o_glob.rearrange("p c (h d) -> p c h d", h=HEADS),
                                  bank[7][:].rearrange("p (c h d) -> p c h d", c=CHUNKS, h=HEADS),
                                  g_inv[:].unsqueeze(3).to_broadcast([P, CHUNKS, HEADS, GLOBAL_DIM]),
                                  ALU.mult).then_inc(a_oe, 1)
                dve.wait_ge(a_oe, s + 1)
                xs_ = x_tok[:, bass.ds(s * CHUNKS, CHUNKS), :]
                dve.tensor_tensor(xs_, xs_, o_glob, ALU.add).then_inc(a_x1, 1)
                normalise(s, 1, True)

            dve.memset(xs_hi[DIM_HEAD:P, 0:1].bitcast(F32), 0.0).then_inc(v0, 1)
            dve.memset(xs_lo[DIM_HEAD:P, 0:1].bitcast(F32), 0.0).then_inc(v0, 1)
            dve.memset(x_sh[DIM_HEAD:P, 0:1], 0.0).then_inc(v0, 1)
            dve.memset(v_sb[:, :, :, DIM_HEAD:2 * DIM_HEAD], 1.0).then_inc(v0, 1)
            dve.wait_ge(v0, 21)
            HALF = D // 2

            def shifted_input(g, ready=None):
                at = (g % SEQS) * TOK
                if not (isinstance(g, int) and g < 2):
                    dve.wait_ge(f_x, g - 1)
                if not (isinstance(g, int) and g == 0):
                    dve.wait_ge(s_xs, g)
                src = (state[0:HALF, bass.ds(at, TOK)], state[HALF:P, bass.ds(at, TOK - 1)])
                dve.tensor_copy(xs_hi[0:HALF, :], src[0])
                dve.tensor_copy(xs_hi[HALF:P, 1:TOK], src[1]).then_inc(s_xhi, 1)
                dve.wait_ge(s_xhi, 2 * g + 1)
                dve.tensor_tensor(xs_lo[0:HALF, :], src[0], xs_hi[0:HALF, :].bitcast(F32), ALU.subtract)
                dve.tensor_tensor(xs_lo[HALF:P, 1:TOK], src[1], xs_hi[HALF:P, 1:TOK].bitcast(F32), ALU.subtract
                                  ).then_inc(s_xhi, 1)
                dve.wait_ge(s_xhi, 2 * g + 2)
                dve.memset(scratch[:, 0:1], 0.0).then_inc(s_xs, 1)

            def times_tables(n, l, i):
                dve.wait_ge(s_p[i], n + 1)
                if not (isinstance(n, int) and n == 0):
                    dve.wait_ge(s_rot[i], n)
                dve.scalar_tensor_tensor(out=t_sin[i][:], in0=bank[1][:], scalar=scales[:, 2 * i + 1, bass.ds(l, 1)],
                                         in1=rot_sb[:, 2 * i + 1, :], op0=ALU.mult, op1=ALU.mult)
                dve.wait_ge(s_sq[i], n + 1)
                dve.scalar_tensor_tensor(out=t_cos[i][:], in0=bank[0][:], scalar=scales[:, 2 * i, bass.ds(l, 1)],
                                         in1=rot_sb[:, 2 * i, :], op0=ALU.mult, op1=ALU.mult).then_inc(s_mul[i], 1)

            def final(n, p, i):
                dve.wait_ge(s_r[i], n + 1)
                dve.wait_ge(s_rot[i], n + 1)
                if not (isinstance(n, int) and n < 2):
                    dve.wait_ge(s_st, 4 * n - 4)
                dst = (q_fin, k_fin)[i][:, p % 2, :]
                dve.scalar_tensor_tensor(out=dst, in0=r_norm[i][:], scalar=NORM_CAP, in1=rotated[i][:],
                                         op0=ALU.min, op1=ALU.mult).then_inc(s_fin[i], 1)
                dve.wait_ge(s_fin[i], n + 1)
                dve.tensor_copy(q16[:, p % 2, :] if i == 0 else k16[:, p % 2, WINDOW:], dst).then_inc(s_16[i], 1)

            def maxima(n, h):
                for b in range(2):
                    dve.wait_ge(s_s, 4 * n + 2 * h + b + 1)
                    if b == 0 and not (isinstance(n, int) and n == 0):
                        dve.wait_ge(s_tm, 2 * n - 1 + h)
                    dve.tensor_reduce(neg_max[:, h, 2 * b:2 * b + 2],
                                      bank[2 + 2 * h + b][:, 0:2 * KEYS].rearrange("p (c k) -> p c k", c=2),
                                      AX_X, ALU.max, negate=True).then_inc(s_mx, 1)

            def normalise_out(n, g, p, h):
                dve.wait_ge(s_sum, 2 * n + h + 1)
                if p == 0 and h == 0 and g is not None:
                    dve.wait_ge(f_wo, g)
                own = slice(DIM_HEAD * h, DIM_HEAD * (h + 1))
                dve.tensor_tensor(o_feat[own, p, :], bank[2 + 2 * h][own, :], inv_sums[own, :], ALU.mult
                                  ).then_inc(s_nrm, 1)

            def ffn_parts(f):
                l = f // SEQS
                at = (f % SEQS) * TOK

                def mid():
                    dve.wait_ge(f_wo, f + 1)
                    dve.wait_ge(f_x, f + 1)
                    dve.tensor_tensor(x_mid[:], bank[7][:], state[:, bass.ds(at, TOK)], ALU.add).then_inc(f_mid, 1)
                    dve.wait_ge(f_mid, f + 1)
                    dve.tensor_copy(x_sh[0:HALF, :], x_mid[0:HALF, :])
                    dve.tensor_copy(x_sh[HALF:P, 1:TOK], x_mid[HALF:P, 0:TOK - 1]).then_inc(f_sh, 1)

                def centre():
                    dve.wait_ge(f_mean, f + 1)
                    dve.tensor_tensor(x_cen[:], x_sh[:], bank[7][:], ALU.subtract).then_inc(f_cen, 1)

                def norm():
                    dve.wait_ge(f_rstd, f + 1)
                    shift = vecs[:, 1, bass.ds(l, 1)]
                    dve.scalar_tensor_tensor(out=y_f[:], in0=x_cen[:], scalar=vecs[:, 0, bass.ds(l, 1)],
                                             in1=rstd_f[:], op0=ALU.mult, op1=ALU.mult).then_inc(f_y, 1)
                    dve.wait_ge(f_y, f + 1)
                    dve.tensor_scalar(y_hi, y_f[:], shift, None, ALU.add).then_inc(f_yhi, 1)
                    dve.wait_ge(f_yhi, f + 1)
                    dve.scalar_tensor_tensor(out=y_lo, in0=y_f[:], scalar=shift, in1=y_hi.bitcast(F32),
                                             op0=ALU.add, op1=ALU.subtract).then_inc(f_ylo, 1)

                def up(i):
                    def run():
                        n = FFN_TILES[i % NF][1]
                        dve.wait_ge(f_h, 2 * NF * f + i + 1)
                        dst = (gates if i < NF else values)[0:n, i % NF, :]
                        dve.tensor_scalar(dst, bank[7][0:n, :], b1_sb[0:n, i, bass.ds(l, 1)], None, ALU.add
                                          ).then_inc(f_he, 1)
                    return run

                def product():
                    n = FFN_TILES[-1][1]
                    dve.wait_ge(f_gelu, f + 1)
                    dve.wait_ge(f_he, 2 * NF * (f + 1))
                    dve.tensor_tensor(gates[:, 0:NF - 1, :], gates[:, 0:NF - 1, :], values[:, 0:NF - 1, :], ALU.mult)
                    dve.tensor_tensor(gates[0:n, NF - 1, :], gates[0:n, NF - 1, :], values[0:n, NF - 1, :], ALU.mult
                                      ).then_inc(f_prod, 1)

                def residual():
                    dve.wait_ge(f_w2, f + 1)
                    dve.scalar_tensor_tensor(out=state[:, bass.ds(at, TOK)], in0=bank[7][:],
                                             scalar=vecs[:, 2, bass.ds(l, 1)], in1=x_mid[:],
                                             op0=ALU.add, op1=ALU.add).then_inc(f_x, 1)

                return {(0, 0): mid, (1, 0): centre, (2, 0): norm, (2, 1): up(0), (3, 0): up(1), (3, 1): up(2),
                        (4, 0): up(3), (4, 1): up(4), (5, 0): up(5), (5, 1): product, (6, 0): residual}

            def body(g, first=False, last=False):
                parts = {} if first else ffn_parts(g - 1)
                for p in range(PAIRS):
                    n = PAIRS * g + p
                    nxt = not (last and p == PAIRS - 1)
                    l = (g if p + 1 < PAIRS else g + 1) // SEQS
                    if nxt:
                        times_tables(n + 1, l, 0)
                    maxima(n, 0)
                    if not (first and p == 0):
                        normalise_out(n - 1, g, (p - 1) % PAIRS, 1)
                    if nxt:
                        times_tables(n + 1, l, 1)
                    if p == 0:
                        if not first:
                            dve.wait_ge(s_o, 2 * PAIRS * g)
                        for t in range(1, V_TILES, 2):
                            dve.wait_ge(s_v, V_TILES * g + t + 1)
                            dve.tensor_copy(value_place(t), value_source(t)).then_inc(s_ve[1], 1)
                    if p == PAIRS - 2 and not last:
                        dve.wait_ge(s_p[1], PAIRS * (g + 1))
                        dve.wait_ge(s_v, V_TILES * (g + 1))
                        shifted_input(g + 1)
                    maxima(n, 1)
                    if (p, 0) in parts:
                        parts[(p, 0)]()
                    if nxt:
                        final(n + 1, p + 1, 0)
                    normalise_out(n, None if first else g, p, 0)
                    if nxt:
                        final(n + 1, p + 1, 1)
                    if (p, 1) in parts:
                        parts[(p, 1)]()

            dve.wait_ge(s_par, 16 * PARAM_LOADS)
            dve.wait_ge(a_state, SEQS)
            dve.memset(scratch[:, 0:1], 0.0).then_inc(f_x, 1)
            shifted_input(0)
            times_tables(0, 0, 0)
            times_tables(0, 0, 1)
            final(0, 0, 0)
            final(0, 0, 1)
            body(0, first=True)
            with dve.Fori(1, BODIES - 1) as g:
                body(g)
            body(BODIES - 1, last=True)
            normalise_out(PAIRS * BODIES - 1, None, PAIRS - 1, 1)
            tail = ffn_parts(BODIES - 1)
            for key in sorted(tail):
                tail[key]()
            for i in range(SEQS * CHUNKS):
                dve.wait_ge(o_t, i // 4 + 1)
                dve.tensor_tensor(x_tok[:, i, :], x_tok[:, i, :], bank[(i // 4) % 2][:, (i % 4) * P:(i % 4 + 1) * P],
                                  ALU.add).then_inc(o_e, 1)


_INS = ['L0_attn_x', 'L0_attn_W_kqv', 'L0_attn_m', 'L0_ffn_Wqkv', 'L0_ffn_q_scale', 'L0_ffn_k_scale', 'L0_ffn_Wo',
        'L0_ffn_ln_g', 'L0_ffn_ln_b', 'L0_ffn_W1', 'L0_ffn_b1', 'L0_ffn_W2', 'L0_ffn_b2']


def kernel(**inputs):
    import concourse.bacc as bacc
    from concourse.bass_utils import run_bass_kernel_spmd

    nc = bacc.Bacc("TRN2", target_bir_lowering=False, num_devices=1)
    arrays, args = {}, []
    masks, wide = shape_constants()
    host = [(name, np.ascontiguousarray(inputs[name])) for name in _INS]
    host += [("rotary", rotary_constants()), ("masks", masks), ("wide", wide)]
    for name, a in host:
        arrays[f"in_{name}"] = a
        args.append(nc.dram_tensor(f"in_{name}", a.shape, mybir.dt.from_np(a.dtype), kind="ExternalInput").ap())
    out = nc.dram_tensor("out_0", (SEQS, TOK, D), F32, kind="ExternalOutput").ap()
    build_program(nc, *args, out)
    r = run_bass_kernel_spmd(nc, [arrays], core_ids=[0])
    return r.results[0]["out_0"]
```

```python
from contextlib import ExitStack

import numpy as np

import concourse.bass as bass
from concourse import mybir

F32 = mybir.dt.float32
F32R = mybir.dt.float32r
BF16 = mybir.dt.bfloat16
ALU = mybir.AluOpType
ACT = mybir.ActivationFunctionType
AX_X = mybir.AxisListType.X

P = 128
SEQS, TOK, D = 4, 512, 128
CHUNKS = TOK // P
HEADS = 16
GLOBAL_DIM = D // HEADS
GROUP = 4
SLOT = P // GROUP
DEPTH = 6
DIM_HEAD = 64
INNER = HEADS * DIM_HEAD
PAIRS = INNER // P
WINDOW = 32
QK_SCALE = 8.0
KEYS = WINDOW + P
FFN = int(D * 4 * 2 / 3)
FFN_TILES = [(j * P, min(P, FFN - j * P)) for j in range(-(-FFN // P))]
NF = len(FFN_TILES)
BODIES = DEPTH * SEQS
LN_EPS = 1e-5
MASKED = -1e30
NORM_SHIFT = 20
NORM_CAP = 1e12
LN_EXP = "natural_log_exp_and_others"
V_TILES = 2 * CHUNKS
SPAN = 3 * DIM_HEAD
V_W = 2


def rotary_constants():
    half = np.arange(0, DIM_HEAD, 2, dtype=np.float32)
    inv_freq = (1.0 / np.float32(10000.0) ** (half / DIM_HEAD)).astype(np.float32)
    t = np.arange(TOK, dtype=np.float32)
    freqs = t[:, None] * inv_freq[None, :]
    freqs = np.concatenate([freqs, freqs], -1)
    base = ((half + np.float32(0.4 * DIM_HEAD)) / np.float32(1.4 * DIM_HEAD)).astype(np.float32)
    power = ((t - TOK // 2) / np.float32(WINDOW // 2)).astype(np.float32)
    scale = base[None, :] ** power[:, None]
    scale = np.concatenate([scale, scale], -1).astype(np.float32)
    sign = np.where(np.arange(DIM_HEAD) < DIM_HEAD // 2, -1.0, 1.0).astype(np.float32)
    inv = np.float32(1.0) / scale
    tables = [np.cos(freqs) * scale * np.float32(QK_SCALE), np.sin(freqs) * sign * scale * np.float32(QK_SCALE),
              np.cos(freqs) * inv, np.sin(freqs) * sign * inv]
    tables[1::2] = [np.roll(x, DIM_HEAD // 2, axis=1) for x in tables[1::2]]
    tables = [x.reshape(TOK, 2, DIM_HEAD // 2).transpose(0, 2, 1).reshape(TOK, DIM_HEAD) for x in tables]
    return np.stack([np.concatenate([x.T, x.T], 0) for x in tables], 1).astype(np.float32)


def shape_constants():
    i = np.arange(P)[:, None]
    j = np.arange(KEYS)[None, :] - WINDOW
    seen = (j <= i) & (j >= i - WINDOW)
    local = np.stack([np.where(seen & (j >= 0), 0.0, MASKED), np.where(seen, 0.0, MASKED),
                      np.where(seen, 0.0, MASKED)], 1)
    key, query = np.arange(P)[:, None], np.arange(KEYS)[None, :]
    turned = np.where((query >= key) & (query <= key + WINDOW), 0.0, MASKED)
    causal = np.where(np.arange(P)[None, :] <= i, 0.0, MASKED)
    masks = np.concatenate([local.reshape(P, -1), turned, turned, causal, np.eye(P)], 1).astype(np.float32)
    eye = np.eye(P, dtype=np.float32)
    mean = np.full((P, P), 1.0 / D, np.float32)
    pair = (np.arange(P)[:, None] // DIM_HEAD == np.arange(P)[None, :] // DIM_HEAD).astype(np.float32)
    squares = np.concatenate([eye, mean, pair], 1)
    row = np.arange(P) % SLOT
    n = GLOBAL_DIM
    pos = np.arange(TOK, dtype=np.float32)[None, :]
    low_q = ((row >= n) & (row < 2 * n)).astype(np.float32)
    low_k = ((row >= 2 * n) & (row < 3 * n)).astype(np.float32)
    real = (row < 3 * n).astype(np.float32)
    q_pos = ((row == 3 * n + 2) | (row == 3 * n + 3))[:, None] * pos
    k_pos = ((row == 3 * n) | (row == 3 * n + 1))[:, None] * pos
    q_m_hi, q_m_lo = (row == 3 * n), (row == 3 * n + 1)
    k_m_hi, k_m_lo = (row == 3 * n + 2), (row == 3 * n + 3)
    cols = np.stack([low_q, low_k, real - 2 * low_q, real - 2 * low_k, q_m_hi, q_m_lo,
                     -1.0 * k_m_hi, -1.0 * k_m_lo,
                     np.full(P, LN_EPS), np.full(P, 2.0 ** -64), np.full(P, 0.5 * NORM_SHIFT * np.log(2.0)),
                     np.zeros(P)], 1).astype(np.float32)
    wide = np.concatenate([squares, q_pos, k_pos, cols], 1).astype(np.float32)
    return masks, np.ascontiguousarray(wide)


LOW_Q, LOW_K, SIGN_Q, SIGN_K, M_HI_Q, M_LO_Q, M_HI_K, M_LO_K, C_EPS, C_TINY, C_SHIFT, C_ZERO = range(12)


def build_program(nc, x, w_kqv, m, w_qkv, q_scale, k_scale, w_o, ln_g, ln_b, w_1, b_1, w_2, b_2,
                  rotary, masks, wide, out):
    with ExitStack() as ctx:
        def sb(name, shape, dt=F32):
            return ctx.enter_context(nc.sbuf_tensor(name, shape, dt))

        def sem(name):
            return ctx.enter_context(nc.semaphore(name))

        bank = [ctx.enter_context(nc.psum_tensor(f"bank{i}", [P, 512], F32)) for i in range(8)]

        mask_sb = sb("mask_sb", [P, 5 * KEYS + 2 * P], BF16)
        local_mask = mask_sb[:, 0:3 * KEYS]
        local_mask_t = mask_sb[:, 3 * KEYS:5 * KEYS]
        causal_mask = mask_sb[:, 5 * KEYS:5 * KEYS + P]
        eye16 = mask_sb[:, 5 * KEYS + P:5 * KEYS + 2 * P]
        ones16 = sb("ones16", [1, P], BF16)
        wide_sb = sb("wide_sb", [P, 3 * P + 2 * TOK + 12])
        eye, mean_w, pair_ones = (wide_sb[:, i * P:(i + 1) * P] for i in range(3))
        q_pos = wide_sb[:, 3 * P:3 * P + TOK]
        k_pos = wide_sb[:, 3 * P + TOK:3 * P + 2 * TOK]

        def const(i, rows=P):
            return wide_sb[0:rows, 3 * P + 2 * TOK + i:3 * P + 2 * TOK + i + 1]

        zero = const(C_ZERO)
        scratch = sb("scratch", [P, 2])

        rot_sb = sb("rot_sb", [P, 4, TOK])
        scales = sb("scales", [P, 2, DEPTH])
        vecs = sb("vecs", [P, 3, DEPTH])
        b1_sb = sb("b1_sb", [P, 2 * NF, DEPTH])
        m_col = sb("m_col", [P, GROUP])

        x_tok = sb("x_tok", [P, SEQS * CHUNKS, D])
        state = sb("state", [P, SEQS * TOK])

        w_hi = sb("w_hi", [P, 3, PAIRS, P], F32R)
        w_lo = sb("w_lo", [P, 3, PAIRS, P], F32R)
        w_raw = sb("w_raw", [P, 2, 3, P])
        wo_sb = sb("wo_sb", [P, PAIRS, D])
        w1_raw = sb("w1_raw", [P, 2 * FFN])
        w1_hi = sb("w1_hi", [P, 2 * FFN], F32R)
        w1_lo = sb("w1_lo", [P, 2 * FFN], F32R)
        w2_sb = sb("w2_sb", [P, NF, D])

        parts_sb = sb("parts_sb", [P, 4, TOK], F32R)
        xs_hi, xs_lo, y_hi, y_lo = (parts_sb[:, i, :] for i in range(4))
        v_sb = sb("v_sb", [P, CHUNKS, PAIRS, SPAN])
        sq = [sb("sq_q", [P, TOK]), sb("sq_k", [P, TOK])]
        sq_hi = sb("sq_hi", [P, 2, TOK], F32R)
        sq_lo = sb("sq_lo", [P, 2, TOK], F32R)
        pair_r = sb("pair_r", [P, P], F32R)
        r_norm = [sb("r_q", [P, TOK]), sb("r_k", [P, TOK])]
        sin_raw = [sb("sr_q", [P, TOK]), sb("sr_k", [P, TOK])]
        t_cos = [sb("tc_q", [P, TOK]), sb("tc_k", [P, TOK])]
        t_sin = [sb("ts_q", [P, TOK]), sb("ts_k", [P, TOK])]
        rotated = [sb("rot_q", [P, TOK]), sb("rot_k", [P, TOK])]
        fin = sb("fin", [P, 4, TOK])
        q_fin, k_fin = fin[:, 0:2, :], fin[:, 2:4, :]
        q16 = sb("q16", [P, 2, TOK], BF16)
        k16 = sb("k16", [P, 2, WINDOW + TOK], BF16)
        neg_max = sb("neg_max", [P, 2, CHUNKS], BF16)
        neg_row = sb("neg_row", [1, 2, TOK], BF16)
        probs_t = sb("probs_t", [P, 2, CHUNKS * KEYS - WINDOW])
        inv_sums = sb("inv_sums", [P, TOK])
        o_feat = sb("o_feat", [P, PAIRS, TOK])
        x_mid = sb("x_mid", [P, TOK])
        x_sh = sb("x_sh", [P, TOK])
        x_cen = sb("x_cen", [P, TOK])
        sq_f = sb("sq_f", [P, TOK])
        rstd_f = q_pos
        y_f = sq_f
        gates = sb("gates", [P, NF, TOK])
        values = sb("values", [P, NF, TOK])

        mask_raw = gates[:].rearrange("p a t -> p (a t)")[:, 0:5 * KEYS + 2 * P]
        wkqv_sb = values[:, 0, 0:3 * P]
        wq_pad = o_feat[:, 0, :]
        wk_pad = o_feat[:, 1, :]
        m_lo = r_norm[1][:, GROUP:2 * GROUP]
        m_cols = r_norm[1][:, 16:16 + 4 * GROUP]
        add_q = o_feat[:, 2:2 + GROUP, :]
        add_k = fin
        qa = parts_sb
        m_round = sb("m_round", [P, GROUP], F32R)
        stats = sq[0][:, 0:CHUNKS * 6].rearrange("p (c k) -> p c k", k=6)
        mean_var = sq[1][:, 0:CHUNKS * 2].rearrange("p (c k) -> p c k", k=2)
        rstd = r_norm[0][:, 0:CHUNKS]
        x_nrm = x_mid[:, :].rearrange("p (c d) -> p c d", c=CHUNKS)
        xn_t = x_sh
        part_hi = t_cos[0]
        scaled = t_sin[0]
        v_slots = [o_feat[:, 6, :], o_feat[:, 7, :], gates[:, 0, :], gates[:, 1, :]]
        o_group = rotated[0]
        v_flat = v_sb[:].rearrange("p c a d -> p c (a d)")
        p_glob = v_flat[:, :, 0:TOK]
        pt_glob = v_flat[:, :, TOK:2 * TOK]
        ka = [w1_hi[:, 0:TOK], w1_lo[:, 0:TOK]] + [sq_hi[:, i, :] for i in range(GROUP - 2)]
        g_max = sb("g_max", [P, HEADS * CHUNKS])
        g_sum = sb("g_sum", [P, CHUNKS, HEADS])
        g_inv = sb("g_inv", [P, CHUNKS, HEADS])
        o_glob = rotated[1][:, :].rearrange("p (c d) -> p c d", c=CHUNKS)

        s_const = sem("const_loaded")
        s_par = sem("params_loaded")
        s_zero = sem("zeroed")
        s_x = sem("x_loaded")
        s_raw = [sem(f"qkv_raw{i}_loaded") for i in range(2)]
        s_w = sem("qkv_split")
        p_hi = sem("pool_hi")
        p_w1 = sem("pool_w1")
        v0 = sem("dve_setup")
        s_wo = sem("wo_loaded")
        s_w1 = sem("w1_loaded")
        s_w1s = sem("w1_split")
        s_w2 = sem("w2_loaded")
        a_m = sem("a_m")
        a_stat = sem("a_stat")
        a_mv = sem("a_mv")
        a_ln = sem("a_ln")
        a_rstd = sem("a_rstd")
        a_xn = sem("a_xn")
        a_xt = sem("a_xt")
        a_xte = sem("a_xte")
        a_proj = sem("a_proj")
        a_hi = sem("a_hi")
        a_mix = sem("a_mix")
        a_qk = sem("a_qk")
        a_v = sem("a_v")
        a_ve = sem("a_ve")
        a_s = sem("a_scores")
        a_max = sem("a_max")
        a_exp = sem("a_exp")
        a_pt = sem("a_pt")
        a_pte = sem("a_pte")
        a_o = sem("a_o")
        a_inv = sem("a_inv")
        a_og = sem("a_og")
        a_ot = sem("a_ot")
        a_oe = sem("a_oe")
        a_x1 = sem("a_x1")
        a_yt = sem("a_yt")
        a_state = sem("a_state")
        s_xs = sem("xs_ready")
        s_xhi = sem("xs_hi_written")
        s_p = [sem("q_proj"), sem("k_proj")]
        s_sq = [sem("q_squared"), sem("k_squared")]
        s_sqh = [sem("q_squares_high"), sem("k_squares_high")]
        s_sql = [sem("q_squares_low"), sem("k_squares_low")]
        s_sin = [sem("q_times_sin"), sem("k_times_sin")]
        s_swap = [sem("q_halves_swapped"), sem("k_halves_swapped")]
        s_mul = [sem("q_times_tables"), sem("k_times_tables")]
        s_rot = [sem("q_rotated"), sem("k_rotated")]
        s_n2 = [sem("q_norm2"), sem("k_norm2")]
        s_ln = [sem("q_ln"), sem("k_ln")]
        s_r = [sem("q_rnorm"), sem("k_rnorm")]
        s_fin = [sem("q_final"), sem("k_final")]
        s_v = sem("v_proj")
        s_ve = [sem("v_even_out"), sem("v_odd_out")]
        s_16 = [sem("q_rounded"), sem("k_rounded")]
        s_s = sem("rounded_scores")
        s_mx = sem("max_ready")
        s_tm = sem("max_turned")
        s_nm = sem("max_row_ready")
        s_st = sem("turned_scores")
        s_e = sem("probs_ready")
        s_o = sem("attended")
        s_lns = sem("sums_ln")
        s_sum = sem("inv_sums_ready")
        s_nrm = sem("o_feat_ready")
        f_wo = sem("f_wo")
        f_mid = sem("f_mid")
        f_sh = sem("f_sh")
        f_mean = sem("f_mean")
        f_cen = sem("f_cen")
        f_sq = sem("f_sq")
        f_var = sem("f_var")
        f_ln = sem("f_ln")
        f_rstd = sem("f_rstd")
        f_y = sem("f_y")
        f_yhi = sem("f_yhi")
        f_ylo = sem("f_ylo")
        f_h = sem("f_h")
        f_he = sem("f_he")
        f_gelu = sem("f_gelu")
        f_prod = sem("f_prod")
        f_w2 = sem("f_w2")
        f_x = sem("f_x")
        o_t = sem("o_t")
        o_e = sem("o_e")
        s_out = sem("out_stored")

        UNITS = HEADS * CHUNKS
        SCORE_BANKS, TURN_BANKS = (3, 4, 0), (5, 6, 2)
        TURN_AT = {(g + 1) * GROUP * CHUNKS + 7: g for g in range(GROUP - 1)}
        NORM_BANKS = (0, 6)
        PROJECT_AT = {(i // 2 - 1) * GROUP * CHUNKS + 4 + 5 * (i % 2): i for i in range(2, 2 * GROUP)}

        def value_place(t):
            c, half = divmod(t, 2)
            pairs = slice(half * PAIRS // 2, (half + 1) * PAIRS // 2)
            return v_sb[:, c, pairs, :].rearrange("p a (x d) -> p a x d", d=DIM_HEAD)[:, :, 0:3:2, :]

        def value_source(t):
            return bank[6 + t % 2][:].rearrange("p (a x d) -> p a x d", x=2, d=DIM_HEAD)

        block = ctx.enter_context(nc.Block())

        @block.sync
        def _(sp):
            sp.dma_start(x_tok[:], x.rearrange("b (c p) d -> p (b c) d", p=P)).then_inc(s_x, 16)
            sp.dma_start(wide_sb[:], wide).then_inc(s_const, 16)
            sp.dma_start(mask_raw, masks).then_inc(s_const, 16)
            sp.dma_start(wkqv_sb, w_kqv).then_inc(s_const, 16)
            sp.wait_ge(s_zero, 1)
            with nc.allow_non_contiguous_dma("sixteen numbers"):
                for r in range(3 * GLOBAL_DIM, 3 * GLOBAL_DIM + 4):
                    sp.dma_start(m_col[r:r + SLOT * (GROUP - 1) + 1:SLOT, :],
                                 m.rearrange("(g h) a b -> h (g a b)", g=GROUP)).then_inc(s_const, 16)
            sp.dma_start(rot_sb[:], rotary).then_inc(s_par, 16)

            def load_pair(l, pair):
                sp.dma_start(w_raw[:, pair % 2, :, :],
                             w_qkv[l, :, :].rearrange("d (t n) -> d t n", t=3)[:, :, pair * P:(pair + 1) * P]
                             ).then_inc(s_raw[pair % 2], 16)

            def load_wo(l):
                if not (isinstance(l, int) and l == 0):
                    sp.wait_ge(f_wo, SEQS * l)
                sp.dma_start(wo_sb[:], w_o[l, :, :].rearrange("(a p) n -> p a n", p=P)).then_inc(s_wo, 16)

            def load_w1(l):
                if not (isinstance(l, int) and l == 0):
                    sp.wait_ge(s_w1s, l)
                sp.dma_start(w1_raw[:], w_1[l, :, :]).then_inc(s_w1, 16)

            def load_w2(l):
                if not (isinstance(l, int) and l == 0):
                    sp.wait_ge(f_w2, SEQS * l)
                sp.dma_start(w2_sb[:, 0:NF - 1, :], w_2[l, 0:(NF - 1) * P, :].rearrange("(a p) n -> p a n", p=P)
                             ).then_inc(s_w2, 16)
                sp.dma_start(w2_sb[0:FFN_TILES[-1][1], NF - 1, :], w_2[l, (NF - 1) * P:FFN, :]).then_inc(s_w2, 16)

            def swap_halves(n, i):
                sp.wait_ge(s_sin[i], n + 1)
                for a in range(2):
                    sp.dma_start(t_sin[i][a:P - 1 + a:2, :], sin_raw[i][1 - a:P - a:2, :]).then_inc(s_swap[i], 16)

            def body(g, l_rest=None, l_next=None, last=False):
                for p in range(PAIRS):
                    n = PAIRS * g + p
                    if not (last and p == PAIRS - 1):
                        swap_halves(n + 1, 0)
                        swap_halves(n + 1, 1)
                    if l_next is not None:
                        if p == 0:
                            sp.wait_ge(s_w, PAIRS * l_next - 1)
                            load_pair(l_next, 0)
                        if p + 1 < PAIRS:
                            sp.wait_ge(s_w, PAIRS * l_next + p)
                            load_pair(l_next, p + 1)
                    if l_rest is not None:
                        if p == 0:
                            load_w1(l_rest)
                        if p == 2:
                            load_wo(l_rest)
                        if p == PAIRS - 1:
                            load_w2(l_rest)

            for pair in range(PAIRS):
                if pair >= 2:
                    sp.wait_ge(s_w, pair - 1)
                load_pair(0, pair)
            with nc.allow_non_contiguous_dma("per-feature parameters, once"):
                for i, src in enumerate((q_scale, k_scale)):
                    cols = src.rearrange("l d -> d l")
                    for h in range(2):
                        base = h * DIM_HEAD
                        for a in range(2):
                            sp.dma_start(scales[base + a:base + DIM_HEAD - 1 + a:2, i, :],
                                         cols[a * DIM_HEAD // 2:(a + 1) * DIM_HEAD // 2, :]).then_inc(s_par, 16)
                for i, src in enumerate((ln_g, ln_b, b_2)):
                    sp.dma_start(vecs[:, i, :], src.rearrange("l d -> d l")).then_inc(s_par, 16)
                for k, off in enumerate((FFN, 0)):
                    for j, (at, n) in enumerate(FFN_TILES):
                        sp.dma_start(b1_sb[0:n, k * NF + j, :], b_1[:, off + at:off + at + n].rearrange("l d -> d l")
                                     ).then_inc(s_par, 16)
            load_wo(0)
            load_w1(0)
            load_w2(0)
            swap_halves(0, 0)
            swap_halves(0, 1)

            def layer(l, first=False, last=False):
                body(SEQS * l, l_rest=None if first else l)
                with sp.Fori(1, SEQS - 1) as s:
                    body(SEQS * l + s)
                body(SEQS * l + SEQS - 1, l_next=None if last else l + 1, last=last)

            layer(0, first=True)
            with sp.Fori(1, DEPTH - 1) as l:
                layer(l)
            layer(DEPTH - 1, last=True)
            for s in range(SEQS):
                for c in range(CHUNKS):
                    i = s * CHUNKS + c
                    sp.wait_ge(o_e, i + 1)
                    sp.dma_start(out[s, c * P:(c + 1) * P, :], x_tok[:, i, :]).then_inc(s_out, 16)
            sp.wait_ge(s_out, 16 * SEQS * CHUNKS)

        PARAM_LOADS = 1 + 8 + 3 + 2 * NF
        CONST_LOADS = 3 + 4

        @block.gpsimd
        def _(pool):
            pool.memset(m_col[:], 0.0).then_inc(s_zero, 1)

            def split_pair(l, pair):
                loads = 16 * (PAIRS // 2 * l + pair // 2 + 1)
                split = PAIRS * l + pair + 1
                pool.wait_ge(s_raw[pair % 2], loads)
                hi, lo = w_hi[:, :, pair, :], w_lo[:, :, pair, :]
                raw = w_raw[:, pair % 2, :, :]
                raw_half = raw[:, 0:2, :].rearrange("p t (h a j) -> p t h a j", h=2, a=2)
                hi_half, lo_half = (part[:, 0:2, :].rearrange("p t (h j a) -> p t h a j", h=2, a=2) for part in (hi, lo))
                for a in range(2):
                    pool.tensor_tensor(hi_half[:, :, :, a, :], raw_half[:, :, :, a, :],
                                       zero.unsqueeze(2).unsqueeze(3).to_broadcast([P, 2, 2, DIM_HEAD // 2]), ALU.add)
                pool.tensor_tensor(hi[:, V_W, :], raw[:, V_W, :], zero.to_broadcast([P, P]), ALU.add).then_inc(p_hi, 1)
                pool.wait_ge(p_hi, split)
                for a in range(2):
                    pool.tensor_tensor(lo_half[:, :, :, a, :], raw_half[:, :, :, a, :],
                                       hi_half[:, :, :, a, :].bitcast(F32), ALU.subtract)
                pool.tensor_tensor(lo[:, V_W, :], raw[:, V_W, :], hi[:, V_W, :].bitcast(F32), ALU.subtract
                                   ).then_inc(s_w, 1)

            def low_squares(n, i):
                pool.wait_ge(s_sqh[i], n + 1)
                if not (isinstance(n, int) and n == 0):
                    pool.wait_ge(s_n2[i], n)
                pool.tensor_tensor(sq_lo[:, i, :], sq[i][:], sq_hi[:, i, :].bitcast(F32), ALU.subtract
                                   ).then_inc(s_sql[i], 1)

            def add(n, i):
                pool.wait_ge(s_mul[i], n + 1)
                pool.wait_ge(s_swap[i], 32 * (n + 1))
                if not (isinstance(n, int) and n == 0):
                    pool.wait_ge(s_fin[i], n)
                pool.tensor_tensor(rotated[i][:], t_cos[i][:], t_sin[i][:], ALU.add).then_inc(s_rot[i], 1)

            def split_w1(l):
                pool.wait_ge(s_w1, 16 * (l + 1))
                pool.wait_ge(f_x, SEQS * l + 1)
                pool.tensor_tensor(w1_hi[:], w1_raw[:], zero.to_broadcast([P, 2 * FFN]), ALU.add).then_inc(p_w1, 1)
                pool.wait_ge(p_w1, l + 1)
                pool.tensor_tensor(w1_lo[:], w1_raw[:], w1_hi[:].bitcast(F32), ALU.subtract).then_inc(s_w1s, 1)

            def body(g, l_next=None, last=False):
                for p in range(PAIRS):
                    if not (last and p == PAIRS - 1):
                        low_squares(PAIRS * g + p + 1, 0)
                        low_squares(PAIRS * g + p + 1, 1)
                        add(PAIRS * g + p + 1, 0)
                        add(PAIRS * g + p + 1, 1)
                    if l_next is not None:
                        pool.wait_ge(s_p[1], PAIRS * g + p + 1)
                        pool.wait_ge(s_v, V_TILES * (g + 1))
                        split_pair(l_next, p)

            pool.wait_ge(s_const, 16 * CONST_LOADS)
            for pair in range(PAIRS):
                split_pair(0, pair)
            pool.wait_ge(a_ot, GROUP * SEQS)
            low_squares(0, 0)
            low_squares(0, 1)
            add(0, 0)
            add(0, 1)

            def layer(l, last):
                body(SEQS * l)
                split_w1(l)
                with pool.Fori(1, SEQS - 1) as s:
                    body(SEQS * l + s)
                body(SEQS * l + SEQS - 1, None if last else l + 1, last)

            with pool.Fori(0, DEPTH - 1) as l:
                layer(l, False)
            layer(DEPTH - 1, True)

        @block.tensor
        def _(pe):
            def three(dst, lhs, rhs, stop=True):
                (lh, ll), (rh, rl) = lhs, rhs
                pe.matmul(dst, lh, rh, start=True, stop=False)
                pe.matmul(dst, lh, rl, start=False, stop=False)
                return pe.matmul(dst, ll, rh, start=False, stop=True)

            pe.wait_ge(s_const, 16 * CONST_LOADS)
            with pe.Fori(0, SEQS) as s:
                pe.wait_ge(a_xn, 2 * s + 1)
                for c in range(CHUNKS):
                    mm = pe.transpose(bank[0][:, c * P:(c + 1) * P], x_nrm[:, c, :], eye)
                mm.then_inc(a_xt, 1)
                pe.wait_ge(a_xte, s + 1)
                def project_group(i):
                    w = (wq_pad, wk_pad)[i % 2]
                    if i >= 2:
                        pe.wait_ge(a_hi, 2 * GROUP * s + i)
                        if i % 2 == 1 and i > 3:
                            pe.wait_ge(a_oe, GROUP * s + i // 2 - 1)
                    elif i == 0:
                        pe.wait_ge(a_m, 1)
                    pe.matmul(bank[2 if i == 1 else 1][:], w[:, (i // 2) * P:(i // 2 + 1) * P], xn_t[:],
                              start=True, stop=True).then_inc(a_proj, 1)

                project_group(0)
                project_group(1)
                for c in range(CHUNKS):
                    mm = pe.matmul(bank[0][:, c * P:(c + 1) * P], xn_t[:, c * P:(c + 1) * P],
                                   wkqv_sb[:, 2 * P:3 * P], start=True, stop=True)
                mm.then_inc(a_v, 1)

                def scores(u):
                    h, c = divmod(u, CHUNKS)
                    grp, r = divmod(h, GROUP)
                    n = (c + 1) * P
                    dst = bank[SCORE_BANKS[u % 3]]
                    if u % (GROUP * CHUNKS) == 0:
                        pe.wait_ge(a_qk, 2 * GROUP * s + 2 * grp + 2)
                    if u == 2:
                        pe.wait_ge(a_ve, s + 1)
                    if u >= 3:
                        pe.wait_ge(a_exp, UNITS * s + u - 2)
                    rows = slice(SLOT * r, SLOT * (r + 1))
                    pe.matmul(dst[:, 0:n], qa[rows, grp, c * P:(c + 1) * P], ka[grp][rows, 0:n],
                              start=True, stop=False)
                    pe.matmul(dst[:, n - P:n], eye16, causal_mask, start=False, stop=True).then_inc(a_s, 1)

                def turn(u):
                    h, c = divmod(u, CHUNKS)
                    pe.wait_ge(a_exp, UNITS * s + u + 1)
                    if u >= 3:
                        pe.wait_ge(a_pte, UNITS * s + u - 2)
                    for b in range(c + 1):
                        mm = pe.transpose(bank[TURN_BANKS[u % 3]][:, b * P:(b + 1) * P], p_glob[:, u % 3, b * P:(b + 1) * P],
                                          eye)
                    mm.then_inc(a_pt, 1)

                def attend(u):
                    h, c = divmod(u, CHUNKS)
                    pe.wait_ge(a_pte, UNITS * s + u + 1)
                    if u == 0:
                        pe.wait_ge(a_ve, s + 1)
                    grp, r = divmod(h, GROUP)
                    if r == 0 and c == 0 and grp > 0:
                        pe.wait_ge(a_og, GROUP * s + grp)
                    slot = slice(SLOT * r, SLOT * (r + 1))
                    for b in range(c + 1):
                        mm = pe.matmul(bank[7][slot, c * P:(c + 1) * P], v_slots[b][:, h * SLOT:(h + 1) * SLOT],
                                       pt_glob[:, u % 3, b * P:(b + 1) * P], start=(b == 0), stop=(b == c),
                                       skip_group_check=True)
                    mm.then_inc(a_o, 1)

                def turn_group(grp):
                    pe.wait_ge(a_og, GROUP * s + grp + 1)
                    pe.wait_ge(a_hi, 2 * GROUP * s + min(2 * grp + 5, 2 * GROUP))
                    for c in range(CHUNKS):
                        mm = pe.transpose(bank[1][:, c * P:(c + 1) * P], o_group[:, c * P:(c + 1) * P], eye)
                    mm.then_inc(a_ot, 1)

                for u in range(UNITS + 3):
                    if u in PROJECT_AT:
                        project_group(PROJECT_AT[u])
                    if u < UNITS:
                        scores(u)
                    if u in TURN_AT:
                        turn_group(TURN_AT[u])
                    if 2 <= u < UNITS + 2:
                        turn(u - 2)
                    if u >= 3:
                        attend(u - 3)
                turn_group(GROUP - 1)
                pe.wait_ge(a_xn, 2 * s + 2)
                for c in range(CHUNKS):
                    mm = pe.transpose(bank[0][:, c * P:(c + 1) * P], x_nrm[:, c, :], eye)
                mm.then_inc(a_yt, 1)

            def project(n, g, p, i):
                if i == 0:
                    pe.wait_ge(s_w, PAIRS * (g // SEQS) + p + 1)
                    if p == 0:
                        pe.wait_ge(s_xs, g + 1)
                if not (isinstance(n, int) and n == 0):
                    pe.wait_ge((s_ln[0], s_mul[1])[i], n)
                three(bank[i][:], (w_hi[:, i, p, :], w_lo[:, i, p, :]), (xs_hi, xs_lo)).then_inc(s_p[i], 1)

            def norm2(n, i, g=None):
                pe.wait_ge(s_sql[i], n + 1)
                if i == 1 and g is not None:
                    pe.wait_ge(s_ve[0], V_TILES // 2 * (g + 1))
                if i == 0:
                    pe.wait_ge(s_mul[0], n + 1)
                dst = bank[NORM_BANKS[i]]
                pe.matmul(dst[:], pair_r[:], sq_hi[:, i, :], start=True, stop=False)
                pe.matmul(dst[:], pair_r[:], sq_lo[:, i, :], start=False, stop=True).then_inc(s_n2[i], 1)

            def value_tiles(g, n):
                pe.wait_ge(s_w, PAIRS * (g // SEQS + 1))
                for t in range(V_TILES):
                    c, half = divmod(t, 2)
                    if t == 0:
                        pe.wait_ge(s_ln[1], n + 1)
                    elif t == 1:
                        if not (isinstance(g, int) and g == 0):
                            pe.wait_ge(f_x, g)
                    else:
                        pe.wait_ge(s_ve[t % 2], V_TILES // 2 * g + t // 2)
                    lhs = (xs_hi[:, c * P:(c + 1) * P], xs_lo[:, c * P:(c + 1) * P])
                    w = slice(half * PAIRS // 2, (half + 1) * PAIRS // 2)
                    three(bank[6 + t % 2][:], lhs, (w_hi[:, V_W, w, :], w_lo[:, V_W, w, :])).then_inc(s_v, 1)

            def max_scores(n, p, h):
                if h == 0:
                    pe.wait_ge(s_16[0], n + 1)
                    pe.wait_ge(s_16[1], n + 1)
                if not (isinstance(n, int) and n == 0):
                    pe.wait_ge(s_nrm, 2 * n - 1 + h)
                rows = slice(DIM_HEAD * h, DIM_HEAD * (h + 1))
                for b in range(2):
                    dst = bank[2 + 2 * h + b]
                    pe.matmul(dst[:, 0:2 * KEYS], eye16, local_mask[:, b * KEYS:(b + 2) * KEYS], start=True, stop=False)
                    for c in range(2 * b, 2 * b + 2):
                        mm = pe.matmul(dst[:, (c % 2) * KEYS:(c % 2 + 1) * KEYS], q16[rows, p % 2, c * P:(c + 1) * P],
                                       k16[rows, p % 2, c * P:c * P + KEYS], start=False, stop=(c % 2 == 1))
                    mm.then_inc(s_s, 1)

            def turn_max(n, h):
                pe.wait_ge(s_mx, 4 * n + 2 * h + 2)
                if h == 1:
                    pe.wait_ge(s_e, 4 * n + 2)
                for c in range(CHUNKS):
                    mm = pe.matmul(bank[5 - 2 * h][0:1, c * P:(c + 1) * P], neg_max[:, h, c:c + 1], eye16,
                                   start=True, stop=True, skip_group_check=True)
                mm.then_inc(s_tm, 1)

            def turned_scores(n, p, h, between=None):
                rows = slice(DIM_HEAD * h, DIM_HEAD * (h + 1))
                spans = [(bank[2 + 2 * h + c // 2], c, (c % 2) * KEYS, min(KEYS, TOK - c * P)) for c in range(CHUNKS)]
                for b in range(2):
                    width = min(2 * KEYS, CHUNKS * KEYS - WINDOW - 2 * b * KEYS)
                    pe.matmul(bank[2 + 2 * h + b][:, 0:width], eye16, local_mask_t[:, 0:width], start=True, stop=False)
                    for dst, c, at, q in spans[2 * b:2 * b + 2]:
                        pe.matmul(dst[:, at:at + q], k_fin[rows, p % 2, c * P:(c + 1) * P],
                                  q_fin[rows, p % 2, c * P:c * P + q], start=False, stop=False)
                if between is not None:
                    between()
                pe.wait_ge(s_nm, 2 * n + h + 1)
                for b in range(2):
                    for dst, c, at, q in spans[2 * b:2 * b + 2]:
                        mm = pe.matmul(dst[:, at:at + q], ones16[:], neg_row[:, h, c * P:c * P + q],
                                       start=False, stop=(c % 2 == 1))
                    mm.then_inc(s_st, 1)

            def attend_local(n, g, p, h):
                if h == 0 and p == 0:
                    pe.wait_ge(s_ve[0], V_TILES // 2 * (g + 1))
                    pe.wait_ge(s_ve[1], V_TILES // 2 * (g + 1))
                pe.wait_ge(s_e, 4 * n + 2 * h + 2)
                dst = bank[2 + 2 * h]
                for c in range(CHUNKS):
                    q = min(KEYS, TOK - c * P)
                    mm = pe.matmul(dst[:, c * P:c * P + q], v_sb[:, c, p, h * DIM_HEAD:h * DIM_HEAD + P],
                                   probs_t[:, h, c * KEYS:c * KEYS + q], start=(c == 0), stop=(c == CHUNKS - 1),
                                   skip_group_check=True)
                mm.then_inc(s_o, 1)

            def ffn_parts(f, after_values):
                l = f // SEQS

                def out_proj():
                    pe.wait_ge(s_nrm, 2 * PAIRS * (f + 1))
                    pe.wait_ge(s_wo, 16 * (l + 1))
                    if after_values:
                        pe.wait_ge(s_ve[1], V_TILES // 2 * (f + 2))
                    else:
                        pe.wait_ge(f_x, f + 1)
                    for a in range(PAIRS):
                        mm = pe.matmul(bank[7][:], wo_sb[:, a, :], o_feat[:, a, :], start=(a == 0),
                                       stop=(a == PAIRS - 1))
                    mm.then_inc(f_wo, 1)

                def mean():
                    pe.wait_ge(f_sh, f + 1)
                    pe.matmul(bank[7][:], mean_w, x_sh[:], start=True, stop=True).then_inc(f_mean, 1)

                def var():
                    pe.wait_ge(f_sq, f + 1)
                    pe.matmul(bank[7][:], mean_w, sq_f[:], start=True, stop=True).then_inc(f_var, 1)

                def up(i):
                    def run():
                        at, n = FFN_TILES[i % NF]
                        off = at + (FFN if i < NF else 0)
                        if i == 0:
                            pe.wait_ge(f_ylo, f + 1)
                            pe.wait_ge(s_w1s, l + 1)
                        else:
                            pe.wait_ge(f_he, 2 * NF * f + i)
                        three(bank[7][0:n, :], (w1_hi[:, off:off + n], w1_lo[:, off:off + n]), (y_hi, y_lo)
                              ).then_inc(f_h, 1)
                    return run

                def down():
                    pe.wait_ge(f_prod, f + 1)
                    pe.wait_ge(s_w2, 32 * (l + 1))
                    for j, (_, n) in enumerate(FFN_TILES):
                        mm = pe.matmul(bank[7][:], w2_sb[0:n, j, :], gates[0:n, j, :], start=(j == 0),
                                       stop=(j == NF - 1))
                    mm.then_inc(f_w2, 1)

                return {(0, 0): out_proj, (1, 0): mean, (1, 1): var, (2, 1): up(0), (3, 0): up(1), (3, 1): up(2),
                        (4, 0): up(3), (4, 1): up(4), (5, -1): up(5), (6, 0): down}

            def body(g, first=False, last=False):
                parts = {} if first else ffn_parts(g - 1, True)
                for p in range(PAIRS):
                    n = PAIRS * g + p
                    nxt = not (last and p == PAIRS - 1)
                    gn, pn = (g, p + 1) if p + 1 < PAIRS else (g + 1, 0)
                    if nxt:
                        project(n + 1, gn, pn, 0)
                        project(n + 1, gn, pn, 1)
                    max_scores(n, p, 0)
                    if not (first and p == 0):
                        attend_local(n - 1, g, (p - 1) % PAIRS, 1)
                    turn_max(n, 0)
                    turned_scores(n, p, 0, parts.get((p, -1)))
                    if p == 0:
                        value_tiles(g, n)
                    if nxt:
                        norm2(n + 1, 0)
                    max_scores(n, p, 1)
                    if nxt:
                        norm2(n + 1, 1, g if p == 0 else None)
                    if (p, 0) in parts:
                        parts[(p, 0)]()
                    attend_local(n, g, p, 0)
                    turn_max(n, 1)
                    turned_scores(n, p, 1)
                    if (p, 1) in parts:
                        parts[(p, 1)]()

            project(0, 0, 0, 0)
            project(0, 0, 0, 1)
            norm2(0, 0)
            norm2(0, 1)
            body(0, first=True)
            with pe.Fori(1, BODIES - 1) as g:
                body(g)
            body(BODIES - 1, last=True)
            attend_local(PAIRS * BODIES - 1, BODIES - 1, PAIRS - 1, 1)
            tail = ffn_parts(BODIES - 1, False)
            for key in sorted(tail):
                tail[key]()
            pe.wait_ge(f_x, BODIES + 1)
            for i in range(SEQS * CHUNKS // 4):
                if i >= 2:
                    pe.wait_ge(o_e, 4 * (i - 1))
                for c in range(4):
                    mm = pe.transpose(bank[i % 2][:, c * P:(c + 1) * P], state[:, (4 * i + c) * P:(4 * i + c + 1) * P],
                                      eye)
                mm.then_inc(o_t, 1)

        @block.scalar
        def _(act):
            def rstd_of(s, k):
                act.wait_ge(a_mv, 2 * s + k + 1)
                act.activation(rstd, mean_var[:, :, 1], ACT.Ln, bias=const(C_EPS)).then_inc(a_ln, 1)
                act.wait_ge(a_ln, 2 * s + k + 1)
                act.activation(rstd, rstd, ACT.Exp, scale=-0.5).then_inc(a_rstd, 1)

            act.preload_act_table_set(LN_EXP)
            act.wait_ge(s_const, 16 * CONST_LOADS)
            with act.Fori(0, SEQS) as s:
                rstd_of(s, 0)
                act.wait_ge(a_xt, s + 1)
                act.activation(xn_t[:], bank[0][:], ACT.Copy).then_inc(a_xte, 1)

                def scale_group(i):
                    j = 2 * GROUP * s + i
                    act.wait_ge(a_proj, j + 1)
                    if i > 0:
                        act.wait_ge(a_qk, j)
                    src = bank[2 if i == 1 else 1]
                    scale = (float(D) ** -0.5, 1.0)[i % 2]
                    act.activation(scaled[:], src[:], ACT.Copy, scale=scale)
                    act.activation(part_hi[:].bitcast(F32R), src[:], ACT.Copy, scale=scale).then_inc(a_hi, 1)

                scale_group(0)
                scale_group(1)
                act.wait_ge(a_v, s + 1)
                for c in range(CHUNKS):
                    one = act.activation(v_slots[c].rearrange("p (h r) -> p h r", r=SLOT)[:, :, 0:GLOBAL_DIM],
                                         bank[0][:, c * P:(c + 1) * P].rearrange("p (h d) -> p h d", d=GLOBAL_DIM),
                                         ACT.Copy)
                one.then_inc(a_ve, 1)

                def group_out(grp):
                    act.wait_ge(a_o, UNITS * s + GROUP * CHUNKS * (grp + 1))
                    if grp > 0:
                        act.wait_ge(a_ot, GROUP * s + grp)
                    act.activation(o_group[:], bank[7][:], ACT.Copy).then_inc(a_og, 1)

                for u in range(UNITS):
                    h, c = divmod(u, CHUNKS)
                    n = (c + 1) * P
                    if u > 3 and (u - 3) % (GROUP * CHUNKS) == 0:
                        group_out((u - 3) // (GROUP * CHUNKS) - 1)
                    act.wait_ge(a_max, UNITS * s + u + 1)
                    if u >= 3:
                        act.wait_ge(a_pt, UNITS * s + u - 2)
                    act.activation(p_glob[:, u % 3, 0:n], bank[SCORE_BANKS[u % 3]][:, 0:n], ACT.Exp,
                                   bias=g_max[:, u:u + 1], accum_out=g_sum[:, c, h:h + 1]).then_inc(a_exp, 1)
                    if u in PROJECT_AT:
                        scale_group(PROJECT_AT[u])
                group_out(GROUP - 1)
                rstd_of(s, 1)
                act.wait_ge(a_yt, s + 1)
                act.activation(state[:, bass.ds(s * TOK, TOK)], bank[0][:], ACT.Copy).then_inc(a_state, 1)

            def square(n, i):
                act.wait_ge(s_p[i], n + 1)
                if not (isinstance(n, int) and n == 0):
                    act.wait_ge(s_n2[i], n)
                act.activation(sq[i][:], bank[i][:], ACT.Square).then_inc(s_sq[i], 1)
                act.wait_ge(s_sq[i], n + 1)
                act.activation(sq_hi[:, i, :], sq[i][:], ACT.Copy).then_inc(s_sqh[i], 1)

            def rnorm(n, i):
                act.wait_ge(s_n2[i], n + 1)
                if not (isinstance(n, int) and n == 0):
                    act.wait_ge(s_fin[i], n)
                act.activation(r_norm[i][:], bank[NORM_BANKS[i]][:], ACT.Ln, bias=const(C_TINY),
                               scale=float(2 ** NORM_SHIFT)).then_inc(s_ln[i], 1)
                act.wait_ge(s_ln[i], n + 1)
                act.activation(r_norm[i][:], r_norm[i][:], ACT.Exp, bias=const(C_SHIFT), scale=-0.5).then_inc(s_r[i], 1)

            def max_row(n, h):
                act.wait_ge(s_tm, 2 * n + h + 1)
                act.activation(neg_row[:, h, :], bank[5 - 2 * h][0:1, :], ACT.Copy).then_inc(s_nm, 1)

            def exps(n, h):
                for b in range(2):
                    width = min(2 * KEYS, CHUNKS * KEYS - WINDOW - 2 * b * KEYS)
                    act.wait_ge(s_st, 4 * n + 2 * h + b + 1)
                    if b == 0 and not (isinstance(n, int) and n == 0):
                        act.wait_ge(s_o, 2 * n - 1 + h)
                    act.activation(probs_t[:, h, 2 * b * KEYS:2 * b * KEYS + width], bank[2 + 2 * h + b][:, 0:width],
                                   ACT.Exp).then_inc(s_e, 1)

            def invert_sums(n, h):
                act.wait_ge(s_o, 2 * n + h + 1)
                if not (isinstance(n, int) and n == 0):
                    act.wait_ge(s_nrm, 2 * n - 1 + h)
                own = slice(DIM_HEAD * h, DIM_HEAD * (h + 1))
                other = slice(DIM_HEAD * (1 - h), DIM_HEAD * (2 - h))
                act.activation(inv_sums[own, :], bank[2 + 2 * h][other, :], ACT.Ln).then_inc(s_lns, 1)
                act.wait_ge(s_lns, 2 * n + h + 1)
                act.activation(inv_sums[own, :], inv_sums[own, :], ACT.Exp, scale=-1.0).then_inc(s_sum, 1)

            def ffn_parts(f):
                def square_f():
                    act.wait_ge(f_cen, f + 1)
                    act.activation(sq_f[:], x_cen[:], ACT.Square).then_inc(f_sq, 1)

                def rstd_f_():
                    act.wait_ge(f_var, f + 1)
                    act.activation(rstd_f, bank[7][:], ACT.Ln, bias=const(C_EPS)).then_inc(f_ln, 1)
                    act.wait_ge(f_ln, f + 1)
                    act.activation(rstd_f, rstd_f, ACT.Exp, scale=-0.5).then_inc(f_rstd, 1)

                def gelu():
                    act.preload_act_table(ACT.Gelu)
                    act.wait_ge(f_he, 2 * NF * f + NF)
                    act.activation(gates[:, 0:NF - 1, :], gates[:, 0:NF - 1, :], ACT.Gelu)

                def gelu_rest():
                    n = FFN_TILES[-1][1]
                    act.activation(gates[0:n, NF - 1, :], gates[0:n, NF - 1, :], ACT.Gelu).then_inc(f_gelu, 1)
                    act.preload_act_table_set(LN_EXP)

                return {(1, 0): square_f, (1, 1): rstd_f_, (4, 1): gelu, (5, -1): gelu_rest}

            def body(g, first=False, last=False):
                parts = {} if first else ffn_parts(g - 1)
                for p in range(PAIRS):
                    n = PAIRS * g + p
                    nxt = not (last and p == PAIRS - 1)
                    if nxt:
                        square(n + 1, 0)
                        square(n + 1, 1)
                    if (p, -1) in parts:
                        parts[(p, -1)]()
                    if not (first and p == 0):
                        invert_sums(n - 1, 1)
                    max_row(n, 0)
                    exps(n, 0)
                    if p == 0:
                        if not first:
                            act.wait_ge(s_o, 2 * PAIRS * g)
                        for t in range(0, V_TILES, 2):
                            act.wait_ge(s_v, V_TILES * g + t + 1)
                            act.activation(value_place(t), value_source(t), ACT.Copy).then_inc(s_ve[0], 1)
                    if nxt:
                        rnorm(n + 1, 0)
                        rnorm(n + 1, 1)
                    if (p, 0) in parts:
                        parts[(p, 0)]()
                    max_row(n, 1)
                    invert_sums(n, 0)
                    exps(n, 1)
                    if (p, 1) in parts:
                        parts[(p, 1)]()

            square(0, 0)
            square(0, 1)
            rnorm(0, 0)
            rnorm(0, 1)
            body(0, first=True)
            with act.Fori(1, BODIES - 1) as g:
                body(g)
            body(BODIES - 1, last=True)
            invert_sums(PAIRS * BODIES - 1, 1)
            tail = ffn_parts(BODIES - 1)
            for key in sorted(tail):
                tail[key]()

        @block.vector
        def _(dve):
            dve.memset(wq_pad[:], 0.0).then_inc(v0, 1)
            dve.memset(wk_pad[:], 0.0).then_inc(v0, 1)
            dve.memset(k16[:, :, 0:WINDOW], 0.0).then_inc(v0, 1)
            dve.memset(ones16[:], 1.0).then_inc(v0, 1)
            dve.wait_ge(s_const, 16 * CONST_LOADS)
            dve.wait_ge(v0, 4)
            dve.tensor_copy(mask_sb[:], mask_raw).then_inc(v0, 1)
            n = GLOBAL_DIM
            for w, at in ((wq_pad, P), (wk_pad, 0)):
                for k in range(3):
                    dst = w.rearrange("p (h r) -> p h r", r=SLOT)[:, :, k * n:(k + 1) * n]
                    dve.tensor_copy(dst, wkqv_sb[:, at:at + P].rearrange("p (h r) -> p h r", r=n)).then_inc(v0, 1)
            dve.tensor_copy(pair_r[:], pair_ones)
            dve.tensor_copy(m_round[:], m_col[:]).then_inc(v0, 1)
            dve.wait_ge(v0, 12)
            dve.tensor_tensor(m_lo, m_col[:], m_round[:].bitcast(F32), ALU.subtract).then_inc(v0, 1)
            dve.wait_ge(v0, 13)
            for slots in v_slots:
                dve.memset(slots, 0.0)
            k = 13
            for i, (hi_row, lo_row) in enumerate(((M_HI_Q, M_LO_Q), (M_HI_K, M_LO_K))):
                dve.tensor_scalar(m_cols[:, 4 * i:4 * i + 4], m_lo, const(lo_row), None, ALU.mult).then_inc(v0, 1)
                k += 1
                dve.wait_ge(v0, k)
                dve.scalar_tensor_tensor(out=m_cols[:, 4 * i:4 * i + 4], in0=m_round[:].bitcast(F32),
                                         scalar=const(hi_row), in1=m_cols[:, 4 * i:4 * i + 4],
                                         op0=ALU.mult, op1=ALU.add).then_inc(v0, 1)
                k += 1
                dve.wait_ge(v0, k)
            for i, (dst, pos) in enumerate(((add_q, q_pos), (add_k, k_pos))):
                for grp in range(GROUP):
                    one = dve.tensor_scalar(dst[:, grp, :], pos, m_cols[:, 4 * i + grp:4 * i + grp + 1], None, ALU.add)
            one.then_inc(a_m, 1)
            dve.wait_ge(a_m, 1)
            dve.wait_ge(s_x, 16)

            def normalise(s, k, after_sum=False):
                if after_sum:
                    dve.wait_ge(a_x1, s + 1)
                    dve.memset(scratch[:, 0:1], 0.0)
                for c in range(CHUNKS):
                    one = dve.bn_stats(stats[:, c, :], x_tok[:, bass.ds(s * CHUNKS + c, 1), :].rearrange("p a d -> p (a d)"))
                one.then_inc(a_stat, 1)
                dve.wait_ge(a_stat, 2 * s + k + 1)
                dve.memset(scratch[:, 1:2], 0.0)
                for c in range(CHUNKS):
                    one = dve.bn_aggr(mean_var[:, c, :], stats[:, c, :])
                one.then_inc(a_mv, 1)
                dve.wait_ge(a_rstd, 2 * s + k + 1)
                for c in range(CHUNKS):
                    one = dve.tensor_scalar(x_nrm[:, c, :], x_tok[:, bass.ds(s * CHUNKS + c, 1), :].rearrange("p a d -> p (a d)"),
                                            mean_var[:, c, 0:1], rstd[:, c:c + 1], ALU.subtract, ALU.mult)
                one.then_inc(a_xn, 1)

            with dve.Fori(0, SEQS) as s:
                normalise(s, 0)

                def split_group(i):
                    grp, k = divmod(i, 2)
                    j = 2 * GROUP * s + i
                    dve.wait_ge(a_hi, j + 1)
                    dve.scalar_tensor_tensor(out=part_hi[:], in0=part_hi[:], scalar=const((SIGN_Q, SIGN_K)[k]),
                                             in1=(add_q, add_k)[k][:, grp, :], op0=ALU.mult, op1=ALU.add
                                             ).then_inc(a_mix, 1)
                    dve.wait_ge(a_mix, j + 1)
                    dve.scalar_tensor_tensor(out=qa[:, grp, :] if k == 0 else ka[grp], in0=scaled[:],
                                             scalar=const((LOW_Q, LOW_K)[k]), in1=part_hi[:],
                                             op0=ALU.mult, op1=ALU.add).then_inc(a_qk, 1)

                split_group(0)
                split_group(1)

                def turned(u):
                    h, c = divmod(u, CHUNKS)
                    m_ = (c + 1) * P
                    dve.wait_ge(a_pt, UNITS * s + u + 1)
                    if u >= 3:
                        dve.wait_ge(a_o, UNITS * s + u - 2)
                    dve.tensor_copy(pt_glob[:, u % 3, 0:m_], bank[TURN_BANKS[u % 3]][:, 0:m_]).then_inc(a_pte, 1)

                def out_group(grp):
                    heads = slice(grp * GROUP, (grp + 1) * GROUP)
                    dve.wait_ge(a_exp, UNITS * s + GROUP * CHUNKS * (grp + 1))
                    dve.reciprocal(g_inv[:, :, heads], g_sum[:, :, heads]).then_inc(a_inv, 1)
                    dve.wait_ge(a_inv, GROUP * s + grp + 1)
                    dve.wait_ge(a_ot, GROUP * s + grp + 1)
                    dve.tensor_tensor(
                        o_glob.rearrange("p c (h d) -> p c h d", h=HEADS)[:, :, heads, :],
                        bank[1][:].rearrange("p (c h r) -> p c h r", c=CHUNKS, r=SLOT)[:, :, :, 0:GLOBAL_DIM],
                        g_inv[:, :, heads].unsqueeze(3).to_broadcast([P, CHUNKS, GROUP, GLOBAL_DIM]),
                        ALU.mult).then_inc(a_oe, 1)

                for u in range(UNITS + 2):
                    if u < UNITS:
                        m_ = (u % CHUNKS + 1) * P
                        dve.wait_ge(a_s, UNITS * s + u + 1)
                        dve.tensor_reduce(g_max[:, u:u + 1], bank[SCORE_BANKS[u % 3]][:, 0:m_], AX_X, ALU.max,
                                          negate=True).then_inc(a_max, 1)
                    if u >= 2:
                        turned(u - 2)
                    if u - 2 in PROJECT_AT:
                        split_group(PROJECT_AT[u - 2])
                    if u in TURN_AT:
                        out_group(TURN_AT[u])
                out_group(GROUP - 1)
                dve.wait_ge(a_oe, GROUP * (s + 1))
                xs_ = x_tok[:, bass.ds(s * CHUNKS, CHUNKS), :]
                dve.tensor_tensor(xs_, xs_, o_glob, ALU.add).then_inc(a_x1, 1)
                normalise(s, 1, True)

            dve.memset(xs_hi[DIM_HEAD:P, 0:1].bitcast(F32), 0.0).then_inc(v0, 1)
            dve.memset(xs_lo[DIM_HEAD:P, 0:1].bitcast(F32), 0.0).then_inc(v0, 1)
            dve.memset(x_sh[DIM_HEAD:P, 0:1], 0.0).then_inc(v0, 1)
            dve.memset(v_sb[:, :, :, DIM_HEAD:2 * DIM_HEAD], 1.0).then_inc(v0, 1)
            dve.wait_ge(v0, 21)
            HALF = D // 2

            def shifted_input(g, ready=None):
                at = (g % SEQS) * TOK
                if not (isinstance(g, int) and g < 2):
                    dve.wait_ge(f_x, g - 1)
                if not (isinstance(g, int) and g == 0):
                    dve.wait_ge(s_xs, g)
                src = (state[0:HALF, bass.ds(at, TOK)], state[HALF:P, bass.ds(at, TOK - 1)])
                dve.tensor_copy(xs_hi[0:HALF, :], src[0])
                dve.tensor_copy(xs_hi[HALF:P, 1:TOK], src[1]).then_inc(s_xhi, 1)
                dve.wait_ge(s_xhi, 2 * g + 1)
                dve.tensor_tensor(xs_lo[0:HALF, :], src[0], xs_hi[0:HALF, :].bitcast(F32), ALU.subtract)
                dve.tensor_tensor(xs_lo[HALF:P, 1:TOK], src[1], xs_hi[HALF:P, 1:TOK].bitcast(F32), ALU.subtract
                                  ).then_inc(s_xhi, 1)
                dve.wait_ge(s_xhi, 2 * g + 2)
                dve.memset(scratch[:, 0:1], 0.0).then_inc(s_xs, 1)

            def times_sin(n, l, i):
                dve.wait_ge(s_sq[i], n + 1)
                if not (isinstance(n, int) and n == 0):
                    dve.wait_ge(s_swap[i], 32 * n)
                    dve.wait_ge(s_rot[i], n)
                dve.scalar_tensor_tensor(out=sin_raw[i][:], in0=bank[i][:], scalar=scales[:, i, bass.ds(l, 1)],
                                         in1=rot_sb[:, 2 * i + 1, :], op0=ALU.mult, op1=ALU.mult).then_inc(s_sin[i], 1)

            def times_cos(n, l, i):
                dve.scalar_tensor_tensor(out=t_cos[i][:], in0=bank[i][:], scalar=scales[:, i, bass.ds(l, 1)],
                                         in1=rot_sb[:, 2 * i, :], op0=ALU.mult, op1=ALU.mult).then_inc(s_mul[i], 1)

            def final(n, p, i):
                dve.wait_ge(s_r[i], n + 1)
                dve.wait_ge(s_rot[i], n + 1)
                if not (isinstance(n, int) and n < 2):
                    dve.wait_ge(s_st, 4 * n - 4)
                dst = (q_fin, k_fin)[i][:, p % 2, :]
                dve.scalar_tensor_tensor(out=dst, in0=r_norm[i][:], scalar=NORM_CAP, in1=rotated[i][:],
                                         op0=ALU.min, op1=ALU.mult).then_inc(s_fin[i], 1)
                dve.wait_ge(s_fin[i], n + 1)
                dve.tensor_copy(q16[:, p % 2, :] if i == 0 else k16[:, p % 2, WINDOW:], dst).then_inc(s_16[i], 1)

            def maxima(n, h):
                for b in range(2):
                    dve.wait_ge(s_s, 4 * n + 2 * h + b + 1)
                    if b == 0 and not (isinstance(n, int) and n == 0):
                        dve.wait_ge(s_tm, 2 * n - 1 + h)
                    dve.tensor_reduce(neg_max[:, h, 2 * b:2 * b + 2],
                                      bank[2 + 2 * h + b][:, 0:2 * KEYS].rearrange("p (c k) -> p c k", c=2),
                                      AX_X, ALU.max, negate=True).then_inc(s_mx, 1)

            def normalise_out(n, g, p, h):
                dve.wait_ge(s_sum, 2 * n + h + 1)
                if p == 0 and h == 0 and g is not None:
                    dve.wait_ge(f_wo, g)
                own = slice(DIM_HEAD * h, DIM_HEAD * (h + 1))
                dve.tensor_tensor(o_feat[own, p, :], bank[2 + 2 * h][own, :], inv_sums[own, :], ALU.mult
                                  ).then_inc(s_nrm, 1)

            def ffn_parts(f):
                l = f // SEQS
                at = (f % SEQS) * TOK

                def mid():
                    dve.wait_ge(f_wo, f + 1)
                    dve.wait_ge(f_x, f + 1)
                    dve.tensor_tensor(x_mid[:], bank[7][:], state[:, bass.ds(at, TOK)], ALU.add).then_inc(f_mid, 1)
                    dve.wait_ge(f_mid, f + 1)
                    dve.tensor_copy(x_sh[0:HALF, :], x_mid[0:HALF, :])
                    dve.tensor_copy(x_sh[HALF:P, 1:TOK], x_mid[HALF:P, 0:TOK - 1]).then_inc(f_sh, 1)

                def centre():
                    dve.wait_ge(f_mean, f + 1)
                    dve.tensor_tensor(x_cen[:], x_sh[:], bank[7][:], ALU.subtract).then_inc(f_cen, 1)

                def norm():
                    dve.wait_ge(f_rstd, f + 1)
                    shift = vecs[:, 1, bass.ds(l, 1)]
                    dve.scalar_tensor_tensor(out=y_f[:], in0=x_cen[:], scalar=vecs[:, 0, bass.ds(l, 1)],
                                             in1=rstd_f, op0=ALU.mult, op1=ALU.mult).then_inc(f_y, 1)
                    dve.wait_ge(f_y, f + 1)
                    dve.tensor_scalar(y_hi, y_f[:], shift, None, ALU.add).then_inc(f_yhi, 1)
                    dve.wait_ge(f_yhi, f + 1)
                    dve.scalar_tensor_tensor(out=y_lo, in0=y_f[:], scalar=shift, in1=y_hi.bitcast(F32),
                                             op0=ALU.add, op1=ALU.subtract).then_inc(f_ylo, 1)

                def up(i):
                    def run():
                        n = FFN_TILES[i % NF][1]
                        dve.wait_ge(f_h, 2 * NF * f + i + 1)
                        dst = (gates if i < NF else values)[0:n, i % NF, :]
                        dve.tensor_scalar(dst, bank[7][0:n, :], b1_sb[0:n, i, bass.ds(l, 1)], None, ALU.add
                                          ).then_inc(f_he, 1)
                    return run

                def product():
                    n = FFN_TILES[-1][1]
                    dve.wait_ge(f_gelu, f + 1)
                    dve.wait_ge(f_he, 2 * NF * (f + 1))
                    dve.tensor_tensor(gates[:, 0:NF - 1, :], gates[:, 0:NF - 1, :], values[:, 0:NF - 1, :], ALU.mult)
                    dve.tensor_tensor(gates[0:n, NF - 1, :], gates[0:n, NF - 1, :], values[0:n, NF - 1, :], ALU.mult
                                      ).then_inc(f_prod, 1)

                def residual():
                    dve.wait_ge(f_w2, f + 1)
                    dve.scalar_tensor_tensor(out=state[:, bass.ds(at, TOK)], in0=bank[7][:],
                                             scalar=vecs[:, 2, bass.ds(l, 1)], in1=x_mid[:],
                                             op0=ALU.add, op1=ALU.add).then_inc(f_x, 1)

                return {(0, 0): mid, (1, 0): centre, (2, 0): norm, (2, 1): up(0), (3, 0): up(1), (3, 1): up(2),
                        (4, 0): up(3), (4, 1): up(4), (5, -1): up(5), (5, 1): product, (6, 0): residual}

            def body(g, first=False, last=False):
                parts = {} if first else ffn_parts(g - 1)
                for p in range(PAIRS):
                    n = PAIRS * g + p
                    nxt = not (last and p == PAIRS - 1)
                    l = (g if p + 1 < PAIRS else g + 1) // SEQS
                    maxima(n, 0)
                    if nxt:
                        times_sin(n + 1, l, 0)
                        times_cos(n + 1, l, 0)
                    if (p, -1) in parts:
                        parts[(p, -1)]()
                    if not (first and p == 0):
                        normalise_out(n - 1, g, (p - 1) % PAIRS, 1)
                    if nxt:
                        times_sin(n + 1, l, 1)
                        times_cos(n + 1, l, 1)
                    if p == 0:
                        if not first:
                            dve.wait_ge(s_o, 2 * PAIRS * g)
                        for t in range(1, V_TILES, 2):
                            dve.wait_ge(s_v, V_TILES * g + t + 1)
                            dve.tensor_copy(value_place(t), value_source(t)).then_inc(s_ve[1], 1)
                    if p == PAIRS - 2 and not last:
                        dve.wait_ge(s_p[1], PAIRS * (g + 1))
                        dve.wait_ge(s_v, V_TILES * (g + 1))
                        shifted_input(g + 1)
                    maxima(n, 1)
                    if (p, 0) in parts:
                        parts[(p, 0)]()
                    if nxt:
                        final(n + 1, p + 1, 0)
                        final(n + 1, p + 1, 1)
                    normalise_out(n, None if first else g, p, 0)
                    if (p, 1) in parts:
                        parts[(p, 1)]()

            dve.wait_ge(s_par, 16 * PARAM_LOADS)
            dve.wait_ge(a_state, SEQS)
            dve.memset(scratch[:, 0:1], 0.0).then_inc(f_x, 1)
            shifted_input(0)
            for i in range(2):
                times_sin(0, 0, i)
                times_cos(0, 0, i)
            final(0, 0, 0)
            final(0, 0, 1)
            body(0, first=True)
            with dve.Fori(1, BODIES - 1) as g:
                body(g)
            body(BODIES - 1, last=True)
            normalise_out(PAIRS * BODIES - 1, None, PAIRS - 1, 1)
            tail = ffn_parts(BODIES - 1)
            for key in sorted(tail):
                tail[key]()
            for i in range(SEQS * CHUNKS):
                dve.wait_ge(o_t, i // 4 + 1)
                dve.tensor_tensor(x_tok[:, i, :], x_tok[:, i, :], bank[(i // 4) % 2][:, (i % 4) * P:(i % 4 + 1) * P],
                                  ALU.add).then_inc(o_e, 1)


_INS = ['L0_attn_x', 'L0_attn_W_kqv', 'L0_attn_m', 'L0_ffn_Wqkv', 'L0_ffn_q_scale', 'L0_ffn_k_scale', 'L0_ffn_Wo',
        'L0_ffn_ln_g', 'L0_ffn_ln_b', 'L0_ffn_W1', 'L0_ffn_b1', 'L0_ffn_W2', 'L0_ffn_b2']


def kernel(**inputs):
    import concourse.bacc as bacc
    from concourse.bass_utils import run_bass_kernel_spmd

    nc = bacc.Bacc("TRN2", target_bir_lowering=False, num_devices=1)
    arrays, args = {}, []
    masks, wide = shape_constants()
    host = [(name, np.ascontiguousarray(inputs[name])) for name in _INS]
    host += [("rotary", rotary_constants()), ("masks", masks), ("wide", wide)]
    for name, a in host:
        arrays[f"in_{name}"] = a
        args.append(nc.dram_tensor(f"in_{name}", a.shape, mybir.dt.from_np(a.dtype), kind="ExternalInput").ap())
    out = nc.dram_tensor("out_0", (SEQS, TOK, D), F32, kind="ExternalOutput").ap()
    build_program(nc, *args, out)
    r = run_bass_kernel_spmd(nc, [arrays], core_ids=[0])
    return r.results[0]["out_0"]
```
